# Optimizing a Trainium2 kernel written in Bass

```python
import numpy as np
import jax
import jax.numpy as jnp

def _softmax(x, axis=-1):
    return jax.nn.softmax(x, axis=axis)

def _gelu(x):
    return jax.nn.gelu(x, approximate=True)

def _silu(x):
    return jax.nn.silu(x)

def _sigmoid(x):
    return jax.nn.sigmoid(x)

def _layernorm(x, axis=-1, eps=1e-05):
    m = jnp.mean(x, axis=axis, keepdims=True)
    v = jnp.var(x, axis=axis, keepdims=True)
    return (x - m) / jnp.sqrt(v + eps)

def _scatter_add(tgt, idx, src, axis=0):
    return tgt.at[idx].add(src)

def _segment_sum(src, seg, n):
    return jax.ops.segment_sum(src, seg, n)
kernel_name = 'mk_macaron_d1_jaxref_r4_ee4b0e'

def setup_inputs(seed: int=0):
    np.random.seed(seed)
    _w = jnp.asarray

    def _L0_attn_setup():
        import jax, jax.numpy as jnp
        import numpy as np
        D_MODEL = 256
        N_HEADS = 16
        KEY_DIM = D_MODEL // 2
        VAL_DIM = D_MODEL
        HEAD_QK = KEY_DIM // N_HEADS
        HEAD_V = VAL_DIM // N_HEADS
        PROJ_LR = 32
        GATE_LR = 64
        EPS = 1e-05
        key = jax.random.key(seed)
        ks = jax.random.split(key, 16)
        s = 0.02
        B, T = (4, 256)
        return {'x': jax.random.normal(ks[0], (B, T, D_MODEL), jnp.float32), 'mu_x': jax.random.normal(ks[1], (D_MODEL,), jnp.float32) * s, 'W_x1': jax.random.normal(ks[2], (D_MODEL, 5 * PROJ_LR), jnp.float32) * s, 'W_x2': jax.random.normal(ks[3], (D_MODEL, 5, PROJ_LR), jnp.float32) * s, 'x_bias': jax.random.normal(ks[4], (5, D_MODEL), jnp.float32) * s, 'W_r': jax.random.normal(ks[5], (D_MODEL, KEY_DIM), jnp.float32) * s, 'W_w1': jax.random.normal(ks[6], (D_MODEL, GATE_LR), jnp.float32) * s, 'W_w2': jax.random.normal(ks[7], (GATE_LR, KEY_DIM), jnp.float32) * s, 'b_w2': jax.random.normal(ks[8], (KEY_DIM,), jnp.float32) * s, 'W_k': jax.random.normal(ks[9], (D_MODEL, KEY_DIM), jnp.float32) * s, 'W_v': jax.random.normal(ks[10], (D_MODEL, VAL_DIM), jnp.float32) * s, 'W_g': jax.random.normal(ks[11], (D_MODEL, VAL_DIM), jnp.float32) * s, 'u': jax.random.normal(ks[12], (N_HEADS, HEAD_QK), jnp.float32) * s, 'gn_w': jnp.ones((VAL_DIM,), jnp.float32), 'gn_b': jnp.zeros((VAL_DIM,), jnp.float32), 'W_o': jax.random.normal(ks[13], (VAL_DIM, D_MODEL), jnp.float32) * s}
    _L0_attn_in = _L0_attn_setup()

    def _L0_ffn_setup():
        import jax, jax.numpy as jnp
        import numpy as np
        S, B, D = (256, 2, 256)
        E, TOPK = (15, 3)
        F = 256
        FS = 512

        def _uinit(k, shape, out_dim):
            std = out_dim ** (-0.5)
            return jax.random.uniform(k, shape, jnp.float32, -std, std)
        key = jax.random.key(seed)
        ks = jax.random.split(key, 10)
        return {'x': jax.random.normal(ks[0], (S, B, D), jnp.float32), 'gate_w': jax.random.normal(ks[1], (E, D), jnp.float32) * D ** (-0.5), 'fc1_w': _uinit(ks[2], (E, 2 * F, D), 2 * F), 'fc1_b': _uinit(ks[3], (E, 2 * F), 2 * F), 'geglu_mult': jnp.ones((E, F), jnp.float32), 'fc2_w': _uinit(ks[4], (E, D, F), D), 'fc2_b': _uinit(ks[5], (E, D), D), 's_fc1_w': _uinit(ks[6], (2 * FS, D), 2 * FS), 's_fc1_b': _uinit(ks[7], (2 * FS,), 2 * FS), 's_geglu_mult': jnp.ones((FS,), jnp.float32), 's_fc2_w': _uinit(ks[8], (D, FS), D), 's_fc2_b': _uinit(ks[9], (D,), D)}
    _L0_ffn_in = _L0_ffn_setup()
    _d = {'L0_attn_x': _L0_attn_in['x'], 'L0_attn_mu_x': _L0_attn_in['mu_x'], 'L0_attn_W_x1': _L0_attn_in['W_x1'], 'L0_attn_W_x2': _L0_attn_in['W_x2'], 'L0_attn_x_bias': _L0_attn_in['x_bias'], 'L0_attn_W_r': _L0_attn_in['W_r'], 'L0_attn_W_w1': _L0_attn_in['W_w1'], 'L0_attn_W_w2': _L0_attn_in['W_w2'], 'L0_attn_b_w2': _L0_attn_in['b_w2'], 'L0_attn_W_k': _L0_attn_in['W_k'], 'L0_attn_W_v': _L0_attn_in['W_v'], 'L0_attn_W_g': _L0_attn_in['W_g'], 'L0_attn_u': _L0_attn_in['u'], 'L0_attn_gn_w': _L0_attn_in['gn_w'], 'L0_attn_gn_b': _L0_attn_in['gn_b'], 'L0_attn_W_o': _L0_attn_in['W_o'], 'L0_ffn_gate_w': _L0_ffn_in['gate_w'], 'L0_ffn_fc1_w': _L0_ffn_in['fc1_w'], 'L0_ffn_fc1_b': _L0_ffn_in['fc1_b'], 'L0_ffn_geglu_mult': _L0_ffn_in['geglu_mult'], 'L0_ffn_fc2_w': _L0_ffn_in['fc2_w'], 'L0_ffn_fc2_b': _L0_ffn_in['fc2_b'], 'L0_ffn_s_fc1_w': _L0_ffn_in['s_fc1_w'], 'L0_ffn_s_fc1_b': _L0_ffn_in['s_fc1_b'], 'L0_ffn_s_geglu_mult': _L0_ffn_in['s_geglu_mult'], 'L0_ffn_s_fc2_w': _L0_ffn_in['s_fc2_w'], 'L0_ffn_s_fc2_b': _L0_ffn_in['s_fc2_b']}
    _x0 = _d['L0_attn_x']
    _d['L0_attn_x'] = jax.random.normal(jax.random.fold_in(jax.random.key(seed), 1), (1, 4096, 256), dtype=_x0.dtype)
    del _x0
    return _d

def reference(L0_attn_x, L0_attn_mu_x, L0_attn_W_x1, L0_attn_W_x2, L0_attn_x_bias, L0_attn_W_r, L0_attn_W_w1, L0_attn_W_w2, L0_attn_b_w2, L0_attn_W_k, L0_attn_W_v, L0_attn_W_g, L0_attn_u, L0_attn_gn_w, L0_attn_gn_b, L0_attn_W_o, L0_ffn_gate_w, L0_ffn_fc1_w, L0_ffn_fc1_b, L0_ffn_geglu_mult, L0_ffn_fc2_w, L0_ffn_fc2_b, L0_ffn_s_fc1_w, L0_ffn_s_fc1_b, L0_ffn_s_geglu_mult, L0_ffn_s_fc2_w, L0_ffn_s_fc2_b):

    def _L0_attn_ref(x, mu_x, W_x1, W_x2, x_bias, W_r, W_w1, W_w2, b_w2, W_k, W_v, W_g, u, gn_w, gn_b, W_o):
        import jax, jax.numpy as jnp
        import numpy as np
        D_MODEL = 256
        N_HEADS = 16
        KEY_DIM = D_MODEL // 2
        VAL_DIM = D_MODEL
        HEAD_QK = KEY_DIM // N_HEADS
        HEAD_V = VAL_DIM // N_HEADS
        PROJ_LR = 32
        GATE_LR = 64
        EPS = 1e-05
        B, T, D = x.shape
        shifted = jnp.pad(x, ((0, 0), (1, 0), (0, 0)))[:, :T]
        delta = shifted - x
        low = jnp.tanh((x + delta * mu_x) @ W_x1).reshape(B, T, 5, PROJ_LR)
        mus = jnp.einsum('blnr,dnr->blnd', low, W_x2) + x_bias
        xr, xw, xk, xv, xg = [x + delta * mus[:, :, i] for i in range(5)]
        r = (xr @ W_r).reshape(B, T, N_HEADS, HEAD_QK)
        w = (jnp.tanh(xw @ W_w1) @ W_w2 + b_w2).reshape(B, T, N_HEADS, HEAD_QK)
        k = (xk @ W_k).reshape(B, T, N_HEADS, HEAD_QK)
        v = (xv @ W_v).reshape(B, T, N_HEADS, HEAD_V)
        g = xg @ W_g
        w = -jnp.exp(w)

        def step(S, inp):
            r_t, k_t, v_t, w_t = inp
            o_t = jnp.einsum('bhk,bhkv->bhv', r_t, S) + jnp.einsum('bhk,hk,bhk,bhv->bhv', r_t, u, k_t, v_t)
            S = jnp.exp(w_t)[..., None] * S + k_t[..., :, None] * v_t[..., None, :]
            return (S, o_t)
        S0 = jnp.zeros((B, N_HEADS, HEAD_QK, HEAD_V), x.dtype)
        xs = tuple((jnp.moveaxis(t, 1, 0) for t in (r, k, v, w)))
        _, o = jax.lax.scan(step, S0, xs)
        o = jnp.moveaxis(o, 0, 1)
        mean = o.mean(-1, keepdims=True)
        var = o.var(-1, keepdims=True)
        o = ((o - mean) * jax.lax.rsqrt(var + EPS)).reshape(B, T, VAL_DIM)
        o = (o * gn_w + gn_b) * (g * jax.nn.sigmoid(g))
        return o @ W_o

    def _L0_ffn_ref(x, gate_w, fc1_w, fc1_b, geglu_mult, fc2_w, fc2_b, s_fc1_w, s_fc1_b, s_geglu_mult, s_fc2_w, s_fc2_b):
        import jax, jax.numpy as jnp
        import numpy as np
        S, B, D = (256, 2, 256)
        E, TOPK = (15, 3)
        F = 256
        FS = 512

        def _uinit(k, shape, out_dim):
            std = out_dim ** (-0.5)
            return jax.random.uniform(k, shape, jnp.float32, -std, std)
        s, b, d = x.shape
        xt = x.reshape(-1, d)
        T = xt.shape[0]
        logits = xt @ gate_w.T
        scores = jax.nn.softmax(logits, axis=-1)
        topk_w, topk_idx = jax.lax.top_k(scores, TOPK)
        topk_w = topk_w / (jnp.sum(topk_w, axis=-1, keepdims=True) + 1e-20)
        comb = jnp.zeros((T, E), xt.dtype).at[jnp.arange(T)[:, None], topk_idx].add(topk_w)
        h = jnp.einsum('td,efd->etf', xt, fc1_w) + fc1_b[:, None, :]
        xh, g = (h[..., :F], h[..., F:])
        a = jax.nn.gelu(g, approximate=False) * xh * geglu_mult[:, None, :]
        yexp = jnp.einsum('etf,edf->etd', a, fc2_w) + fc2_b[:, None, :]
        y = jnp.einsum('etd,te->td', yexp, comb)
        hs = xt @ s_fc1_w.T + s_fc1_b
        xs, gs = (hs[..., :FS], hs[..., FS:])
        as_ = jax.nn.gelu(gs, approximate=False) * xs * s_geglu_mult
        ys = as_ @ s_fc2_w.T + s_fc2_b
        return (y + ys).reshape(s, b, d)
    x = L0_attn_x
    x = x + 0.5 * _L0_ffn_ref(_layernorm(x, axis=-1), L0_ffn_gate_w, L0_ffn_fc1_w, L0_ffn_fc1_b, L0_ffn_geglu_mult, L0_ffn_fc2_w, L0_ffn_fc2_b, L0_ffn_s_fc1_w, L0_ffn_s_fc1_b, L0_ffn_s_geglu_mult, L0_ffn_s_fc2_w, L0_ffn_s_fc2_b)
    x = x + _L0_attn_ref(_layernorm(x, axis=-1), L0_attn_mu_x, L0_attn_W_x1, L0_attn_W_x2, L0_attn_x_bias, L0_attn_W_r, L0_attn_W_w1, L0_attn_W_w2, L0_attn_b_w2, L0_attn_W_k, L0_attn_W_v, L0_attn_W_g, L0_attn_u, L0_attn_gn_w, L0_attn_gn_b, L0_attn_W_o)
    x = x + 0.5 * _L0_ffn_ref(_layernorm(x, axis=-1), L0_ffn_gate_w, L0_ffn_fc1_w, L0_ffn_fc1_b, L0_ffn_geglu_mult, L0_ffn_fc2_w, L0_ffn_fc2_b, L0_ffn_s_fc1_w, L0_ffn_s_fc1_b, L0_ffn_s_geglu_mult, L0_ffn_s_fc2_w, L0_ffn_s_fc2_b)
    return x

_drawn_inputs = setup_inputs


def setup_inputs(seed=0):
    import zlib

    import numpy as np

    out = dict(_drawn_inputs(seed))
    spreads = {'L0_attn_gn_w': (1.0, 0.6),
     'L0_attn_gn_b': (0.0, 0.8),
     'L0_ffn_geglu_mult': (1.0, 0.6),
     'L0_ffn_s_geglu_mult': (1.0, 0.6)}
    factors = {'L0_attn_mu_x': 8.0,
     'L0_attn_W_x1': 7.526,
     'L0_attn_W_x2': 7.593,
     'L0_attn_x_bias': 8.0,
     'L0_attn_W_w1': 8.0,
     'L0_attn_W_w2': 8.0,
     'L0_attn_b_w2': 42.102,
     'L0_attn_u': 8.0,
     'L0_ffn_fc1_b': 8.0,
     'L0_ffn_s_fc1_b': 8.0}
    for name, (base, spread) in spreads.items():
        noise = np.random.default_rng([zlib.crc32(name.encode()), seed]).standard_normal(out[name].shape)
        drawn = base * np.exp(spread * noise) if base else spread * noise
        out[name] = jnp.asarray(drawn.astype(out[name].dtype))
    for name, factor in factors.items():
        out[name] = (out[name] * factor).astype(out[name].dtype)
    return out
```

```python
import concourse.bass as bass
from concourse import mybir
from contextlib import ExitStack

FP32 = mybir.dt.float32
BF16 = mybir.dt.bfloat16
I32 = mybir.dt.int32
U32 = mybir.dt.uint32
ALU = mybir.AluOpType
ACT = mybir.ActivationFunctionType
AX = mybir.AxisListType.X

P = 128
T = 4096
D = 256
KD = D // P
E = 15
TOPK = 3
F = 256
KF = F // P
FS = 512
KFS = FS // P
H = 16
DK = 8
DV = 16
LR = 32
GL = 64
EPS = 1e-5
NT = T // P
C = 512
NC = T // C
TC = C // P
NB = T * TOPK // P + E
NB += NB % 2
MIX_R, MIX_W, MIX_K, MIX_V, MIX_G = range(5)


class Chain:

    def __init__(self, eng, sem, turn=0, per_turn=0):
        self.eng, self.sem, self.turn, self.per_turn, self.n = eng, sem, turn, per_turn, 0

    def link(self, ins):
        self.n += 1
        ins.then_inc(self.sem, 1)
        self.eng.wait_ge(self.sem, self.turn * self.per_turn + self.n)

    def close(self):
        assert self.n == self.per_turn, (self.n, self.per_turn)


def bcast(ap, axis, n):
    ap = ap.unsqueeze(axis)
    shape = list(ap.shape)
    shape[axis] = n
    return ap.to_broadcast(shape)


def macaron_kernel(nc, x, mu_x, W_x1, W_x2, x_biasT, W_r, W_w1, W_w2, b_w2, W_k, W_v, W_v_vh, W_g, u, gn_w, gn_b,
                   W_o, gate_wT, fc1_wT, fc1_b, geglu_mult, fc2_wT, fc2_b, s_fc1_wT, s_fc1_b, s_geglu_mult,
                   s_fc2_wT, s_fc2_b, out):
    ctx = ExitStack()
    in_use = []
    with ctx:
        def dram(name, shape, dt):
            return nc.dram_tensor(name, shape, dt, kind="Internal").ap()

        def sb(name, shape, dt=FP32, scope=ctx):
            return scope.enter_context(nc.sbuf_tensor(name, shape, dt))

        def ps(name, shape, dt=FP32, scope=ctx):
            return scope.enter_context(nc.psum_tensor(name, shape, dt))

        def sem(name):
            in_use.append(nc.alloc_semaphore(name=name))
            return in_use[-1]

        def end_phase():
            nc.clear_and_free_semaphores(in_use)
            nc.all_engine_barrier()
            in_use.clear()

        xn_dram = dram("xn_scratch", (T, D), FP32)
        xnT_dram = dram("xnT_scratch", (D, T), FP32)
        x2_dram = dram("x2_scratch", (T, D), FP32)
        acc_dram = dram("acc_scratch", (T, D), FP32)
        rows_dram = dram("rows_scratch", (NB * P, D), FP32)
        yrows_dram = dram("yrows_scratch", (NB * P, D), FP32)

        ident = sb("ident", [P, P])
        eps = sb("eps", [P, 1])
        pad = sb("pad", [P, 2])
        ones3 = sb("ones3", [P, P], BF16)
        tri = sb("tri", [P, P], BF16)
        ones = sb("ones", [P, P], BF16)
        gate = sb("gate", [P, KD, E])
        logits = sb("logits", [P, NT, E])
        pos = sb("pos", [P, TOPK, NT], I32)
        wsel = sb("wsel", [P, TOPK, NT])
        block_expert = sb("block_expert", [1, NB], I32)

        def phase_norm():
            s_ident, s_cst, s_zero, s_fill, s_gate = (sem(f"a_{n}") for n in ("ident", "cst", "zero", "fill", "gate"))
            s_xin = [sem(f"a_xin{p}") for p in range(2)]
            s_xnout = [sem(f"a_xnout{p}") for p in range(2)]
            s_xTout = [sem(f"a_xTout{p}") for p in range(2)]
            s_stats, s_std, s_norm, s_tr, s_xT, s_lg, s_lgsb = (
                sem(f"a_{n}") for n in ("stats", "std", "norm", "tr", "xT", "lg", "lgsb"))
            s_dve = sem("a_dve")
            with ExitStack() as sc:
                zero = sb("a_zero", [P, 2048], scope=sc)
                xin = [sb(f"a_x{p}", [P, TC, D], scope=sc) for p in range(2)]
                xn = [sb(f"a_xn{p}", [P, TC, D], scope=sc) for p in range(2)]
                xT = [sb(f"a_xT{p}", [P, KD, C], scope=sc) for p in range(2)]
                st = [sb(f"a_st{p}", [P, TC, 6], scope=sc) for p in range(2)]
                mv = [sb(f"a_mv{p}", [P, TC, 2], scope=sc) for p in range(2)]
                sd = [sb(f"a_sd{p}", [P, TC], scope=sc) for p in range(2)]
                rs = [sb(f"a_rs{p}", [P, TC], scope=sc) for p in range(2)]
                psT = [ps(f"a_psT{p}", [P, KD, C], scope=sc) for p in range(2)]
                psL = [ps(f"a_psL{p}", [P, TC, P], scope=sc) for p in range(2)]
                x_v = x.rearrange("a (i p) d -> p (a i) d", p=P)
                xn_v = xn_dram.rearrange("(i p) d -> p i d", p=P)
                xnT_v = xnT_dram.rearrange("(k p) t -> p k t", p=P)
                block = sc.enter_context(nc.Block())

                @block.sync
                def _(sp):
                    sp.dma_start(gate[:, :, :], gate_wT.rearrange("(k p) e -> p k e", p=P)).then_inc(s_gate, 16)
                    with sp.Fori(0, NC // 2) as half:
                        c0 = 2 * half
                        for p in range(2):
                            c = c0 + p
                            if p == 0:
                                sp.wait_ge(s_norm, c)
                            else:
                                sp.wait_ge(s_norm, c)
                            sp.dma_start(xin[p][:, :, :], x_v[:, bass.ds(c * TC, TC), :]).then_inc(s_xin[p], 16)
                            sp.wait_ge(s_xT, c + 1)
                            sp.dma_start(xnT_v[:, :, bass.ds(c * C, C)], xT[p][:, :, :]).then_inc(s_xTout[p], 16)
                    for p in range(2):
                        sp.wait_ge(s_xTout[p], 16 * (NC // 2))

                @block.gpsimd
                def _(pool):
                    pool.memset(zero[:, :], 0.0).then_inc(s_zero, 1)
                    pool.memset(ident[:, :], 0.0).then_inc(s_ident, 1)
                    pool.wait_ge(s_ident, 1)
                    pool.affine_select(out=ident[:, :], in_=ident[:, :], compare_op=ALU.not_equal, fill=1.0,
                                       base=0, pattern=[[-1, P]], channel_multiplier=1).then_inc(s_ident, 1)
                    pool.memset(ones[:, :], 1.0).then_inc(s_cst, 1)
                    pool.memset(ones3[:, :], 0.0).then_inc(s_cst, 1)
                    pool.memset(eps[:, :], EPS).then_inc(s_cst, 1)
                    pool.wait_ge(s_cst, 3)
                    pool.affine_select(out=tri[:, :], in_=ones[:, :], compare_op=ALU.is_gt, fill=0.0,
                                       base=0, pattern=[[1, P]], channel_multiplier=-1).then_inc(s_cst, 1)
                    for n, r in enumerate((0, 32, 64)):
                        pool.wait_ge(s_cst, 4 + n)
                        pool.memset(ones3[r:r + 1, :], 1.0).then_inc(s_cst, 1)

                @block.vector
                def _(dve):
                    ch_per_turn = 2 * 3
                    with dve.Fori(0, NC // 2) as half:
                        c0 = 2 * half
                        ch = Chain(dve, s_dve, half, ch_per_turn)
                        for p in range(2):
                            c = c0 + p
                            dve.wait_ge(s_xin[p], 8 * c0 + 16)
                            for j in range(TC):
                                last = dve.bn_stats(st[p][:, j, :], xin[p][:, j, :])
                            ch.link(last)
                            dve.memset(pad[:, 0:1], 0.0)
                            for j in range(TC):
                                last = dve.bn_aggr(mv[p][:, j, :], st[p][:, j, :])
                            last.then_inc(s_stats, 1)
                            dve.wait_ge(s_std, c + 1)
                            ch.link(dve.reciprocal(rs[p][:, :], sd[p][:, :]))
                            if p == 0:
                                dve.wait_ge(s_xnout[0], 8 * c0)
                            else:
                                dve.wait_ge(s_xnout[1], 8 * c0)
                            dve.wait_ge(s_tr, c)
                            for j in range(TC):
                                last = dve.tensor_scalar(xn[p][:, j, :], xin[p][:, j, :], mv[p][:, j, 0:1],
                                                         rs[p][:, j:j + 1], ALU.subtract, ALU.mult)
                            last.then_inc(s_norm, 1)
                            dve.wait_ge(s_lg, c + 1)
                            ch.link(dve.tensor_copy(logits[:, bass.ds(c * TC, TC), :], psL[p][:, :, 0:E]))
                        ch.close()

                @block.scalar
                def _(act):
                    act.wait_ge(s_zero, 1)
                    rows_v = rows_dram.rearrange("(n q r) d -> n q (r d)", q=P, r=8)
                    for n in range(NB // 8):
                        act.dma_start(rows_v[n], zero[:, :]).then_inc(s_fill, 16)
                    act.wait_ge(s_cst, 7)
                    with act.Fori(0, NC // 2) as half:
                        c0 = 2 * half
                        for p in range(2):
                            c = c0 + p
                            act.wait_ge(s_stats, c + 1)
                            act.activation(sd[p][:, :], mv[p][:, :, 1], ACT.Sqrt, bias=eps[:, 0:1]).then_inc(s_std, 1)
                            act.wait_ge(s_norm, c + 1)
                            act.dma_start(xn_v[:, bass.ds(c * TC, TC), :], xn[p][:, :, :]).then_inc(s_xnout[p], 16)
                            act.wait_ge(s_tr, c + 1)
                            act.wait_ge(s_xTout[p], 8 * c0)
                            act.activation(xT[p][:, :, :], psT[p][:, :, :], ACT.Copy).then_inc(s_xT, 1)
                    for p in range(2):
                        act.wait_ge(s_xnout[p], 16 * (NC // 2))
                    act.wait_ge(s_fill, 16 * (NB // 8))

                @block.tensor
                def _(pe):
                    pe.wait_ge(s_ident, 2)
                    pe.wait_ge(s_gate, 16)
                    with pe.Fori(0, NC // 2) as half:
                        c0 = 2 * half
                        for p in range(2):
                            c = c0 + p
                            pe.wait_ge(s_norm, c + 1)
                            for k in range(KD):
                                for j in range(TC):
                                    last = pe.transpose(psT[p][:, k, j * P:(j + 1) * P],
                                                        xn[p][:, j, k * P:(k + 1) * P], ident[:, :])
                            last.then_inc(s_tr, 1)
                            pe.wait_ge(s_xT, c + 1)
                            for j in range(TC):
                                for k in range(KD):
                                    last = pe.matmul(psL[p][:, j, 0:E], xT[p][:, k, j * P:(j + 1) * P],
                                                     gate[:, k, :], start=k == 0, stop=k == KD - 1)
                            last.then_inc(s_lg, 1)

        def phase_experts(tag, x_src):
            with ExitStack() as we:
                w1 = sb(f"{tag}_w1", [P, E * KD * 2 * F], scope=we)
                w2 = sb(f"{tag}_w2", [P, E * KF * D], scope=we)
                b1 = sb(f"{tag}_b1", [P, E * 2 * F], BF16, scope=we)
                b2 = sb(f"{tag}_b2", [P, E * D], BF16, scope=we)
                bs2 = sb(f"{tag}_bs2", [P, D], BF16, scope=we)
                route(tag, x_src, w1, w2, b1, b2, bs2)
                experts(tag, w1, w2, b1, b2)

        def route(tag, x_src, w1, w2, b1, b2, bs2):
            def s(n):
                return sem(f"{tag}r_{n}")
            s_w1, s_w2, s_gm, s_ws, s_bias, s_xn, s_iota = (s(n) for n in ("w1", "w2", "gm", "ws", "bias", "xn", "iota"))
            s_xT = [s(f"xT{p}") for p in range(2)]
            s_xr = [s(f"xr{p}") for p in range(2)]
            s_out = [s(f"out{p}") for p in range(2)]
            s_dve, s_bdone, s_bz, s_hot, s_rank, s_exp, s_soft, s_pos, s_scat, s_fold, s_wfold = (
                s(n) for n in ("dve", "bdone", "bz", "hot", "rank", "exp", "soft", "pos", "scat", "fold", "wfold"))
            s_h, s_ge, s_a, s_y, s_acc = (s(n) for n in ("h", "ge", "a", "y", "acc"))
            with ExitStack() as sc:
                ws1 = sb(f"{tag}_ws1", [P, KD, 2 * FS], scope=sc)
                ws2 = sb(f"{tag}_ws2", [P, KFS, D], scope=sc)
                gms = sb(f"{tag}_gms", [P, KFS], scope=sc)
                gm = sb(f"{tag}_gm", [P, E * KF], scope=sc)
                bs1 = sb(f"{tag}_bs1", [P, 2 * KFS], scope=sc)
                HB = 2 * C
                xn = sb(f"{tag}_xn", [P, NT, D], scope=sc)
                bpart = sb(f"{tag}_bpart", [65, HB], BF16, scope=sc)
                xT = [sb(f"{tag}_xT{p}", [P, KD, C], scope=sc) for p in range(2)]
                xr = [sb(f"{tag}_xr{p}", [P, TC, D], scope=sc) for p in range(2)]
                ge = sb(f"{tag}_ge", [P, 2, C], scope=sc)
                braw = ge[0:65, :, :].rearrange("p a c -> p (a c)")
                aT = sb(f"{tag}_aT", [P, KFS, C], scope=sc)
                ph = [ps(f"{tag}_ph{q}", [P, 2, C], scope=sc) for q in range(2)]
                py = ps(f"{tag}_py", [P, TC, D], scope=sc)
                prank = ps(f"{tag}_prank", [P, NT * E], scope=sc)
                ptot = ps(f"{tag}_ptot", [P, NT * E], scope=sc)

                def small(n, shape, dt=FP32):
                    return sb(f"{tag}_{n}", shape, dt, scope=sc)
                top = small("top", [P, NT, 8])
                topi = small("topi", [P, NT, 8], U32)
                chosen = small("chosen", [P, TOPK, NT])
                iota_e = small("iota_e", [P, E])
                iota_b = small("iota_b", [1, NB])
                hot = aT[:, :, :].rearrange("p k c -> p (k c)")[:, 0:TOPK * NT * E].rearrange(
                    "p (j i e) -> p j i e", j=TOPK, i=NT)
                past = aT[0:1, :, :].rearrange("p k c -> p (k c)")[:, 0:NB * E].rearrange("p (b e) -> p b e", e=E)
                many = small("many", [P, NT, E], BF16)
                tmp = small("tmp", [P, NT, E])
                tot = small("tot", [P, E, NT])
                inc = small("inc", [P, E, NT])
                keep = small("keep", [P, E, NT])
                nblk = small("nblk", [P, E])
                nblk_i = small("nblk_i", [P, E], I32)
                endb = small("endb", [P, E])
                off = small("off", [P, E])
                one_e = small("one_e", [P, E])
                pastn = small("pastn", [1, NB])
                soft = small("soft", [P, NT])
                etop = small("etop", [P, TOPK, NT])
                posf = small("posf", [P, TOPK, NT])

                x_v = x_src.rearrange("(i p) d -> p i d", p=P)
                xn_v = xn_dram.rearrange("(i p) d -> p i d", p=P)
                xnT_v = xnT_dram.rearrange("(k p) t -> p k t", p=P)
                acc_v = acc_dram.rearrange("(i p) d -> p i d", p=P)
                block = sc.enter_context(nc.Block())

                lots = [(dst[:, :], src.rearrange("e f -> (e f)"), at, min(HB, E * n - at))
                        for dst, src, n in ((b1, fc1_b, 2 * F), (b2, fc2_b, D)) for at in range(0, E * n, HB)]
                lots += [(bs2[:, :], s_fc2_b, 0, D)]

                @block.sync
                def _(sp):
                    sp.dma_start(ws1[:, :, :], s_fc1_wT.rearrange("(k p) f -> p k f", p=P)).then_inc(s_ws, 16)
                    sp.dma_start(ws2[:, :, :], s_fc2_wT.rearrange("(k p) d -> p k d", p=P)).then_inc(s_ws, 16)
                    with nc.allow_non_contiguous_dma(reason="small per-channel vectors"):
                        sp.dma_start(gms[:, :], s_geglu_mult.rearrange("(k p) -> p k", p=P)).then_inc(s_ws, 16)
                        sp.dma_start(bs1[:, :], s_fc1_b.rearrange("(k p) -> p k", p=P)).then_inc(s_ws, 16)
                        sp.dma_start(gm[:, :], geglu_mult.rearrange("e (k p) -> p (e k)", p=P)).then_inc(s_gm, 16)
                    for n in range(2):
                        sp.dma_start(xn[:, n * NT // 2:(n + 1) * NT // 2, :],
                                     xn_v[:, n * NT // 2:(n + 1) * NT // 2, :]).then_inc(s_xn, 16)
                    for n, (dst, src, at, size) in enumerate(lots):
                        if n:
                            sp.wait_ge(s_bdone, n)
                        for r in (0, 32, 64):
                            sp.dma_start(braw[r:r + 1, 0:size], src[at:at + size].unsqueeze(0)).then_inc(s_bias, 16)
                    for e in range(E):
                        sp.dma_start(w2[:, e * KF * D:(e + 1) * KF * D].rearrange("p (k d) -> p k d", d=D),
                                     fc2_wT[e].rearrange("(k p) d -> p k d", p=P)).then_inc(s_w2, 16)
                    for e in range(E):
                        sp.dma_start(w1[:, e * KD * 2 * F:(e + 1) * KD * 2 * F].rearrange("p (k f) -> p k f", f=2 * F),
                                     fc1_wT[e].rearrange("(k p) f -> p k f", p=P)).then_inc(s_w1, 16)
                    sp.wait_ge(s_w1, 16 * E)

                @block.gpsimd
                def _(pool):
                    pool.iota(iota_e[:, :], pattern=[[1, E]], base=0, channel_multiplier=0,
                              allow_small_or_imprecise_dtypes=True).then_inc(s_iota, 1)
                    pool.iota(iota_b[:, :], pattern=[[1, NB]], base=0, channel_multiplier=0,
                              allow_small_or_imprecise_dtypes=True).then_inc(s_iota, 1)
                    pool.memset(b1[:, :], 0.0).then_inc(s_bz, 1)
                    pool.memset(b2[:, :], 0.0).then_inc(s_bz, 1)
                    pool.memset(bs2[:, :], 0.0).then_inc(s_bz, 1)
                    pool.wait_ge(s_xn, 32)
                    pool.wait_ge(s_pos, 1)
                    for i in range(NT):
                        for j in range(TOPK):
                            pool.indirect_dma_start(
                                out=rows_dram[:, :], out_offset=bass.IndirectOffsetOnAxis(ap=pos[:, j, i:i + 1], axis=0),
                                in_=xn[:, i, :], in_offset=None).then_inc(s_scat, 16)
                    pool.wait_ge(s_scat, 16 * NT * TOPK)

                @block.vector
                def _(dve):
                    ch = Chain(dve, s_dve)

                    for i in range(NT):
                        last = dve.max(top[:, i, :], logits[:, i, :])
                    ch.link(last)
                    for i in range(NT):
                        last = dve.max_index(topi[:, i, :], top[:, i, :], logits[:, i, :])
                    ch.link(last)
                    ch.link(dve.tensor_copy(chosen[:, :, :].rearrange("p j i -> p i j"), topi[:, :, 0:TOPK]))
                    dve.wait_ge(s_iota, 2)
                    for j in range(TOPK):
                        last = dve.tensor_tensor(hot[:, j, :, :], bcast(iota_e[:, :], 1, NT),
                                                 bcast(chosen[:, j, :], 2, E), ALU.is_equal)
                    ch.link(last)
                    ch.link(dve.tensor_tensor(tmp[:, :, :], hot[:, 0, :, :], hot[:, 1, :, :], ALU.add))
                    dve.tensor_tensor(many[:, :, :], tmp[:, :, :], hot[:, 2, :, :], ALU.add).then_inc(s_hot, 1)
                    ch.link(dve.memset(keep[:, :, :], 1.0))
                    ch.link(dve.memset(keep[:, :, 0:1], 0.0))
                    ch.link(dve.memset(one_e[:, :], 1.0))
                    dve.tensor_tensor(etop[:, :, :], top[:, :, 0:TOPK].rearrange("p i j -> p j i"),
                                      bcast(top[:, :, 0], 1, TOPK), ALU.subtract)
                    dve.wait_ge(s_hot, 1)
                    dve.tensor_tensor(tmp[:, :, :], logits[:, :, :], bcast(top[:, :, 0], 2, E),
                                      ALU.subtract).then_inc(s_soft, 1)
                    dve.wait_ge(s_rank, 1)
                    ch.link(dve.tensor_copy(tot[:, :, :], ptot[:, :].rearrange("p (i e) -> p e i", e=E)))
                    ch.link(dve.tensor_tensor_scan(inc[:, :, :].rearrange("p e i -> p (e i)"),
                                                   keep[:, :, :].rearrange("p e i -> p (e i)"),
                                                   tot[:, :, :].rearrange("p e i -> p (e i)"), 0.0, ALU.mult, ALU.add))
                    ch.link(dve.tensor_scalar(nblk_i[:, :], inc[:, :, NT - 1], float(P - 1), None, ALU.add))
                    ch.link(dve.tensor_scalar(nblk_i[:, :], nblk_i[:, :], 7, None, ALU.arith_shift_right))
                    ch.link(dve.tensor_copy(nblk[:, :], nblk_i[:, :]))
                    ch.link(dve.tensor_tensor_scan(endb[:, :], one_e[:, :], nblk[:, :], 0.0, ALU.mult, ALU.add))
                    ch.link(dve.tensor_tensor(off[:, :], endb[:, :], nblk[:, :], ALU.subtract))
                    ch.link(dve.tensor_scalar(off[:, :], off[:, :], float(P), None, ALU.mult))
                    ch.link(dve.tensor_tensor(inc[:, :, :], inc[:, :, :], tot[:, :, :], ALU.subtract))
                    ch.link(dve.tensor_tensor(inc[:, :, :], inc[:, :, :], bcast(off[:, :], 2, NT), ALU.add))
                    ch.link(dve.tensor_tensor(tot[:, :, :], prank[:, :].rearrange("p (i e) -> p e i", e=E),
                                              inc[:, :, :], ALU.add))
                    for j in range(TOPK):
                        ch.link(dve.tensor_tensor(inc[:, :, :], hot[:, j, :, :].rearrange("p i e -> p e i"),
                                                  tot[:, :, :], ALU.mult))
                        ch.link(dve.tensor_reduce(posf[:, j, :], inc[:, :, :].rearrange("p e i -> p i e"), AX, ALU.add))
                    dve.tensor_copy(pos[:, :, :], posf[:, :, :]).then_inc(s_pos, 1)
                    ch.link(dve.tensor_tensor(past[:, :, :], bcast(iota_b[:, :], 2, E), bcast(endb[0:1, :], 1, NB),
                                              ALU.is_ge))
                    ch.link(dve.tensor_reduce(pastn[:, :], past[:, :, :], AX, ALU.add))
                    ch.link(dve.tensor_scalar(block_expert[:, :], pastn[:, :], float(E - 1), None, ALU.min))
                    dve.wait_ge(s_exp, 2)
                    ch.link(dve.tensor_reduce(soft[:, :], tmp[:, :, :], AX, ALU.add))
                    ch.link(dve.reciprocal(soft[:, :], soft[:, :]))
                    ch.link(dve.tensor_tensor(etop[:, :, :], etop[:, :, :], bcast(soft[:, :], 1, TOPK), ALU.mult))
                    ch.link(dve.tensor_reduce(soft[:, :], etop[:, :, :].rearrange("p j i -> p i j"), AX, ALU.add))
                    ch.link(dve.tensor_scalar(soft[:, :], soft[:, :], 1e-20, None, ALU.add))
                    ch.link(dve.reciprocal(soft[:, :], soft[:, :]))
                    ch.link(dve.tensor_scalar(soft[:, :], soft[:, :], 0.5, None, ALU.mult))
                    ch.link(dve.tensor_tensor(wsel[:, :, :], etop[:, :, :], bcast(soft[:, :], 1, TOPK), ALU.mult))

                    dve.wait_ge(s_ws, 64)
                    for k in range(KFS):
                        last = dve.tensor_scalar(ws2[:, k, :], ws2[:, k, :], gms[:, k:k + 1], None, ALU.mult)
                    last.then_inc(s_fold, 1)
                    dve.wait_ge(s_bz, 3)
                    for n, (dst, src, at, size) in enumerate(lots):
                        dve.wait_ge(s_bias, 48 * (n + 1))
                        for r in (0, 32, 64):
                            if r:
                                ch.link(dve.tensor_copy(bpart[r:r + 1, 0:size], braw[r:r + 1, 0:size]))
                                ch.link(dve.tensor_tensor(braw[r:r + 1, 0:size], braw[r:r + 1, 0:size],
                                                          bpart[r:r + 1, 0:size], ALU.subtract))
                            if r == 64:
                                ch.link(dve.tensor_copy(bpart[r:r + 1, 0:size], braw[r:r + 1, 0:size]))
                                ch.link(dve.tensor_tensor(braw[r:r + 1, 0:size], braw[r:r + 1, 0:size],
                                                          bpart[r:r + 1, 0:size], ALU.subtract))
                            last = dve.tensor_copy(dst[r:r + 1, at:at + size], braw[r:r + 1, 0:size])
                        last.then_inc(s_bdone, 1)
                    dve.wait_ge(s_gm, 16)
                    dve.wait_ge(s_w2, 16 * E)
                    for n in range(E * KF):
                        last = dve.tensor_scalar(w2[:, n * D:(n + 1) * D], w2[:, n * D:(n + 1) * D], gm[:, n:n + 1],
                                                 None, ALU.mult)
                    last.then_inc(s_wfold, 1)

                    with dve.Fori(0, NC // 2) as half:
                        c0 = 2 * half
                        for p in range(2):
                            c = c0 + p
                            for f in range(KFS):
                                dve.wait_ge(s_ge, c * KFS + f + 1)
                                if f == 0:
                                    dve.wait_ge(s_y, c)
                                dve.scalar_tensor_tensor(
                                    aT[:, f, :], ph[f % 2][:, 0, :], bs1[:, f:f + 1], ge[:, f % 2, :],
                                    ALU.add, ALU.mult).then_inc(s_a, 1)
                            dve.wait_ge(s_y, c + 1)
                            dve.wait_ge(s_xr[p], 8 * c0 + 16)
                            dve.scalar_tensor_tensor(xr[p][:, :, :], py[:, :, :], 0.5, xr[p][:, :, :],
                                                     ALU.mult, ALU.add).then_inc(s_acc, 1)

                @block.scalar
                def _(act):
                    act.wait_ge(s_soft, 1)
                    act.activation(tmp[:, :, :], tmp[:, :, :], ACT.Exp).then_inc(s_exp, 1)
                    act.activation(etop[:, :, :], etop[:, :, :], ACT.Exp).then_inc(s_exp, 1)
                    act.wait_ge(s_ws, 64)
                    with act.Fori(0, NC // 2) as half:
                        c0 = 2 * half
                        for p in range(2):
                            c = c0 + p
                            act.wait_ge(s_out[p], 8 * c0)
                            act.dma_start(xr[p][:, :, :], x_v[:, bass.ds(c * TC, TC), :]).then_inc(s_xr[p], 16)
                            act.wait_ge(s_y, c)
                            act.dma_start(xT[p][:, :, :], xnT_v[:, :, bass.ds(c * C, C)]).then_inc(s_xT[p], 16)
                            for f in range(KFS):
                                act.wait_ge(s_h, c * KFS + f + 1)
                                if f >= 2:
                                    act.wait_ge(s_a, c * KFS + f - 1)
                                else:
                                    act.wait_ge(s_a, c * KFS)
                                act.activation(ge[:, f % 2, :], ph[f % 2][:, 1, :], ACT.Gelu,
                                               bias=bs1[:, KFS + f:KFS + f + 1]).then_inc(s_ge, 1)
                            act.wait_ge(s_acc, c + 1)
                            act.dma_start(acc_v[:, bass.ds(c * TC, TC), :], xr[p][:, :, :]).then_inc(s_out[p], 16)
                    for p in range(2):
                        act.wait_ge(s_out[p], 8 * NC)

                @block.tensor
                def _(pe):
                    pe.wait_ge(s_hot, 1)
                    pe.matmul(prank[:, :], tri[:, :], many[:, :, :].rearrange("p i e -> p (i e)"), start=True, stop=True)
                    pe.matmul(ptot[:, :], ones[:, :], many[:, :, :].rearrange("p i e -> p (i e)"), start=True,
                              stop=True).then_inc(s_rank, 1)
                    pe.wait_ge(s_ws, 64)
                    pe.wait_ge(s_fold, 1)
                    pe.wait_ge(s_bdone, len(lots))
                    with pe.Fori(0, NC // 2) as half:
                        c0 = 2 * half
                        for p in range(2):
                            c = c0 + p
                            pe.wait_ge(s_xT[p], 8 * c0 + 16)
                            for f in range(KFS):
                                if f >= 2:
                                    pe.wait_ge(s_a, c * KFS + f - 1)
                                else:
                                    pe.wait_ge(s_a, c * KFS)
                                for side in range(2):
                                    for k in range(KD):
                                        last = pe.matmul(ph[f % 2][:, side, :],
                                                         ws1[:, k, side * FS + f * P:side * FS + (f + 1) * P],
                                                         xT[p][:, k, :], start=k == 0, stop=k == KD - 1)
                                last.then_inc(s_h, 1)
                            pe.wait_ge(s_a, (c + 1) * KFS)
                            pe.wait_ge(s_acc, c)
                            for j in range(TC):
                                pe.matmul(py[:, j, :], ones3[:, :], bs2[:, :], start=True, stop=False)
                                for f in range(KFS):
                                    last = pe.matmul(py[:, j, :], aT[:, f, j * P:(j + 1) * P], ws2[:, f, :],
                                                     start=False, stop=f == KFS - 1)
                            last.then_inc(s_y, 1)

        def experts(tag, w1, w2, b1, b2):
            def s(n):
                return sem(f"{tag}e_{n}")
            s_in = [s(f"in{p}") for p in range(2)]
            s_out = [s(f"out{p}") for p in range(2)]
            s_tr, s_xT, s_h, s_ge, s_a, s_atr, s_aT, s_y, s_ysb = (
                s(n) for n in ("tr", "xT", "h", "ge", "a", "atr", "aT", "y", "ysb"))
            with ExitStack() as sc:
                rows = [sb(f"{tag}_rows{p}", [P, D], scope=sc) for p in range(2)]
                xT = [sb(f"{tag}_exT{p}", [P, KD, P], scope=sc) for p in range(2)]
                ge = [sb(f"{tag}_ege{p}", [P, F], scope=sc) for p in range(2)]
                a = [sb(f"{tag}_ea{p}", [P, F], scope=sc) for p in range(2)]
                aT = [sb(f"{tag}_eaT{p}", [P, KF, P], scope=sc) for p in range(2)]
                y = [sb(f"{tag}_ey{p}", [P, D], scope=sc) for p in range(2)]
                pT = [ps(f"{tag}_epT{p}", [P, KD, P], scope=sc) for p in range(2)]
                ph = [ps(f"{tag}_eph{p}", [P, 2 * F], scope=sc) for p in range(2)]
                pA = [ps(f"{tag}_epA{p}", [P, KF, P], scope=sc) for p in range(2)]
                py = [ps(f"{tag}_epy{p}", [P, D], scope=sc) for p in range(2)]
                block = sc.enter_context(nc.Block())

                @block.sync
                def _(sp):
                    with sp.Fori(0, NB // 2) as pair:
                        b0 = 2 * pair
                        for p in range(2):
                            b = b0 + p
                            sp.wait_ge(s_tr, b0 + p - 1 if p else b0)
                            sp.dma_start(rows[p][:, :], rows_dram[bass.ds(b * P, P), :]).then_inc(s_in[p], 16)

                @block.gpsimd
                def _(pool):
                    with pool.Fori(0, NB // 2) as pair:
                        b0 = 2 * pair
                        for p in range(2):
                            b = b0 + p
                            pool.wait_ge(s_ysb, b + 1)
                            pool.dma_start(yrows_dram[bass.ds(b * P, P), :], y[p][:, :]).then_inc(s_out[p], 16)
                    for p in range(2):
                        pool.wait_ge(s_out[p], 8 * NB)

                @block.scalar
                def _(act):
                    def copy_x(b, p):
                        act.wait_ge(s_tr, b + 1)
                        if not isinstance(b, int) or b >= 2:
                            act.wait_ge(s_h, b - 1)
                        act.activation(xT[p][:, :, :], pT[p][:, :, :], ACT.Copy).then_inc(s_xT, 1)

                    def gelu(b, p):
                        act.wait_ge(s_h, b + 1)
                        if not isinstance(b, int) or b >= 2:
                            act.wait_ge(s_a, b - 1)
                        act.activation(ge[p][:, :], ph[p][:, F:2 * F], ACT.Gelu).then_inc(s_ge, 1)

                    def copy_y(b, p, b0):
                        act.wait_ge(s_y, b + 1)
                        if b0 is not None:
                            act.wait_ge(s_out[p], 8 * b0)
                        act.activation(y[p][:, :], py[p][:, :], ACT.Copy).then_inc(s_ysb, 1)

                    copy_x(0, 0)
                    copy_x(1, 1)
                    gelu(0, 0)
                    copy_x(2, 0)
                    gelu(1, 1)
                    copy_y(0, 0, None)
                    copy_x(3, 1)
                    gelu(2, 0)
                    copy_y(1, 1, None)
                    with act.Fori(2, NB // 2) as pair:
                        b0 = 2 * pair
                        for p in range(2):
                            b = b0 + p
                            copy_x(b, p)
                            gelu(b - 1, 1 - p)
                            copy_y(b - 2, p, b0 - 2)
                    gelu(NB - 1, 1)
                    copy_y(NB - 2, 0, NB - 2)
                    copy_y(NB - 1, 1, NB - 2)

                @block.vector
                def _(dve):
                    def product(b, p):
                        dve.wait_ge(s_ge, b + 1)
                        if not isinstance(b, int) or b >= 2:
                            dve.wait_ge(s_atr, b - 1)
                        dve.tensor_tensor(a[p][:, :], ph[p][:, 0:F], ge[p][:, :], ALU.mult).then_inc(s_a, 1)

                    def copy_a(b, p):
                        dve.wait_ge(s_atr, b + 1)
                        if not isinstance(b, int) or b >= 2:
                            dve.wait_ge(s_y, b - 1)
                        dve.tensor_copy(aT[p][:, :, :], pA[p][:, :, :]).then_inc(s_aT, 1)

                    product(0, 0)
                    product(1, 1)
                    copy_a(0, 0)
                    with dve.Fori(1, NB // 2) as pair:
                        b0 = 2 * pair
                        for p in range(2):
                            b = b0 + p
                            product(b, p)
                            copy_a(b - 1, 1 - p)
                    copy_a(NB - 1, 1)

                @block.tensor
                def _(pe):
                    def turn_x(b, p, loads):
                        pe.wait_ge(s_in[p], loads)
                        if not isinstance(b, int) or b >= 2:
                            pe.wait_ge(s_xT, b - 1)
                        for k in range(KD):
                            last = pe.transpose(pT[p][:, k, :], rows[p][:, k * P:(k + 1) * P], ident[:, :])
                        last.then_inc(s_tr, 1)

                    def fc1(b, p):
                        e = pe.value_load(block_expert[0:1, bass.ds(b, 1)], min_val=0, max_val=E - 1)
                        pe.wait_ge(s_xT, b + 1)
                        if not isinstance(b, int) or b >= 2:
                            pe.wait_ge(s_a, b - 1)
                        pe.matmul(ph[p][:, :], ones3[:, :], b1[:, bass.ds(e * (2 * F), 2 * F)], start=True, stop=False)
                        for k in range(KD):
                            last = pe.matmul(ph[p][:, :], xT[p][:, k, :],
                                             w1[:, bass.ds(e * (KD * 2 * F) + k * 2 * F, 2 * F)],
                                             start=False, stop=k == KD - 1)
                        last.then_inc(s_h, 1)

                    def turn_a(b, p):
                        pe.wait_ge(s_a, b + 1)
                        if not isinstance(b, int) or b >= 2:
                            pe.wait_ge(s_aT, b - 1)
                        for k in range(KF):
                            last = pe.transpose(pA[p][:, k, :], a[p][:, k * P:(k + 1) * P], ident[:, :])
                        last.then_inc(s_atr, 1)

                    def fc2(b, p):
                        e = pe.value_load(block_expert[0:1, bass.ds(b, 1)], min_val=0, max_val=E - 1)
                        pe.wait_ge(s_aT, b + 1)
                        if not isinstance(b, int) or b >= 2:
                            pe.wait_ge(s_ysb, b - 1)
                        pe.matmul(py[p][:, :], ones3[:, :], b2[:, bass.ds(e * D, D)], start=True, stop=False)
                        for k in range(KF):
                            last = pe.matmul(py[p][:, :], aT[p][:, k, :], w2[:, bass.ds(e * (KF * D) + k * D, D)],
                                             start=False, stop=k == KF - 1)
                        last.then_inc(s_y, 1)

                    turn_x(0, 0, 16)
                    turn_x(1, 1, 16)
                    fc1(0, 0)
                    turn_x(2, 0, 32)
                    fc1(1, 1)
                    turn_a(0, 0)
                    for b in (2, 3):
                        turn_x(b + 1, (b + 1) % 2, 16 * ((b + 1) // 2 + 1))
                        fc1(b, b % 2)
                        fc2(b - 2, b % 2)
                        turn_a(b - 1, (b - 1) % 2)
                    with pe.Fori(2, NB // 2 - 1) as pair:
                        b0 = 2 * pair
                        for p in range(2):
                            b = b0 + p
                            turn_x(b + 1, 1 - p, 8 * b0 + 16 + 16 * p)
                            fc1(b, p)
                            fc2(b - 2, p)
                            turn_a(b - 1, 1 - p)
                    turn_x(NB - 1, 1, 8 * NB)
                    fc1(NB - 2, 0)
                    fc2(NB - 4, 0)
                    turn_a(NB - 3, 1)
                    fc1(NB - 1, 1)
                    fc2(NB - 3, 1)
                    turn_a(NB - 2, 0)
                    turn_a(NB - 1, 1)
                    fc2(NB - 2, 0)
                    fc2(NB - 1, 1)

        def phase_attention():
            names = ("acc", "idx", "gath", "x1", "st", "sd", "y", "tr", "yT", "xx", "low", "lowT", "mus", "tm", "xi",
                     "vps", "vT", "vt", "rps", "rT", "kps", "kT", "w1p", "w1T", "w2p", "dec", "gps", "sg",
                     "vr", "S", "P", "o", "rk", "cp", "z", "ztr", "zT", "wo", "x2", "st2", "sd2", "n2", "ntr", "nT", "lg",
                     "dve", "act", "pool", "w", "sel", "gsd", "gst", "ew")
            S = {n: sem(f"t_{n}") for n in names}
            s_out = sem("t_out")
            s_outT = sem("t_outT")
            with ExitStack() as sc:
                def t(n, shape, dt=FP32):
                    return sb(f"t_{n}", shape, dt, scope=sc)
                wx1 = t("wx1", [P, KD, 5 * LR])
                wx2 = t("wx2", [P, D])
                wx2l = t("wx2l", [LR, D])
                xb = t("xb", [P, KD, 5])
                mu = t("mu", [P, KD])
                wr, wk = t("wr", [P, KD, P]), t("wk", [P, KD, P])
                ww1 = t("ww1", [P, KD, GL])
                ww2 = t("ww2", [GL, P])
                bw2 = t("bw2", [P, 1])
                wv, wvT, wg, wo = (t(n, [P, KD, D]) for n in ("wv", "wvT", "wg", "wo"))
                gnw, gnb = t("gnw", [P, D]), t("gnb", [P, D])
                uk = t("uk", [P, 1])
                sel = t("sel", [P, 8, H, DK])
                headsum = t("headsum", [P, H])
                uhead = t("uhead", [P, H])
                acc = t("acc", [P, TC, D])
                gath = t("gath", [P, TOPK, TC, D])
                idx = t("idx", [P, TOPK, TC], I32)
                wc = t("wc", [P, TOPK, TC])
                x1 = t("x1", [P, TC, D])
                st = t("st", [P, TC, 6])
                mv = t("mv", [P, TC, 2])
                sd = t("sd", [P, TC])
                rs = t("rs", [P, TC])
                y = t("y", [P, TC, D])
                yT = t("yT", [P, KD, C + 1])
                dl = t("dl", [P, KD, C])
                xx = t("xx", [P, KD, C])
                lowT = t("lowT", [P, C])
                lowTl = t("lowTl", [LR, C])
                tm = t("tm", [P, 2, C])
                xi = t("xi", [P, KD, C])
                rT, kT, ew = t("rT", [P, C]), t("kT", [P, C]), t("ew", [P, C])
                dec = t("dec", [P, C])
                w1T = t("w1T", [GL, C])
                vT = t("vT", [P, KD, C])
                vt = t("vt", [P, TC, D])
                sg = t("sg", [P, TC, D])
                kv = [t(f"kv{q}", [P, 2, C]) for q in range(2)]
                St = [t(f"S{q}", [P, 2, C + 1]) for q in range(2)]
                Pr = [t(f"P{q}", [P, 2, C]) for q in range(2)]
                carry = t("carry", [P, DV])
                rk = t("rk", [P, C])
                cs = t("cs", [P, TC * H])
                o = t("o", [P, TC, D])
                o2 = t("o2", [P, TC, D])
                gs = t("gs", [P, TC * H])
                gm_ = t("gm", [P, TC * H])
                zT = t("zT", [P, KD, C])
                psR = [ps(f"t_psR{q}", [P, 2, C], scope=sc) for q in range(2)]
                psO = ps("t_psO", [P, TC, D], scope=sc)
                psM = [ps(f"t_psM{q}", [P, C], scope=sc) for q in range(2)]

                acc_v = acc_dram.rearrange("(i p) d -> p i d", p=P)
                x2_v = x2_dram.rearrange("(i p) d -> p i d", p=P)
                xn_v = xn_dram.rearrange("(i p) d -> p i d", p=P)
                xnT_v = xnT_dram.rearrange("(k p) t -> p k t", p=P)
                order = (MIX_V, MIX_R, MIX_K, MIX_W, MIX_G)
                block = sc.enter_context(nc.Block())

                @block.sync
                def _(sp):
                    n = 0
                    with nc.allow_non_contiguous_dma(reason="small per-channel vectors"):
                        for dst, src in (
                                (wx1[:, :, :], W_x1.rearrange("(k p) r -> p k r", p=P)),
                                (wx2[:, :], W_x2[0:P, :]), (wx2l[:, :], W_x2[P:P + LR, :]),
                                (xb[:, :, :], x_biasT.rearrange("(k p) i -> p k i", p=P)),
                                (mu[:, :], mu_x.rearrange("(k p) -> p k", p=P)),
                                (wr[:, :, :], W_r.rearrange("(k p) m -> p k m", p=P)),
                                (wk[:, :, :], W_k.rearrange("(k p) m -> p k m", p=P)),
                                (ww1[:, :, :], W_w1.rearrange("(k p) m -> p k m", p=P)),
                                (ww2[:, :], W_w2[:, :]), (bw2[:, :], b_w2.unsqueeze(1)),
                                (wv[:, :, :], W_v.rearrange("(k p) m -> p k m", p=P)),
                                (wvT[:, :, :], W_v_vh.rearrange("(k p) m -> p k m", p=P)),
                                (wg[:, :, :], W_g.rearrange("(k p) m -> p k m", p=P)),
                                (wo[:, :, :], W_o.rearrange("(k p) m -> p k m", p=P)),
                                (gnw[:, :], bcast(gn_w, 0, P)), (gnb[:, :], bcast(gn_b, 0, P)),
                                (uk[:, :], u.rearrange("h k -> (h k)").unsqueeze(1))):
                            sp.dma_start(dst, src).then_inc(S["w"], 16)
                            n += 1
                    assert n == 17
                    with sp.Fori(0, NC) as c:
                        sp.wait_ge(S["x1"], c)
                        sp.dma_start(acc[:, :, :], acc_v[:, bass.ds(c * TC, TC), :]).then_inc(S["acc"], 16)
                        sp.wait_ge(S["x2"], c + 1)
                        sp.dma_start(x2_v[:, bass.ds(c * TC, TC), :], o[:, :, :]).then_inc(s_out, 16)
                        sp.wait_ge(S["n2"], c + 1)
                        sp.dma_start(xn_v[:, bass.ds(c * TC, TC), :], o2[:, :, :]).then_inc(s_out, 16)
                        sp.wait_ge(S["nT"], c + 1)
                        sp.dma_start(xnT_v[:, :, bass.ds(c * C, C)], zT[:, :, :]).then_inc(s_outT, 16)
                    sp.wait_ge(s_out, 32 * NC)
                    sp.wait_ge(s_outT, 16 * NC)

                @block.gpsimd
                def _(pool):
                    pool.memset(sel[:, :, :, :], 0.0).then_inc(S["sel"], 1)
                    pool.memset(headsum[:, :], 1.0).then_inc(S["sel"], 1)
                    pool.memset(carry[:, :], 0.0).then_inc(S["sel"], 1)
                    pool.memset(yT[:, :, C:C + 1], 0.0).then_inc(S["sel"], 1)
                    pool.wait_ge(S["sel"], 4)
                    pool.affine_select(out=sel[:, :, :, :], in_=sel[:, :, :, :], compare_op=ALU.not_equal, fill=1.0,
                                       base=0, pattern=[[-16, 8], [-1, H], [0, DK]], channel_multiplier=1
                                       ).then_inc(S["sel"], 1)
                    pool.affine_select(out=headsum[:, :], in_=headsum[:, :], compare_op=ALU.is_ge, fill=0.0,
                                       base=0, pattern=[[-DK, H]], channel_multiplier=1).then_inc(S["sel"], 1)
                    pool.wait_ge(S["sel"], 6)
                    pool.affine_select(out=headsum[:, :], in_=headsum[:, :], compare_op=ALU.is_ge, fill=0.0,
                                       base=DK - 1, pattern=[[DK, H]], channel_multiplier=-1).then_inc(S["sel"], 1)
                    pool.wait_ge(S["sel"], 7)
                    pool.wait_ge(S["w"], 16 * 17)
                    pool.tensor_scalar(uhead[:, :], headsum[:, :], uk[:, 0:1], None, ALU.mult).then_inc(S["sel"], 1)
                    with pool.Fori(0, NC) as c:
                        pool.tensor_copy(idx[:, :, :], pos[:, :, bass.ds(c * TC, TC)]).then_inc(S["idx"], 1)
                        pool.wait_ge(S["idx"], c + 1)
                        pool.wait_ge(S["x1"], c)
                        pool.tensor_tensor(pad[:, 1:2], eps[:, :], eps[:, :], ALU.add)
                        for j in range(TOPK):
                            for i in range(TC):
                                pool.indirect_dma_start(
                                    out=gath[:, j, i, :], out_offset=None, in_=yrows_dram[:, :],
                                    in_offset=bass.IndirectOffsetOnAxis(ap=idx[:, j, i:i + 1], axis=0)
                                    ).then_inc(S["gath"], 16)
                        for n in range(5):
                            for k in range(KD):
                                m = 2 * n + k
                                pool.wait_ge(S["tm"], 10 * c + m + 1)
                                if k == 0:
                                    if n == 1:
                                        pool.wait_ge(S["vps"], 2 * c + 2)
                                    if n == 2:
                                        pool.wait_ge(S["rps"], c + 1)
                                    if n == 3:
                                        pool.wait_ge(S["kps"], c + 1)
                                    if n == 4:
                                        pool.wait_ge(S["w1p"], c + 1)
                                    if n == 0:
                                        pool.wait_ge(S["gps"], c)
                                pool.tensor_tensor(xi[:, k, :], tm[:, m % 2, :], yT[:, k, 1:C + 1],
                                                   ALU.add).then_inc(S["xi"], 1)
                        pool.wait_ge(S["rT"], c + 1)
                        pool.wait_ge(S["kT"], c + 1)
                        pool.wait_ge(S["cp"], c)
                        pool.tensor_tensor(rk[:, :], rT[:, :], kT[:, :], ALU.mult).then_inc(S["rk"], 1)
                        for g in range(8):
                            pool.wait_ge(S["S"], 8 * c + g + 1)
                            pool.wait_ge(S["o"], 8 * c + g - 1 if g >= 1 else 8 * c)
                            pool.tensor_tensor(Pr[g % 2][:, :, :], St[g % 2][:, :, 0:C], bcast(rT[:, :], 1, 2),
                                               ALU.mult).then_inc(S["P"], 1)

                @block.vector
                def _(dve):
                    dve.wait_ge(S["w"], 16 * 17)
                    dve.wait_ge(S["sel"], 8)
                    PER = 36
                    with dve.Fori(0, NC) as c:
                        ch = Chain(dve, S["dve"], c, PER)
                        ch.link(dve.tensor_copy(wc[:, :, :], wsel[:, :, bass.ds(c * TC, TC)]))
                        dve.wait_ge(S["acc"], 16 * (c + 1))
                        dve.wait_ge(S["gath"], 16 * TOPK * TC * (c + 1))
                        for j in range(TOPK):
                            for i in range(TC):
                                last = dve.scalar_tensor_tensor(
                                    x1[:, i, :], gath[:, j, i, :], wc[:, j, i:i + 1],
                                    acc[:, i, :] if j == 0 else x1[:, i, :], ALU.mult, ALU.add)
                            if j < TOPK - 1:
                                ch.link(last)
                        last.then_inc(S["x1"], 1)
                        dve.wait_ge(S["x1"], c + 1)
                        for i in range(TC):
                            last = dve.bn_stats(st[:, i, :], x1[:, i, :])
                        ch.link(last)
                        dve.memset(pad[:, 0:1], 0.0)
                        for i in range(TC):
                            last = dve.bn_aggr(mv[:, i, :], st[:, i, :])
                        last.then_inc(S["st"], 1)
                        dve.wait_ge(S["sd"], c + 1)
                        ch.link(dve.reciprocal(rs[:, :], sd[:, :]))
                        for i in range(TC):
                            last = dve.tensor_scalar(y[:, i, :], x1[:, i, :], mv[:, i, 0:1], rs[:, i:i + 1],
                                                     ALU.subtract, ALU.mult)
                        last.then_inc(S["y"], 1)
                        dve.wait_ge(S["yT"], c + 1)
                        ch.link(dve.tensor_tensor(dl[:, :, :], yT[:, :, 0:C], yT[:, :, 1:C + 1], ALU.subtract))
                        for k in range(KD):
                            last = dve.scalar_tensor_tensor(xx[:, k, :], dl[:, k, :], mu[:, k:k + 1],
                                                            yT[:, k, 1:C + 1], ALU.mult, ALU.add)
                        last.then_inc(S["xx"], 1)
                        for n in range(5):
                            for k in range(KD):
                                m = 2 * n + k
                                dve.wait_ge(S["mus"], 10 * c + m + 1)
                                if m >= 2:
                                    dve.wait_ge(S["xi"], 10 * c + m - 1)
                                dve.scalar_tensor_tensor(tm[:, m % 2, :], psM[m % 2][:, :],
                                                         xb[:, k, order[n]:order[n] + 1], dl[:, k, :],
                                                         ALU.add, ALU.mult).then_inc(S["tm"], 1)
                        dve.wait_ge(S["kT"], c + 1)
                        dve.wait_ge(S["dec"], c + 1)
                        for g in range(8):
                            q = g % 2
                            dve.wait_ge(S["vr"], 8 * c + g + 1)
                            dve.tensor_tensor(kv[q][:, :, :], psR[q][:, :, :], bcast(kT[:, :], 1, 2), ALU.mult)
                            dve.wait_ge(S["P"], 8 * c + g - 1 if g >= 1 else 8 * c)
                            ch.link(dve.tensor_copy(St[q][:, :, 0:1], carry[:, 2 * g:2 * g + 2].unsqueeze(2)))
                            for j in range(2):
                                last = dve.tensor_tensor_scan(St[q][:, j, 1:C + 1], dec[:, :], kv[q][:, j, :],
                                                              St[q][:, j, 0:1], ALU.mult, ALU.add)
                            last.then_inc(S["S"], 1)
                            dve.wait_ge(S["S"], 8 * c + g + 1)
                            ch.link(dve.tensor_copy(carry[:, 2 * g:2 * g + 2].unsqueeze(2), St[q][:, :, C:C + 1]))
                        dve.wait_ge(S["cp"], c + 1)
                        dve.wait_ge(S["vt"], c + 1)
                        ch.link(dve.tensor_copy(cs[:, :], psM[0][:, 0:TC * H]))
                        dve.wait_ge(s_out, 32 * c)
                        o_h = o[:, :, :].rearrange("p i (h v) -> p (i h) v", v=DV)
                        o2_h = o2[:, :, :].rearrange("p i (h v) -> p (i h) v", v=DV)
                        vt_h = vt[:, :, :].rearrange("p i (h v) -> p (i h) v", v=DV)
                        ch.link(dve.tensor_tensor(o_h, vt_h, bcast(cs[:, :], 2, DV), ALU.mult))
                        dve.wait_ge(S["o"], 8 * (c + 1))
                        ch.link(dve.tensor_tensor(o[:, :, :], psO[:, :, :], o[:, :, :], ALU.add))
                        ch.link(dve.tensor_reduce(gs[:, :], o_h, AX, ALU.add))
                        ch.link(dve.tensor_scalar(gs[:, :], gs[:, :], 1.0 / DV, None, ALU.mult))
                        ch.link(dve.tensor_tensor(o_h, o_h, bcast(gs[:, :], 2, DV), ALU.subtract))
                        ch.link(dve.tensor_tensor(o2_h, o_h, o_h, ALU.mult))
                        dve.tensor_reduce(gm_[:, :], o2_h, AX, ALU.add).then_inc(S["gst"], 1)
                        dve.wait_ge(S["gsd"], c + 1)
                        ch.link(dve.reciprocal(gs[:, :], gm_[:, :]))
                        ch.link(dve.tensor_tensor(o_h, o_h, bcast(gs[:, :], 2, DV), ALU.mult))
                        ch.link(dve.tensor_tensor(o[:, :, :], o[:, :, :], bcast(gnw[:, :], 1, TC), ALU.mult))
                        ch.link(dve.tensor_tensor(o[:, :, :], o[:, :, :], bcast(gnb[:, :], 1, TC), ALU.add))
                        dve.wait_ge(S["sg"], c + 1)
                        dve.tensor_tensor(o2[:, :, :], o[:, :, :], sg[:, :, :], ALU.mult).then_inc(S["z"], 1)
                        dve.wait_ge(S["z"], c + 1)
                        dve.wait_ge(S["wo"], c + 1)
                        dve.tensor_tensor(o[:, :, :], psR[1][:, :, :].rearrange("p a b -> p (a b)"),
                                          x1[:, :, :].rearrange("p i d -> p (i d)"), ALU.add).then_inc(S["x2"], 1)
                        dve.wait_ge(S["x2"], c + 1)
                        for i in range(TC):
                            last = dve.bn_stats(st[:, i, :], o[:, i, :])
                        ch.link(last)
                        dve.memset(pad[:, 0:1], 0.0)
                        for i in range(TC):
                            last = dve.bn_aggr(mv[:, i, :], st[:, i, :])
                        last.then_inc(S["st2"], 1)
                        dve.wait_ge(S["sd2"], c + 1)
                        ch.link(dve.reciprocal(rs[:, :], sd[:, :]))
                        for i in range(TC):
                            last = dve.tensor_scalar(o2[:, i, :], o[:, i, :], mv[:, i, 0:1], rs[:, i:i + 1],
                                                     ALU.subtract, ALU.mult)
                        last.then_inc(S["n2"], 1)
                        dve.wait_ge(S["lg"], c + 1)
                        ch.link(dve.tensor_copy(logits[:, bass.ds(c * TC, TC), :],
                                                psM[1][:, :].rearrange("p (i e) -> p i e", e=P)[:, :, 0:E]))
                        ch.close()

                @block.scalar
                def _(act):
                    act.wait_ge(S["sel"], 8)
                    with act.Fori(0, NC) as c:
                        act.wait_ge(S["st"], c + 1)
                        act.activation(sd[:, :], mv[:, :, 1], ACT.Sqrt, bias=eps[:, 0:1]).then_inc(S["sd"], 1)
                        act.wait_ge(S["xi"], 10 * c)
                        act.activation(yT[:, :, 0:1], yT[:, :, C:C + 1], ACT.Copy).then_inc(S["act"], 1)
                        act.wait_ge(S["act"], c + 1)
                        act.wait_ge(S["tr"], c + 1)
                        act.activation(yT[:, :, 1:C + 1], psR[0][:, :, :], ACT.Copy).then_inc(S["yT"], 1)
                        act.wait_ge(S["low"], c + 1)
                        act.activation(lowT[:, :], psR[1][:, 0, :], ACT.Tanh)
                        act.activation(lowTl[:, :], psR[1][0:LR, 1, :], ACT.Tanh).then_inc(S["lowT"], 1)
                        act.wait_ge(S["vps"], 2 * c + 1)
                        act.activation(vT[:, :, :], psR[0][:, :, :], ACT.Copy).then_inc(S["vT"], 1)
                        act.wait_ge(S["vps"], 2 * c + 2)
                        act.activation(vt[:, :, :], psR[1][:, :, :].rearrange("p a (b d) -> p (a b) d", d=D),
                                       ACT.Copy).then_inc(S["vt"], 1)
                        act.wait_ge(S["rps"], c + 1)
                        act.activation(rT[:, :], psR[0][:, 0, :], ACT.Copy).then_inc(S["rT"], 1)
                        act.wait_ge(S["kps"], c + 1)
                        act.activation(kT[:, :], psR[0][:, 1, :], ACT.Copy).then_inc(S["kT"], 1)
                        act.wait_ge(S["w1p"], c + 1)
                        act.activation(w1T[:, :], psR[1][0:GL, 0, :], ACT.Tanh).then_inc(S["w1T"], 1)
                        act.wait_ge(S["w2p"], c + 1)
                        act.activation(ew[:, :], psR[1][:, 1, :], ACT.Exp, bias=bw2[:, 0:1]).then_inc(S["ew"], 1)
                        act.wait_ge(S["ew"], c + 1)
                        act.activation(dec[:, :], ew[:, :], ACT.Exp, scale=-1.0).then_inc(S["dec"], 1)
                        act.wait_ge(S["gps"], c + 1)
                        act.activation(sg[:, :, :], psO[:, :, :], ACT.Silu).then_inc(S["sg"], 1)
                        act.wait_ge(S["gst"], c + 1)
                        act.activation(gm_[:, :], gm_[:, :], ACT.Sqrt, bias=eps[:, 0:1],
                                       scale=1.0 / DV).then_inc(S["gsd"], 1)
                        act.wait_ge(S["ztr"], c + 1)
                        act.wait_ge(s_outT, 16 * c)
                        act.activation(zT[:, :, :], psR[0][:, :, :], ACT.Copy).then_inc(S["zT"], 1)
                        act.wait_ge(S["st2"], c + 1)
                        act.activation(sd[:, :], mv[:, :, 1], ACT.Sqrt, bias=eps[:, 0:1]).then_inc(S["sd2"], 1)
                        act.wait_ge(S["ntr"], c + 1)
                        act.activation(zT[:, :, :], psR[0][:, :, :], ACT.Copy).then_inc(S["nT"], 1)

                @block.tensor
                def _(pe):
                    pe.wait_ge(S["sel"], 8)
                    pe.wait_ge(S["w"], 16 * 17)

                    def turn(dst, src, done):
                        for k in range(KD):
                            for i in range(TC):
                                last = pe.transpose(dst[:, k, i * P:(i + 1) * P], src[:, i, k * P:(k + 1) * P],
                                                    ident[:, :])
                        last.then_inc(done, 1)

                    def project(dst, w, src):
                        for k in range(KD):
                            last = pe.matmul(dst, w(k), src(k), start=k == 0, stop=k == KD - 1)
                        return last

                    def by_token(dst, w, src, done):
                        for i in range(TC):
                            last = project(dst[:, i, :], lambda k: src[:, k, i * P:(i + 1) * P], lambda k: w[:, k, :])
                        last.then_inc(done, 1)

                    with pe.Fori(0, NC) as c:
                        pe.wait_ge(S["y"], c + 1)
                        pe.wait_ge(S["nT"], c)
                        turn(psR[0], y, S["tr"])
                        pe.wait_ge(S["xx"], c + 1)
                        project(psR[1][:, 0, :], lambda k: wx1[:, k, 0:P], lambda k: xx[:, k, :])
                        project(psR[1][0:LR, 1, :], lambda k: wx1[:, k, P:P + LR],
                                lambda k: xx[:, k, :]).then_inc(S["low"], 1)
                        pe.wait_ge(S["lowT"], c + 1)
                        for n in range(5):
                            i = order[n]
                            for k in range(KD):
                                m = 2 * n + k
                                if m >= 2:
                                    pe.wait_ge(S["tm"], 10 * c + m - 1)
                                if i < 4:
                                    ins = pe.matmul(psM[m % 2][:, :], wx2[i * LR:(i + 1) * LR, k * P:(k + 1) * P],
                                                    lowT[i * LR:(i + 1) * LR, :], start=True, stop=True)
                                else:
                                    ins = pe.matmul(psM[m % 2][:, :], wx2l[:, k * P:(k + 1) * P], lowTl[:, :],
                                                    start=True, stop=True)
                                ins.then_inc(S["mus"], 1)
                            pe.wait_ge(S["xi"], 10 * c + 2 * n + 2)
                            if i == MIX_V:
                                for half in range(KD):
                                    last = project(psR[0][:, half, :], lambda k: wvT[:, k, half * P:(half + 1) * P],
                                                   lambda k: xi[:, k, :])
                                last.then_inc(S["vps"], 1)
                                by_token(psR[1][:, :, :].rearrange("p a (b d) -> p (a b) d", d=D), wv, xi, S["vps"])
                            if i == MIX_R:
                                pe.wait_ge(S["vT"], c + 1)
                                project(psR[0][:, 0, :], lambda k: wr[:, k, :], lambda k: xi[:, k, :]).then_inc(S["rps"], 1)
                            if i == MIX_K:
                                project(psR[0][:, 1, :], lambda k: wk[:, k, :], lambda k: xi[:, k, :]).then_inc(S["kps"], 1)
                            if i == MIX_W:
                                pe.wait_ge(S["vt"], c + 1)
                                project(psR[1][0:GL, 0, :], lambda k: ww1[:, k, :],
                                        lambda k: xi[:, k, :]).then_inc(S["w1p"], 1)
                                pe.wait_ge(S["w1T"], c + 1)
                                pe.matmul(psR[1][:, 1, :], ww2[:, :], w1T[:, :], start=True,
                                          stop=True).then_inc(S["w2p"], 1)
                            if i == MIX_G:
                                by_token(psO, wg, xi, S["gps"])
                        pe.wait_ge(S["kT"], c + 1)
                        pe.wait_ge(S["dec"], c + 1)
                        pe.wait_ge(S["rk"], c + 1)
                        for i in range(TC):
                            last = pe.matmul(psM[0][:, i * H:(i + 1) * H], rk[:, i * P:(i + 1) * P], uhead[:, :],
                                             start=True, stop=True)
                        last.then_inc(S["cp"], 1)
                        pe.wait_ge(S["sg"], c + 1)

                        def spread(g):
                            if g >= 2:
                                pe.wait_ge(S["S"], 8 * c + g - 1)
                            for j in range(2):
                                v = 2 * g + j
                                last = pe.matmul(psR[g % 2][:, j, :], sel[:, v % 8, :, :].rearrange("p h k -> p (h k)"),
                                                 vT[:, v // 8, :], start=True, stop=True)
                            last.then_inc(S["vr"], 1)

                        def head_sums(g):
                            pe.wait_ge(S["P"], 8 * c + g + 1)
                            for j in range(2):
                                v = 2 * g + j
                                for i in range(TC):
                                    last = pe.matmul(psO[:, i, v:D:DV], Pr[g % 2][:, j, i * P:(i + 1) * P],
                                                     headsum[:, :], start=True, stop=True)
                            last.then_inc(S["o"], 1)
                        spread(0)
                        spread(1)
                        for g in range(8):
                            head_sums(g)
                            if g + 2 < 8:
                                spread(g + 2)
                        pe.wait_ge(S["z"], c + 1)
                        turn(psR[0], o2, S["ztr"])
                        pe.wait_ge(S["zT"], c + 1)
                        by_token(psR[1][:, :, :].rearrange("p a (b d) -> p (a b) d", d=D), wo, zT, S["wo"])
                        pe.wait_ge(S["n2"], c + 1)
                        turn(psR[0], o2, S["ntr"])
                        pe.wait_ge(S["nT"], c + 1)
                        for i in range(TC):
                            last = project(psM[1][:, i * P:i * P + E], lambda k: zT[:, k, i * P:(i + 1) * P],
                                           lambda k: gate[:, k, :])
                        last.then_inc(S["lg"], 1)

        def phase_out():
            s_acc = [sem(f"f_acc{p}") for p in range(2)]
            s_gath = [sem(f"f_gath{p}") for p in range(2)]
            s_out = [sem(f"f_out{p}") for p in range(2)]
            s_idx, s_sum, s_dve = (sem(f"f_{n}") for n in ("idx", "sum", "dve"))
            with ExitStack() as sc:
                acc = [sb(f"f_acc{p}", [P, TC, D], scope=sc) for p in range(2)]
                gath = [sb(f"f_gath{p}", [P, TOPK, TC, D], scope=sc) for p in range(2)]
                idx = [sb(f"f_idx{p}", [P, TOPK, TC], I32, scope=sc) for p in range(2)]
                wc = [sb(f"f_wc{p}", [P, TOPK, TC], scope=sc) for p in range(2)]
                acc_v = acc_dram.rearrange("(i p) d -> p i d", p=P)
                out_v = out.rearrange("a (i p) d -> p (a i) d", p=P)
                block = sc.enter_context(nc.Block())

                @block.sync
                def _(sp):
                    with sp.Fori(0, NC // 2) as half:
                        c0 = 2 * half
                        for p in range(2):
                            c = c0 + p
                            sp.wait_ge(s_out[p], 8 * c0)
                            sp.dma_start(acc[p][:, :, :], acc_v[:, bass.ds(c * TC, TC), :]).then_inc(s_acc[p], 16)

                @block.scalar
                def _(act):
                    with act.Fori(0, NC // 2) as half:
                        c0 = 2 * half
                        for p in range(2):
                            c = c0 + p
                            act.wait_ge(s_sum, c + 1)
                            act.dma_start(out_v[:, bass.ds(c * TC, TC), :], acc[p][:, :, :]).then_inc(s_out[p], 16)
                    for p in range(2):
                        act.wait_ge(s_out[p], 8 * NC)

                @block.gpsimd
                def _(pool):
                    with pool.Fori(0, NC // 2) as half:
                        c0 = 2 * half
                        for p in range(2):
                            c = c0 + p
                            pool.wait_ge(s_sum, c0 + p - 1 if p else c0)
                            pool.wait_ge(s_idx, 3 * c)
                            pool.tensor_tensor(pad[:, 1:2], eps[:, :], eps[:, :], ALU.add).then_inc(s_idx, 1)
                            pool.wait_ge(s_idx, 3 * c + 1)
                            pool.tensor_copy(idx[p][:, :, :], pos[:, :, bass.ds(c * TC, TC)]).then_inc(s_idx, 1)
                            pool.wait_ge(s_idx, 3 * c + 2)
                            pool.tensor_tensor(pad[:, 1:2], eps[:, :], eps[:, :], ALU.add).then_inc(s_idx, 1)
                            for j in range(TOPK):
                                for i in range(TC):
                                    pool.indirect_dma_start(
                                        out=gath[p][:, j, i, :], out_offset=None, in_=yrows_dram[:, :],
                                        in_offset=bass.IndirectOffsetOnAxis(ap=idx[p][:, j, i:i + 1], axis=0)
                                        ).then_inc(s_gath[p], 16)

                @block.vector
                def _(dve):
                    with dve.Fori(0, NC // 2) as half:
                        c0 = 2 * half
                        ch = Chain(dve, s_dve, half, 6)
                        for p in range(2):
                            c = c0 + p
                            ch.link(dve.tensor_copy(wc[p][:, :, :], wsel[:, :, bass.ds(c * TC, TC)]))
                            dve.wait_ge(s_acc[p], 8 * c0 + 16)
                            dve.wait_ge(s_gath[p], (8 * c0 + 16) * TOPK * TC)
                            for j in range(TOPK):
                                for i in range(TC):
                                    last = dve.scalar_tensor_tensor(
                                        acc[p][:, i, :], gath[p][:, j, i, :], wc[p][:, j, i:i + 1],
                                        acc[p][:, i, :], ALU.mult, ALU.add)
                                if j < TOPK - 1:
                                    ch.link(last)
                            last.then_inc(s_sum, 1)
                        ch.close()

        phase_norm()
        end_phase()
        phase_experts("m1", x.rearrange("a t d -> (a t) d"))
        end_phase()
        phase_attention()
        end_phase()
        phase_experts("m2", x2_dram)
        end_phase()
        phase_out()


def kernel(**inputs):
    import numpy as _np
    import concourse.bacc as _bacc
    from concourse import mybir as _mybir
    from concourse.bass_utils import run_bass_kernel_spmd as _run

    a = {k.replace("L0_attn_", "").replace("L0_ffn_", "f_"): _np.asarray(v) for k, v in inputs.items()}
    w_v = a["W_v"]
    lay = {
        "x": a["x"], "mu_x": a["mu_x"], "W_x1": a["W_x1"],
        "W_x2": a["W_x2"].transpose(1, 2, 0).reshape(5 * LR, D),
        "x_biasT": a["x_bias"].T, "W_r": a["W_r"], "W_w1": a["W_w1"], "W_w2": a["W_w2"], "b_w2": a["b_w2"],
        "W_k": a["W_k"], "W_v": w_v,
        "W_v_vh": w_v.reshape(D, H, DV).transpose(0, 2, 1).reshape(D, D),
        "W_g": a["W_g"], "u": a["u"], "gn_w": a["gn_w"], "gn_b": a["gn_b"], "W_o": a["W_o"],
        "gate_wT": a["f_gate_w"].T, "fc1_wT": a["f_fc1_w"].transpose(0, 2, 1), "fc1_b": a["f_fc1_b"],
        "geglu_mult": a["f_geglu_mult"], "fc2_wT": a["f_fc2_w"].transpose(0, 2, 1), "fc2_b": a["f_fc2_b"],
        "s_fc1_wT": a["f_s_fc1_w"].T, "s_fc1_b": a["f_s_fc1_b"], "s_geglu_mult": a["f_s_geglu_mult"],
        "s_fc2_wT": a["f_s_fc2_w"].T, "s_fc2_b": a["f_s_fc2_b"],
    }
    nc = _bacc.Bacc("TRN2", target_bir_lowering=False, num_devices=1)
    arrays, args = {}, []
    for name, v in lay.items():
        v = _np.ascontiguousarray(v)
        arrays[f"in_{name}"] = v
        args.append(nc.dram_tensor(f"in_{name}", v.shape, _mybir.dt.from_np(v.dtype), kind="ExternalInput").ap())
    res = nc.dram_tensor("out_x", (1, T, D), _mybir.dt.float32, kind="ExternalOutput").ap()
    macaron_kernel(nc, *args, res)
    r = _run(nc, [arrays], core_ids=[0])
    return r.results[0]["out_x"]
```

```python
import concourse.bass as bass
from concourse import mybir
from contextlib import ExitStack, contextmanager

FP32 = mybir.dt.float32
BF16 = mybir.dt.bfloat16
I32 = mybir.dt.int32
U32 = mybir.dt.uint32
ALU = mybir.AluOpType
ACT = mybir.ActivationFunctionType
AX = mybir.AxisListType.X

P = 128
T = 4096
D = 256
KD = D // P
E = 15
TOPK = 3
F = 256
KF = F // P
FS = 512
KFS = FS // P
H = 16
DK = 8
DV = 16
LR = 32
GL = 64
EPS = 1e-5
NT = T // P
C = 512
NC = T // C
TC = C // P
NB = T * TOPK // P + E
NB += -NB % 4
IDX = D
SHARE = D + 1
ROW = D + 1 + E
NBIAS = E * 2 * F + E * D + D
B1, B2, BS2 = 0, E * 2 * F, E * 2 * F + E * D
MIX_R, MIX_W, MIX_K, MIX_V, MIX_G = range(5)


class Chain:

    def __init__(self, eng, sem):
        self.eng, self.sem, self.base, self.n = eng, sem, 0, 0

    def link(self, ins):
        self.n += 1
        ins.then_inc(self.sem, 1)
        self.eng.wait_ge(self.sem, self.base + self.n)

    @contextmanager
    def turns(self, i, count, per_turn):
        before = self.base + self.n
        self.base, self.n = before + i * per_turn, 0
        yield
        assert self.n == per_turn, (self.n, per_turn)
        self.base, self.n = before + count * per_turn, 0


def after(eng, sem, value):
    if not isinstance(value, int) or value > 0:
        eng.wait_ge(sem, value)


def bcast(ap, axis, n):
    ap = ap.unsqueeze(axis)
    shape = list(ap.shape)
    shape[axis] = n
    return ap.to_broadcast(shape)


def macaron_kernel(nc, x, mu_x, W_x1, W_x2, x_biasT, W_r, W_w1, W_w2, b_w2, W_k, W_v, W_v_vh, W_g, u, gn_w, gn_b,
                   W_o, gate_wT, fc1_wT, fc1_b, geglu_mult, fc2_wT, fc2_b, s_fc1_wT, s_fc1_b, s_geglu_mult,
                   s_fc2_wT, s_fc2_b, out):
    ctx = ExitStack()
    in_use = []
    with ctx:
        def dram(name, shape, dt):
            return nc.dram_tensor(name, shape, dt, kind="Internal").ap()

        def sb(name, shape, dt=FP32, scope=ctx):
            return scope.enter_context(nc.sbuf_tensor(name, shape, dt))

        def ps(name, shape, dt=FP32, scope=ctx):
            return scope.enter_context(nc.psum_tensor(name, shape, dt))

        def sem(name):
            in_use.append(nc.alloc_semaphore(name=name))
            return in_use[-1]

        def end_phase():
            nc.clear_and_free_semaphores(in_use)
            nc.all_engine_barrier()
            in_use.clear()

        xn_dram = dram("xn_scratch", (T, D), FP32)
        xnT_dram = dram("xnT_scratch", (D, T), FP32)
        x1_dram = dram("x1_scratch", (T, D), FP32)
        x2_dram = dram("x2_scratch", (T, D), FP32)
        bias_dram = dram("bias_scratch", (3, NBIAS), BF16)
        rows_dram = dram("rows_scratch", (NB * P, ROW), FP32)
        sums_dram = [dram(f"sum{q}_scratch", (T + P, D), FP32) for q in range(2)]

        ident = sb("ident", [P, P])
        eps = sb("eps", [P, 1])
        pad = sb("pad", [P, 2])
        ones3 = sb("ones3", [P, P], BF16)
        tri = sb("tri", [P, P], BF16)
        ones = sb("ones", [P, P], BF16)
        gate = sb("gate", [P, KD, E])
        logits = sb("logits", [P, NT, E])
        bias = sb("bias", [P, NBIAS], BF16)
        zero = sb("zero", [P, D])
        fill = sb("fill", [P, ROW])
        s_fill = nc.alloc_semaphore(name="fill")
        block_expert = sb("block_expert", [1, NB], I32)

        def phase_norm():
            s_ident, s_cst, s_zero, s_gate, s_braw, s_bpart, s_bout, s_bin, s_sums = (
                sem(f"a_{n}") for n in ("ident", "cst", "zero", "gate", "braw", "bpart", "bout", "bin", "sums"))
            s_xin = [sem(f"a_xin{p}") for p in range(2)]
            s_xnout = [sem(f"a_xnout{p}") for p in range(2)]
            s_xTout = [sem(f"a_xTout{p}") for p in range(2)]
            s_stats, s_std, s_norm, s_tr, s_xT, s_lg, s_lgsb = (
                sem(f"a_{n}") for n in ("stats", "std", "norm", "tr", "xT", "lg", "lgsb"))
            s_dve = sem("a_dve")
            with ExitStack() as sc:
                braw = sb("a_braw", [P, NBIAS // P], scope=sc)
                bpart = sb("a_bpart", [P, 3, NBIAS // P], BF16, scope=sc)
                xin = [sb(f"a_x{p}", [P, TC, D], scope=sc) for p in range(2)]
                xn = [sb(f"a_xn{p}", [P, TC, D], scope=sc) for p in range(2)]
                xT = [sb(f"a_xT{p}", [P, KD, C], scope=sc) for p in range(2)]
                st = [sb(f"a_st{p}", [P, TC, 6], scope=sc) for p in range(2)]
                mv = [sb(f"a_mv{p}", [P, TC, 2], scope=sc) for p in range(2)]
                sd = [sb(f"a_sd{p}", [P, TC], scope=sc) for p in range(2)]
                rs = [sb(f"a_rs{p}", [P, TC], scope=sc) for p in range(2)]
                psT = [ps(f"a_psT{p}", [P, KD, C], scope=sc) for p in range(2)]
                psL = [ps(f"a_psL{p}", [P, TC, P], scope=sc) for p in range(2)]
                x_v = x.rearrange("a (i p) d -> p (a i) d", p=P)
                xn_v = xn_dram.rearrange("(i p) d -> p i d", p=P)
                xnT_v = xnT_dram.rearrange("(k p) t -> p k t", p=P)
                flat = [(fc1_b.rearrange("e f -> (e f)"), B1, B2), (fc2_b.rearrange("e d -> (e d)"), B2, BS2),
                        (s_fc2_b, BS2, NBIAS)]
                block = sc.enter_context(nc.Block())

                @block.sync
                def _(sp):
                    for src, lo, hi in flat:
                        sp.dma_start(braw[:, lo // P:hi // P], src.rearrange("(p n) -> p n", p=P)).then_inc(s_braw, 16)
                    sp.dma_start(gate[:, :, :], gate_wT.rearrange("(k p) e -> p k e", p=P)).then_inc(s_gate, 16)

                    def turn(h, p):
                        c = 2 * h + p
                        after(sp, s_norm, c - 1)
                        sp.dma_start(xin[p][:, :, :], x_v[:, bass.ds(c * TC, TC), :]).then_inc(s_xin[p], 16)
                    for p in range(2):
                        turn(0, p)
                    with sp.Fori(1, NC // 2) as h:
                        for p in range(2):
                            turn(h, p)
                    sp.wait_ge(s_bpart, 3)
                    for n in range(3):
                        for src, lo, hi in flat:
                            sp.dma_start(bias_dram[n, lo:hi].rearrange("(p n) -> p n", p=P),
                                         bpart[:, n, lo // P:hi // P]).then_inc(s_bout, 16)
                    sp.wait_ge(s_bout, 9 * 16)
                    sp.wait_ge(s_zero, 3)
                    for n, r in enumerate((0, 32, 64)):
                        sp.dma_start(bias[r:r + 1, :], bias_dram[n:n + 1, :]).then_inc(s_bin, 16)
                    sp.wait_ge(s_bin, 3 * 16)

                @block.gpsimd
                def _(pool):
                    pool.memset(ident[:, :], 0.0).then_inc(s_ident, 1)
                    pool.wait_ge(s_ident, 1)
                    pool.affine_select(out=ident[:, :], in_=ident[:, :], compare_op=ALU.not_equal, fill=1.0,
                                       base=0, pattern=[[-1, P]], channel_multiplier=1).then_inc(s_ident, 1)
                    pool.memset(eps[:, :], EPS).then_inc(s_cst, 1)
                    pool.memset(zero[:, :], 0.0).then_inc(s_zero, 1)
                    pool.memset(fill[:, :], 0.0).then_inc(s_zero, 1)
                    pool.wait_ge(s_zero, 2)
                    pool.iota(fill[:, IDX:IDX + 1], pattern=[[0, 1]], base=T, channel_multiplier=1,
                              allow_small_or_imprecise_dtypes=True).then_inc(s_cst, 1)
                    pool.memset(bias[:, :].bitcast(U32), 0).then_inc(s_zero, 1)
                    pool.memset(ones[:, :], 1.0).then_inc(s_cst, 1)
                    pool.memset(ones3[:, :], 0.0).then_inc(s_cst, 1)
                    pool.wait_ge(s_cst, 4)
                    pool.affine_select(out=tri[:, :], in_=ones[:, :], compare_op=ALU.is_gt, fill=0.0,
                                       base=0, pattern=[[1, P]], channel_multiplier=-1).then_inc(s_cst, 1)
                    for n, r in enumerate((0, 32, 64)):
                        pool.wait_ge(s_cst, 5 + n)
                        pool.memset(ones3[r:r + 1, :], 1.0).then_inc(s_cst, 1)

                @block.vector
                def _(dve):
                    ch = Chain(dve, s_dve)

                    def turn(h, p):
                        c = 2 * h + p
                        dve.wait_ge(s_xin[p], 16 * h + 16)
                        for j in range(TC):
                            last = dve.bn_stats(st[p][:, j, :], xin[p][:, j, :])
                        ch.link(last)
                        dve.memset(pad[:, 0:1], 0.0)
                        for j in range(TC):
                            last = dve.bn_aggr(mv[p][:, j, :], st[p][:, j, :])
                        last.then_inc(s_stats, 1)
                        dve.wait_ge(s_std, c + 1)
                        ch.link(dve.reciprocal(rs[p][:, :], sd[p][:, :]))
                        after(dve, s_xnout[p], 16 * h)
                        after(dve, s_tr, c - 1)
                        for j in range(TC):
                            last = dve.tensor_scalar(xn[p][:, j, :], xin[p][:, j, :], mv[p][:, j, 0:1],
                                                     rs[p][:, j:j + 1], ALU.subtract, ALU.mult)
                        last.then_inc(s_norm, 1)
                        dve.wait_ge(s_lg, c + 1)
                        ch.link(dve.tensor_copy(logits[:, bass.ds(c * TC, TC), :], psL[p][:, :, 0:E]))
                    dve.wait_ge(s_braw, 3 * 16)
                    for n in range(3):
                        if n:
                            ch.link(dve.tensor_tensor(braw[:, :], braw[:, :], bpart[:, n - 1, :], ALU.subtract))
                        dve.tensor_copy(bpart[:, n, :], braw[:, :]).then_inc(s_bpart, 1)
                        dve.wait_ge(s_bpart, n + 1)
                    for p in range(2):
                        turn(0, p)
                    with dve.Fori(1, NC // 2) as h, ch.turns(h - 1, NC // 2 - 1, 2 * 3):
                        for p in range(2):
                            turn(h, p)

                @block.scalar
                def _(act):
                    act.wait_ge(s_cst, 2)
                    rows_v = rows_dram.rearrange("(n p) d -> p n d", p=P)
                    for n in range(4):
                        act.dma_start(rows_v[:, n * NB // 4:(n + 1) * NB // 4, :],
                                      bcast(fill[:, :], 1, NB // 4)).then_inc(s_fill, 16)
                    sums_v = [q.rearrange("(n p) d -> p n d", p=P) for q in sums_dram]
                    act.dma_start(sums_v[1], bcast(zero[:, :], 1, NT + 1)).then_inc(s_sums, 16)
                    act.dma_start(sums_v[0][:, NT:, :], bcast(zero[:, :], 1, 1)).then_inc(s_sums, 16)

                    def turn(h, p):
                        c = 2 * h + p
                        act.wait_ge(s_stats, c + 1)
                        act.activation(sd[p][:, :], mv[p][:, :, 1], ACT.Sqrt, bias=eps[:, 0:1]).then_inc(s_std, 1)
                        act.wait_ge(s_norm, c + 1)
                        act.dma_start(xn_v[:, bass.ds(c * TC, TC), :], xn[p][:, :, :]).then_inc(s_xnout[p], 16)
                        act.wait_ge(s_tr, c + 1)
                        after(act, s_xTout[p], 16 * h)
                        act.activation(xT[p][:, :, :], psT[p][:, :, :], ACT.Copy).then_inc(s_xT, 1)
                        act.wait_ge(s_xT, c + 1)
                        act.dma_start(xnT_v[:, :, bass.ds(c * C, C)], xT[p][:, :, :]).then_inc(s_xTout[p], 16)
                    for p in range(2):
                        turn(0, p)
                    with act.Fori(1, NC // 2) as h:
                        for p in range(2):
                            turn(h, p)
                    for p in range(2):
                        act.wait_ge(s_xnout[p], 16 * (NC // 2))
                        act.wait_ge(s_xTout[p], 16 * (NC // 2))
                    act.wait_ge(s_sums, 32)

                @block.tensor
                def _(pe):
                    pe.wait_ge(s_ident, 2)
                    pe.wait_ge(s_gate, 16)

                    def turn(h, p):
                        c = 2 * h + p
                        pe.wait_ge(s_norm, c + 1)
                        for k in range(KD):
                            for j in range(TC):
                                last = pe.transpose(psT[p][:, k, j * P:(j + 1) * P],
                                                    xn[p][:, j, k * P:(k + 1) * P], ident[:, :])
                        last.then_inc(s_tr, 1)
                        pe.wait_ge(s_xT, c + 1)
                        for j in range(TC):
                            for k in range(KD):
                                last = pe.matmul(psL[p][:, j, 0:E], xT[p][:, k, j * P:(j + 1) * P],
                                                 gate[:, k, :], start=k == 0, stop=k == KD - 1)
                        last.then_inc(s_lg, 1)
                    for p in range(2):
                        turn(0, p)
                    with pe.Fori(1, NC // 2) as h:
                        for p in range(2):
                            turn(h, p)

        def phase_experts(tag, x_src):
            with ExitStack() as we:
                w1 = sb(f"{tag}_w1", [P, E * KD * 2 * F], scope=we)
                w2 = sb(f"{tag}_w2", [P, E * KF * D], scope=we)
                route(tag, x_src, w1, w2)
                experts(tag, w1, w2)

        def route(tag, x_src, w1, w2):
            def s(n):
                return sem(f"{tag}r_{n}")
            s_w, s_gm, s_ws, s_xn, s_iota, s_idx, s_fold, s_wfold = (
                s(n) for n in ("w", "gm", "ws", "xn", "iota", "idx", "fold", "wfold"))
            s_xT = [s(f"xT{p}") for p in range(2)]
            s_xr = [s(f"xr{p}") for p in range(2)]
            s_out = [s(f"out{p}") for p in range(2)]
            s_dve, s_hot, s_rank, s_exp, s_soft, s_pos, s_scat = (
                s(n) for n in ("dve", "hot", "rank", "exp", "soft", "pos", "scat"))
            s_h, s_ge, s_a, s_y, s_acc, s_zeroed = (s(n) for n in ("h", "ge", "a", "y", "acc", "zeroed"))
            with ExitStack() as sc:
                def small(n, shape, dt=FP32):
                    return sb(f"{tag}_{n}", shape, dt, scope=sc)
                ws1 = small("ws1", [P, KD, 2 * FS])
                ws2 = small("ws2", [P, KFS, D])
                gms = small("gms", [P, KFS])
                gm = small("gm", [P, E * KF])
                bs1 = small("bs1", [P, 2 * KFS])
                rows = small("rows", [P, NT, ROW])
                xT = [small(f"xT{p}", [P, KD, C]) for p in range(2)]
                xr = [small(f"xr{p}", [P, TC, D]) for p in range(2)]
                ge = small("ge", [P, 2, C])
                aT = small("aT", [P, KFS, C])
                ph = [ps(f"{tag}_ph{q}", [P, 2, C], scope=sc) for q in range(2)]
                py = ps(f"{tag}_py", [P, TC, D], scope=sc)
                prank = ps(f"{tag}_prank", [P, NT * E], scope=sc)
                ptot = ps(f"{tag}_ptot", [P, NT * E], scope=sc)
                top = small("top", [P, NT, 8])
                topi = small("topi", [P, NT, 8], U32)
                chosen = small("chosen", [P, TOPK, NT])
                iota_e = small("iota_e", [P, E])
                iota_b = small("iota_b", [1, NB])
                flat_a = aT[:, :, :].rearrange("p k c -> p (k c)")
                hot = flat_a[:, 0:TOPK * NT * E].rearrange("p (j i e) -> p j i e", j=TOPK, i=NT)
                past = flat_a[0:1, 0:NB * E].rearrange("p (b e) -> p b e", e=E)
                many = small("many", [P, NT, E], BF16)
                tmp = small("tmp", [P, NT, E])
                tot = small("tot", [P, E, NT])
                inc = small("inc", [P, E, NT])
                keep = small("keep", [P, E, NT])
                nblk = small("nblk", [P, E])
                nblk_i = small("nblk_i", [P, E], I32)
                endb = small("endb", [P, E])
                off = small("off", [P, E])
                one_e = small("one_e", [P, E])
                pastn = small("pastn", [1, NB])
                soft = small("soft", [P, NT])
                etop = small("etop", [P, TOPK, NT])
                posf = small("posf", [P, TOPK, NT])
                pos = small("pos", [P, TOPK, NT], I32)

                x_v = x_src.rearrange("(i p) d -> p i d", p=P)
                xn_v = xn_dram.rearrange("(i p) d -> p i d", p=P)
                xnT_v = xnT_dram.rearrange("(k p) t -> p k t", p=P)
                sum_v = sums_dram[0].rearrange("(i p) d -> p i d", p=P)
                w2_e = w2[:, :].rearrange("p (e k d) -> p e k d", e=E, k=KF)
                w1_e = w1[:, :].rearrange("p (e k f) -> p e k f", e=E, k=KD)
                block = sc.enter_context(nc.Block())

                @block.sync
                def _(sp):
                    def load(h, p):
                        c = 2 * h + p
                        after(sp, s_h, (c - 1) * KFS)
                        sp.dma_start(xT[p][:, :, :], xnT_v[:, :, bass.ds(c * C, C)]).then_inc(s_xT[p], 16)
                        after(sp, s_out[p], 16 * h)
                        sp.dma_start(xr[p][:, :, :], x_v[:, bass.ds(c * TC, TC), :]).then_inc(s_xr[p], 16)
                    sp.dma_start(ws1[:, :, :], s_fc1_wT.rearrange("(k p) f -> p k f", p=P)).then_inc(s_ws, 16)
                    with nc.allow_non_contiguous_dma(reason="small per-channel vectors"):
                        sp.dma_start(gms[:, :], s_geglu_mult.rearrange("(k p) -> p k", p=P)).then_inc(s_ws, 16)
                        sp.dma_start(bs1[:, :], s_fc1_b.rearrange("(k p) -> p k", p=P)).then_inc(s_ws, 16)
                        sp.dma_start(gm[:, :], geglu_mult.rearrange("e (k p) -> p (e k)", p=P)).then_inc(s_gm, 16)
                    load(0, 0)
                    sp.dma_start(ws2[:, :, :], s_fc2_wT.rearrange("(k p) d -> p k d", p=P)).then_inc(s_ws, 16)
                    load(0, 1)
                    for n in range(2):
                        sp.dma_start(rows[:, n * NT // 2:(n + 1) * NT // 2, 0:D],
                                     xn_v[:, n * NT // 2:(n + 1) * NT // 2, :]).then_inc(s_xn, 16)
                    for e in range(E):
                        sp.dma_start(w2_e[:, e], fc2_wT[e].rearrange("(k p) d -> p k d", p=P)).then_inc(s_w, 16)
                        sp.dma_start(w1_e[:, e], fc1_wT[e].rearrange("(k p) f -> p k f", p=P)).then_inc(s_w, 16)
                    with sp.Fori(1, NC // 2) as h:
                        for p in range(2):
                            load(h, p)
                    sp.wait_ge(s_w, 32 * E)

                @block.gpsimd
                def _(pool):
                    pool.iota(iota_e[:, :], pattern=[[1, E]], base=0, channel_multiplier=0,
                              allow_small_or_imprecise_dtypes=True).then_inc(s_iota, 1)
                    pool.iota(iota_b[:, :], pattern=[[1, NB]], base=0, channel_multiplier=0,
                              allow_small_or_imprecise_dtypes=True).then_inc(s_iota, 1)
                    pool.iota(rows[:, :, IDX:IDX + 1], pattern=[[P, NT]], base=0, channel_multiplier=1,
                              allow_small_or_imprecise_dtypes=True).then_inc(s_idx, 1)
                    pool.wait_ge(s_xn, 32)
                    pool.wait_ge(s_idx, 1)
                    pool.wait_ge(s_fill, 64 if tag == "m1" else 80)
                    pool.wait_ge(s_pos, 2)
                    for i in range(NT):
                        for j in range(TOPK):
                            pool.indirect_dma_start(
                                out=rows_dram[:, :], out_offset=bass.IndirectOffsetOnAxis(ap=pos[:, j, i:i + 1], axis=0),
                                in_=rows[:, i, :], in_offset=None).then_inc(s_scat, 16)
                    pool.wait_ge(s_gm, 16)
                    pool.wait_ge(s_w, 32 * E)
                    for n in range(E * KF):
                        last = pool.tensor_scalar(w2[:, n * D:(n + 1) * D], w2[:, n * D:(n + 1) * D], gm[:, n:n + 1],
                                                  None, ALU.mult)
                    last.then_inc(s_wfold, 1)
                    pool.wait_ge(s_scat, 16 * NT * TOPK)

                @block.vector
                def _(dve):
                    ch = Chain(dve, s_dve)

                    for i in range(NT):
                        last = dve.max(top[:, i, :], logits[:, i, :])
                    ch.link(last)
                    for i in range(NT):
                        last = dve.max_index(topi[:, i, :], top[:, i, :], logits[:, i, :])
                    ch.link(last)
                    ch.link(dve.tensor_copy(chosen[:, :, :].rearrange("p j i -> p i j"), topi[:, :, 0:TOPK]))
                    dve.wait_ge(s_iota, 2)
                    for j in range(TOPK):
                        last = dve.tensor_tensor(hot[:, j, :, :], bcast(iota_e[:, :], 1, NT),
                                                 bcast(chosen[:, j, :], 2, E), ALU.is_equal)
                    ch.link(last)
                    ch.link(dve.tensor_tensor(tmp[:, :, :], hot[:, 0, :, :], hot[:, 1, :, :], ALU.add))
                    dve.tensor_tensor(many[:, :, :], tmp[:, :, :], hot[:, 2, :, :], ALU.add).then_inc(s_hot, 1)
                    ch.link(dve.memset(keep[:, :, :], 1.0))
                    ch.link(dve.memset(keep[:, :, 0:1], 0.0))
                    ch.link(dve.memset(one_e[:, :], 1.0))
                    dve.tensor_tensor(etop[:, :, :], top[:, :, 0:TOPK].rearrange("p i j -> p j i"),
                                      bcast(top[:, :, 0], 1, TOPK), ALU.subtract)
                    dve.wait_ge(s_hot, 1)
                    dve.tensor_tensor(tmp[:, :, :], logits[:, :, :], bcast(top[:, :, 0], 2, E),
                                      ALU.subtract).then_inc(s_soft, 1)
                    dve.wait_ge(s_ws, 64)
                    for k in range(KFS):
                        last = dve.tensor_scalar(ws2[:, k, :], ws2[:, k, :], gms[:, k:k + 1], None, ALU.mult)
                    last.then_inc(s_fold, 1)
                    dve.wait_ge(s_rank, 1)
                    ch.link(dve.tensor_copy(tot[:, :, :], ptot[:, :].rearrange("p (i e) -> p e i", e=E)))
                    ch.link(dve.tensor_tensor_scan(inc[:, :, :].rearrange("p e i -> p (e i)"),
                                                   keep[:, :, :].rearrange("p e i -> p (e i)"),
                                                   tot[:, :, :].rearrange("p e i -> p (e i)"), 0.0, ALU.mult, ALU.add))
                    ch.link(dve.tensor_scalar(nblk_i[:, :], inc[:, :, NT - 1], float(P - 1), None, ALU.add))
                    ch.link(dve.tensor_scalar(nblk_i[:, :], nblk_i[:, :], 7, None, ALU.arith_shift_right))
                    ch.link(dve.tensor_copy(nblk[:, :], nblk_i[:, :]))
                    ch.link(dve.tensor_tensor_scan(endb[:, :], one_e[:, :], nblk[:, :], 0.0, ALU.mult, ALU.add))
                    ch.link(dve.tensor_tensor(off[:, :], endb[:, :], nblk[:, :], ALU.subtract))
                    ch.link(dve.tensor_scalar(off[:, :], off[:, :], float(P), None, ALU.mult))
                    ch.link(dve.tensor_tensor(inc[:, :, :], inc[:, :, :], tot[:, :, :], ALU.subtract))
                    ch.link(dve.tensor_tensor(inc[:, :, :], inc[:, :, :], bcast(off[:, :], 2, NT), ALU.add))
                    ch.link(dve.tensor_tensor(tot[:, :, :], prank[:, :].rearrange("p (i e) -> p e i", e=E),
                                              inc[:, :, :], ALU.add))
                    for j in range(TOPK):
                        ch.link(dve.tensor_tensor(inc[:, :, :], hot[:, j, :, :].rearrange("p i e -> p e i"),
                                                  tot[:, :, :], ALU.mult))
                        ch.link(dve.tensor_reduce(posf[:, j, :], inc[:, :, :].rearrange("p e i -> p i e"), AX, ALU.add))
                    dve.tensor_copy(pos[:, :, :], posf[:, :, :]).then_inc(s_pos, 1)
                    dve.wait_ge(s_exp, 2)
                    ch.link(dve.tensor_reduce(soft[:, :], tmp[:, :, :], AX, ALU.add))
                    ch.link(dve.reciprocal(soft[:, :], soft[:, :]))
                    ch.link(dve.tensor_tensor(etop[:, :, :], etop[:, :, :], bcast(soft[:, :], 1, TOPK), ALU.mult))
                    ch.link(dve.tensor_reduce(soft[:, :], etop[:, :, :].rearrange("p j i -> p i j"), AX, ALU.add))
                    ch.link(dve.tensor_scalar(soft[:, :], soft[:, :], 1e-20, None, ALU.add))
                    ch.link(dve.reciprocal(soft[:, :], soft[:, :]))
                    ch.link(dve.tensor_scalar(soft[:, :], soft[:, :], 0.5, None, ALU.mult))
                    ch.link(dve.tensor_tensor(etop[:, :, :], etop[:, :, :], bcast(soft[:, :], 1, TOPK), ALU.mult))
                    for j in range(TOPK):
                        last = dve.tensor_tensor(hot[:, j, :, :], hot[:, j, :, :], bcast(etop[:, j, :], 2, E), ALU.mult)
                    ch.link(last)
                    ch.link(dve.tensor_tensor(tmp[:, :, :], hot[:, 0, :, :], hot[:, 1, :, :], ALU.add))
                    dve.tensor_tensor(rows[:, :, SHARE:ROW], tmp[:, :, :], hot[:, 2, :, :], ALU.add).then_inc(s_pos, 1)
                    dve.wait_ge(s_pos, 2)
                    ch.link(dve.tensor_tensor(past, bcast(iota_b[:, :], 2, E), bcast(endb[0:1, :], 1, NB), ALU.is_ge))
                    ch.link(dve.tensor_reduce(pastn[:, :], past, AX, ALU.add))
                    ch.link(dve.tensor_scalar(block_expert[:, :], pastn[:, :], float(E - 1), None, ALU.min))

                    def turn(h, p):
                        c = 2 * h + p
                        after(dve, s_y, c)
                        for f in range(KFS):
                            dve.wait_ge(s_ge, c * KFS + f + 1)
                            dve.scalar_tensor_tensor(
                                aT[:, f, :], ph[f % 2][:, 0, :], bs1[:, f:f + 1], ge[:, f % 2, :],
                                ALU.add, ALU.mult).then_inc(s_a, 1)
                        dve.wait_ge(s_y, c + 1)
                        dve.wait_ge(s_xr[p], 16 * h + 16)
                        dve.scalar_tensor_tensor(xr[p][:, :, :], py[:, :, :], 0.5, xr[p][:, :, :],
                                                 ALU.mult, ALU.add).then_inc(s_acc, 1)
                    for p in range(2):
                        turn(0, p)
                    with dve.Fori(1, NC // 2) as h:
                        for p in range(2):
                            turn(h, p)

                @block.scalar
                def _(act):
                    if tag == "m2":
                        act.dma_start(sums_dram[1].rearrange("(n p) d -> p n d", p=P),
                                      bcast(zero[:, :], 1, NT + 1)).then_inc(s_zeroed, 16)
                    act.wait_ge(s_soft, 1)
                    act.activation(tmp[:, :, :], tmp[:, :, :], ACT.Exp).then_inc(s_exp, 1)
                    act.activation(etop[:, :, :], etop[:, :, :], ACT.Exp).then_inc(s_exp, 1)
                    act.wait_ge(s_ws, 64)

                    def store(h, p):
                        c = 2 * h + p
                        act.wait_ge(s_acc, c + 1)
                        act.dma_start(sum_v[:, bass.ds(c * TC, TC), :], xr[p][:, :, :]).then_inc(s_out[p], 16)

                    def turn(h, p):
                        c = 2 * h + p
                        for f in range(KFS):
                            act.wait_ge(s_h, c * KFS + f + 1)
                            after(act, s_a, c * KFS + f - 1)
                            act.activation(ge[:, f % 2, :], ph[f % 2][:, 1, :], ACT.Gelu,
                                           bias=bs1[:, KFS + f:KFS + f + 1]).then_inc(s_ge, 1)
                        if p:
                            store(h, 0)
                        elif not isinstance(h, int) or h:
                            store(h - 1, 1)
                    for p in range(2):
                        turn(0, p)
                    with act.Fori(1, NC // 2) as h:
                        for p in range(2):
                            turn(h, p)
                    store(NC // 2 - 1, 1)
                    for p in range(2):
                        act.wait_ge(s_out[p], 8 * NC)
                    if tag == "m2":
                        act.wait_ge(s_zeroed, 16)

                @block.tensor
                def _(pe):
                    def ranks():
                        pe.wait_ge(s_hot, 1)
                        pe.matmul(prank[:, :], tri[:, :], many[:, :, :].rearrange("p i e -> p (i e)"), start=True,
                                  stop=True)
                        pe.matmul(ptot[:, :], ones[:, :], many[:, :, :].rearrange("p i e -> p (i e)"), start=True,
                                  stop=True).then_inc(s_rank, 1)

                    def turn(h, p):
                        c = 2 * h + p
                        pe.wait_ge(s_xT[p], 16 * h + 16)
                        for f in range(KFS):
                            after(pe, s_a, c * KFS + f - 1)
                            for side in range(2):
                                for k in range(KD):
                                    last = pe.matmul(ph[f % 2][:, side, :],
                                                     ws1[:, k, side * FS + f * P:side * FS + (f + 1) * P],
                                                     xT[p][:, k, :], start=k == 0, stop=k == KD - 1)
                            last.then_inc(s_h, 1)
                        pe.wait_ge(s_a, (c + 1) * KFS)
                        after(pe, s_acc, c)
                        for j in range(TC):
                            pe.matmul(py[:, j, :], ones3[:, :], bias[:, BS2:NBIAS], start=True, stop=False)
                            for f in range(KFS):
                                last = pe.matmul(py[:, j, :], aT[:, f, j * P:(j + 1) * P], ws2[:, f, :],
                                                 start=False, stop=f == KFS - 1)
                        last.then_inc(s_y, 1)
                    ranks()
                    pe.wait_ge(s_ws, 64)
                    pe.wait_ge(s_fold, 1)
                    for p in range(2):
                        turn(0, p)
                    with pe.Fori(1, NC // 2) as h:
                        for p in range(2):
                            turn(h, p)

        def experts(tag, w1, w2):
            def s(n):
                return sem(f"{tag}e_{n}")
            s_in = [s(f"in{q}") for q in range(4)]
            s_add = [s(f"add{q}") for q in range(2)]
            s_tr, s_xT, s_h, s_ge, s_a, s_atr, s_aT, s_y, s_ysb, s_meta, s_pad = (
                s(n) for n in ("tr", "xT", "h", "ge", "a", "atr", "aT", "y", "ysb", "meta", "pad"))
            with ExitStack() as sc:
                rows = [sb(f"{tag}_erows{q}", [P, ROW], scope=sc) for q in range(4)]
                idx = [sb(f"{tag}_eidx{q}", [P, 1], I32, scope=sc) for q in range(4)]
                share = [sb(f"{tag}_eshare{q}", [P, 1], scope=sc) for q in range(4)]
                y = [sb(f"{tag}_ey{q}", [P, D], scope=sc) for q in range(4)]
                xT = [sb(f"{tag}_exT{p}", [P, KD, P], scope=sc) for p in range(2)]
                ge = [sb(f"{tag}_ege{p}", [P, F], scope=sc) for p in range(2)]
                a = [sb(f"{tag}_ea{p}", [P, F], scope=sc) for p in range(2)]
                aT = [sb(f"{tag}_eaT{p}", [P, KF, P], scope=sc) for p in range(2)]
                pT = [ps(f"{tag}_epT{p}", [P, KD, P], scope=sc) for p in range(2)]
                ph = [ps(f"{tag}_eph{p}", [P, 2 * F], scope=sc) for p in range(2)]
                pA = [ps(f"{tag}_epA{p}", [P, KF, P], scope=sc) for p in range(2)]
                py = [ps(f"{tag}_epy{p}", [P, D], scope=sc) for p in range(2)]
                NQ = NB // 4
                block = sc.enter_context(nc.Block())


                @block.sync
                def _(sp):
                    def load(h, q):
                        b = 4 * h + q
                        after(sp, s_tr, b - 3)
                        after(sp, s_meta, b - 3)
                        sp.dma_start(rows[q][:, :], rows_dram[bass.ds(b * P, P), :]).then_inc(s_in[q], 16)
                    for q in range(4):
                        load(0, q)
                    with sp.Fori(1, NQ) as h:
                        for q in range(4):
                            load(h, q)

                @block.gpsimd
                def _(pool):
                    def add(h, q):
                        b = 4 * h + q
                        pool.wait_ge(s_ysb, b + 1)
                        after(pool, s_add[q % 2], 16 * (2 * h + q // 2))
                        after(pool, s_pad, b)
                        pool.tensor_tensor(pad[:, 1:2], eps[:, :], eps[:, :], ALU.add).then_inc(s_pad, 1)
                        pool.indirect_dma_start(
                            out=sums_dram[q % 2][:, :], out_offset=bass.IndirectOffsetOnAxis(ap=idx[q][:, 0:1], axis=0),
                            in_=y[q][:, :], in_offset=None, compute_op=ALU.add).then_inc(s_add[q % 2], 16)
                    for q in range(4):
                        add(0, q)
                    with pool.Fori(1, NQ) as h:
                        for q in range(4):
                            add(h, q)
                    for p in range(2):
                        pool.wait_ge(s_add[p], 16 * (NB // 2))

                @block.scalar
                def _(act):
                    def copy_x(h, q):
                        b = 4 * h + q
                        act.wait_ge(s_tr, b + 1)
                        after(act, s_h, b - 1)
                        act.activation(xT[q % 2][:, :, :], pT[q % 2][:, :, :], ACT.Copy).then_inc(s_xT, 1)

                    def copy_a(h, q):
                        b = 4 * h + q
                        act.wait_ge(s_atr, b + 1)
                        after(act, s_y, b - 1)
                        act.activation(aT[q % 2][:, :, :], pA[q % 2][:, :, :], ACT.Copy).then_inc(s_aT, 1)

                    def gelu(h, q):
                        b = 4 * h + q
                        act.wait_ge(s_h, b + 1)
                        after(act, s_a, b - 1)
                        act.activation(ge[q % 2][:, :], ph[q % 2][:, F:2 * F], ACT.Gelu).then_inc(s_ge, 1)

                    def turn(h, q, first=False):
                        copy_x(h + (q + 1) // 4, (q + 1) % 4)
                        if not first:
                            copy_a(h + (q - 1) // 4, (q - 1) % 4)
                        gelu(h, q)
                    copy_x(0, 0)
                    for q in range(4):
                        turn(0, q, first=q == 0)
                    with act.Fori(1, NQ - 1) as h:
                        for q in range(4):
                            turn(h, q)
                    for q in range(3):
                        turn(NQ - 1, q)
                    copy_a(NQ - 1, 2)
                    gelu(NQ - 1, 3)
                    copy_a(NQ - 1, 3)

                @block.vector
                def _(dve):
                    def meta(h, q, e):
                        b = 4 * h + q
                        dve.wait_ge(s_in[q], 16 * h + 16)
                        after(dve, s_add[q % 2], 16 * (2 * h + q // 2 - 1))
                        dve.tensor_copy(idx[q][:, :], rows[q][:, IDX:IDX + 1])
                        dve.tensor_copy(share[q][:, :], rows[q][:, bass.ds(e + SHARE, 1)]).then_inc(s_meta, 1)

                    def scale(h, q):
                        b = 4 * h + q
                        dve.wait_ge(s_y, b + 1)
                        dve.wait_ge(s_meta, b + 1)
                        dve.tensor_scalar(y[q][:, :], py[q % 2][:, :], share[q][:, 0:1], None,
                                          ALU.mult).then_inc(s_ysb, 1)

                    def product(h, q):
                        b = 4 * h + q
                        dve.wait_ge(s_ge, b + 1)
                        after(dve, s_atr, b - 1)
                        dve.tensor_tensor(a[q % 2][:, :], ph[q % 2][:, 0:F], ge[q % 2][:, :], ALU.mult).then_inc(s_a, 1)

                    def turns(h, first=False):
                        es = [dve.value_load(block_expert[0:1, bass.ds(4 * h + q, 1)], min_val=0, max_val=E - 1)
                              for q in range(4)]
                        for q in range(4):
                            meta(h, q, es[q])
                            if not first or q >= 2:
                                scale(h + (q - 2) // 4, (q - 2) % 4)
                            product(h, q)
                    turns(0, first=True)
                    with dve.Fori(1, NQ) as h:
                        turns(h)
                    scale(NQ - 1, 2)
                    scale(NQ - 1, 3)

                @block.tensor
                def _(pe):
                    def expert(b):
                        return pe.value_load(block_expert[0:1, bass.ds(b, 1)], min_val=0, max_val=E - 1)

                    def turn_x(h, q):
                        b = 4 * h + q
                        pe.wait_ge(s_in[q], 16 * h + 16)
                        after(pe, s_xT, b - 1)
                        for k in range(KD):
                            last = pe.transpose(pT[q % 2][:, k, :], rows[q][:, k * P:(k + 1) * P], ident[:, :])
                        last.then_inc(s_tr, 1)

                    def fc1(h, q, e):
                        b = 4 * h + q
                        pe.wait_ge(s_xT, b + 1)
                        after(pe, s_a, b - 1)
                        pe.matmul(ph[q % 2][:, :], ones3[:, :], bias[:, bass.ds(e * (2 * F) + B1, 2 * F)],
                                  start=True, stop=False)
                        for k in range(KD):
                            last = pe.matmul(ph[q % 2][:, :], xT[q % 2][:, k, :],
                                             w1[:, bass.ds(e * (KD * 2 * F) + k * 2 * F, 2 * F)],
                                             start=False, stop=k == KD - 1)
                        last.then_inc(s_h, 1)

                    def turn_a(h, q):
                        b = 4 * h + q
                        pe.wait_ge(s_a, b + 1)
                        after(pe, s_aT, b - 1)
                        for k in range(KF):
                            last = pe.transpose(pA[q % 2][:, k, :], a[q % 2][:, k * P:(k + 1) * P], ident[:, :])
                        last.then_inc(s_atr, 1)

                    def fc2(h, q, e):
                        b = 4 * h + q
                        pe.wait_ge(s_aT, b + 1)
                        after(pe, s_ysb, b - 1)
                        pe.matmul(py[q % 2][:, :], ones3[:, :], bias[:, bass.ds(e * D + B2, D)], start=True, stop=False)
                        for k in range(KF):
                            last = pe.matmul(py[q % 2][:, :], aT[q % 2][:, k, :],
                                             w2[:, bass.ds(e * (KF * D) + k * D, D)],
                                             start=False, stop=k == KF - 1)
                        last.then_inc(s_y, 1)

                    def turns(h, first=False, last=False):
                        es = {q: expert(4 * h + q) for q in range(0 if first else -2, 4)}
                        for q in range(4):
                            if not last or q < 3:
                                turn_x(h + (q + 1) // 4, (q + 1) % 4)
                            if not first or q >= 2:
                                fc2(h + (q - 2) // 4, (q - 2) % 4, es[q - 2])
                            if not first or q >= 1:
                                turn_a(h + (q - 1) // 4, (q - 1) % 4)
                            fc1(h, q, es[q])
                        return es
                    turn_x(0, 0)
                    turns(0, first=True)
                    turns(1)
                    with pe.Fori(2, NQ - 1) as h:
                        turns(h)
                    es = turns(NQ - 1, last=True)
                    fc2(NQ - 1, 2, es[2])
                    turn_a(NQ - 1, 3)
                    fc2(NQ - 1, 3, es[3])

        def phase_attention():
            names = ("w", "cst", "xsum", "st", "sd", "rs", "y", "tr", "yc", "yT", "xx", "low", "lowT", "mus", "tm", "xi",
                     "rps", "kps", "vps", "w1p", "w2p", "gps", "rT", "kT", "rk", "cp", "cs", "vT", "bo", "w1T", "ew",
                     "dec", "sg", "spread", "kv", "S", "P", "o", "oadd", "oc", "sq", "gv", "gsd", "gn", "z", "ztr",
                     "zT", "wo", "x2", "st2", "sd2", "rs2", "n2", "ntr", "nT", "lg", "lgs", "dve",
                     "l_sum", "o_x1", "l_x1", "o_x2", "o_xn", "o_xnT")
            S = {n: sem(f"t_{n}") for n in names}
            with ExitStack() as sc:
                def t(n, shape, dt=FP32):
                    return sb(f"t_{n}", shape, dt, scope=sc)
                wx1 = t("wx1", [P, KD, 5 * LR])
                wx2 = t("wx2", [P, D])
                wx2l = t("wx2l", [LR, D])
                xb = t("xb", [P, KD, 5])
                mu = t("mu", [P, KD])
                wr, wk = t("wr", [P, KD, P]), t("wk", [P, KD, P])
                ww1 = t("ww1", [P, KD, GL])
                ww2 = t("ww2", [GL, P])
                bw2 = t("bw2", [P, 1])
                wv, wvT, wg, wo = (t(n, [P, KD, D]) for n in ("wv", "wvT", "wg", "wo"))
                gnw, gnb = t("gnw", [P, D]), t("gnb", [P, D])
                uk = t("uk", [P, 1])
                sel = t("sel", [P, 8, H, DK])
                headsum = t("headsum", [P, H])
                uhead = t("uhead", [P, H])
                parts = [t(f"part{q}", [P, TC, D]) for q in range(2)]
                x1 = t("x1", [P, TC, D])
                st = t("st", [P, TC, 6])
                mv = t("mv", [P, TC, 2])
                sd = t("sd", [P, TC])
                rs = t("rs", [P, TC])
                nb = t("nb", [P, TC])
                y = t("y", [P, TC, D])
                yT = t("yT", [P, KD, C + 1])
                dl = t("dl", [P, KD, C])
                xx = t("xx", [P, KD, C])
                lowT = t("lowT", [P, C])
                lowTl = t("lowTl", [LR, C])
                tm = t("tm", [P, 2, C])
                xi = [t(f"xi{q}", [P, KD, C]) for q in range(2)]
                ew = t("ew", [P, C])
                w1T = t("w1T", [GL, C])
                rk = t("rk", [P, C])
                cs = t("cs", [P, TC * H])
                rT = [t(f"rT{q}", [P, C]) for q in range(2)]
                kT = [t(f"kT{q}", [P, C]) for q in range(2)]
                dec = [t(f"dec{q}", [P, C]) for q in range(2)]
                vT = [t(f"vT{q}", [P, KD, C]) for q in range(2)]
                bo = [t(f"bo{q}", [P, TC, D]) for q in range(2)]
                sg = [t(f"sg{q}", [P, TC, D]) for q in range(2)]
                kv = [t(f"kv{q}", [P, C]) for q in range(2)]
                St = t("S", [P, DV, C + 1])
                Pr = [t(f"P{q}", [P, C]) for q in range(4)]
                o = t("o", [P, TC, D])
                o2 = t("o2", [P, TC, D])
                gs = t("gs", [P, TC * H])
                gv = t("gv", [P, TC * H])
                zT = t("zT", [P, KD, C])
                xr = t("xr", [P, TC, D])
                st2 = t("st2", [P, TC, 6])
                mv2 = t("mv2", [P, TC, 2])
                sd2 = t("sd2", [P, TC])
                rs2 = t("rs2", [P, TC])
                nb2 = t("nb2", [P, TC])
                n2 = t("n2", [P, TC, D])
                psX = ps("t_psX", [P, KD, C], scope=sc)
                psX_tok = psX[:, :, :].rearrange("p a (b d) -> p (a b) d", d=D)
                psO = ps("t_psO", [P, TC, D], scope=sc)
                psM = [ps(f"t_psM{q}", [P, C], scope=sc) for q in range(2)]
                psV = [ps(f"t_psV{q}", [P, C], scope=sc) for q in range(2)]

                def tok(ap):
                    return ap.rearrange("(i p) d -> p i d", p=P)
                sum_v = [tok(q) for q in sums_dram]
                x1_v, x2_v, xn_v = tok(x1_dram), tok(x2_dram), tok(xn_dram)
                xnT_v = xnT_dram.rearrange("(k p) t -> p k t", p=P)
                order = (MIX_R, MIX_K, MIX_V, MIX_W, MIX_G)
                block = sc.enter_context(nc.Block())

                def chunk(c):
                    return bass.ds(c * TC, TC)

                def iterations(eng, body, ch=None, per_turn=0):
                    for it in (-1, 0, 1):
                        body(it, it % 2, True, it >= 0, it >= 1)
                    with eng.Fori(1, NC // 2 - 1) as h, ExitStack() as counted:
                        if ch:
                            counted.enter_context(ch.turns(h - 1, NC // 2 - 2, per_turn))
                        for q in range(2):
                            body(2 * h + q, q, True, True, True)
                    for it in (NC - 2, NC - 1, NC):
                        body(it, it % 2, it < NC - 1, it < NC, True)

                @block.sync
                def _(sp):
                    with nc.allow_non_contiguous_dma(reason="small per-channel vectors"):
                        loads = (
                            (wx1[:, :, :], W_x1.rearrange("(k p) r -> p k r", p=P)),
                            (wx2[:, :], W_x2[0:P, :]), (wx2l[:, :], W_x2[P:P + LR, :]),
                            (xb[:, :, :], x_biasT.rearrange("(k p) i -> p k i", p=P)),
                            (mu[:, :], mu_x.rearrange("(k p) -> p k", p=P)),
                            (wr[:, :, :], W_r.rearrange("(k p) m -> p k m", p=P)),
                            (wk[:, :, :], W_k.rearrange("(k p) m -> p k m", p=P)),
                            (ww1[:, :, :], W_w1.rearrange("(k p) m -> p k m", p=P)),
                            (ww2[:, :], W_w2[:, :]), (bw2[:, :], b_w2.unsqueeze(1)),
                            (wv[:, :, :], W_v.rearrange("(k p) m -> p k m", p=P)),
                            (wvT[:, :, :], W_v_vh.rearrange("(k p) m -> p k m", p=P)),
                            (wg[:, :, :], W_g.rearrange("(k p) m -> p k m", p=P)),
                            (wo[:, :, :], W_o.rearrange("(k p) m -> p k m", p=P)),
                            (gnw[:, :], bcast(gn_w, 0, P)), (gnb[:, :], bcast(gn_b, 0, P)),
                            (uk[:, :], u.rearrange("h k -> (h k)").unsqueeze(1)))
                        for n, (dst, src) in enumerate(loads):
                            if n == 1:
                                for q in range(2):
                                    sp.dma_start(parts[q][:, :, :], sum_v[q][:, chunk(0), :]).then_inc(S["l_sum"], 16)
                            sp.dma_start(dst, src).then_inc(S["w"], 16)
                        assert len(loads) == 17

                    def body(it, par, has_a, has_b, has_c):
                        if has_a:
                            a = it + 1
                            sp.wait_ge(S["xsum"], a + 1)
                            sp.dma_start(x1_v[:, chunk(a), :], x1[:, :, :]).then_inc(S["o_x1"], 16)
                            if not isinstance(it, int) or it < NC - 2:
                                for q in range(2):
                                    sp.dma_start(parts[q][:, :, :], sum_v[q][:, chunk(a + 1), :]).then_inc(S["l_sum"], 16)
                        if has_c:
                            c = it - 1
                            after(sp, S["o_x2"], 16 * c)
                            after(sp, S["rs2"], c)
                            after(sp, S["n2"], c)
                            sp.dma_start(xr[:, :, :], x1_v[:, chunk(c), :]).then_inc(S["l_x1"], 16)
                            sp.wait_ge(S["x2"], c + 1)
                            sp.dma_start(x2_v[:, chunk(c), :], xr[:, :, :]).then_inc(S["o_x2"], 16)
                            sp.wait_ge(S["n2"], c + 1)
                            sp.dma_start(xn_v[:, chunk(c), :], n2[:, :, :]).then_inc(S["o_xn"], 16)
                            sp.wait_ge(S["nT"], c + 1)
                            sp.dma_start(xnT_v[:, :, bass.ds(c * C, C)], zT[:, :, :]).then_inc(S["o_xnT"], 16)
                    iterations(sp, body)
                    sp.wait_ge(S["o_x1"], 16 * NC)
                    for n in ("o_x2", "o_xn", "o_xnT"):
                        sp.wait_ge(S[n], 16 * NC)

                @block.gpsimd
                def _(pool):
                    pool.memset(sel[:, :, :, :], 0.0).then_inc(S["cst"], 1)
                    pool.memset(headsum[:, :], 1.0).then_inc(S["cst"], 1)
                    pool.memset(St[:, :, C:C + 1], 0.0).then_inc(S["cst"], 1)
                    pool.memset(yT[:, :, C:C + 1], 0.0).then_inc(S["cst"], 1)
                    pool.wait_ge(S["cst"], 4)
                    pool.affine_select(out=sel[:, :, :, :], in_=sel[:, :, :, :], compare_op=ALU.not_equal, fill=1.0,
                                       base=0, pattern=[[-16, 8], [-1, H], [0, DK]], channel_multiplier=1
                                       ).then_inc(S["cst"], 1)
                    pool.affine_select(out=headsum[:, :], in_=headsum[:, :], compare_op=ALU.is_ge, fill=0.0,
                                       base=0, pattern=[[-DK, H]], channel_multiplier=1).then_inc(S["cst"], 1)
                    pool.wait_ge(S["cst"], 6)
                    pool.affine_select(out=headsum[:, :], in_=headsum[:, :], compare_op=ALU.is_ge, fill=0.0,
                                       base=DK - 1, pattern=[[DK, H]], channel_multiplier=-1).then_inc(S["cst"], 1)
                    pool.wait_ge(S["cst"], 7)
                    pool.wait_ge(S["w"], 16 * 17)
                    pool.tensor_scalar(uhead[:, :], headsum[:, :], uk[:, 0:1], None, ALU.mult).then_inc(S["cst"], 1)

                    def body(it, par, has_a, has_b, has_c):
                        a, c = it + 1, it - 1
                        pa = 1 - par

                        def x_sum():
                            pool.wait_ge(S["l_sum"], 32 * (a + 1))
                            after(pool, S["y"], a)
                            after(pool, S["o_x1"], 16 * a)
                            pool.tensor_tensor(x1[:, :, :], parts[0][:, :, :], parts[1][:, :, :],
                                               ALU.add).then_inc(S["xsum"], 1)

                        def mixed(n):
                            if n == 0:
                                after(pool, S["gps"], a)
                            if n == 1:
                                after(pool, S["w1p"], a)
                            if n == 2:
                                pool.wait_ge(S["rps"], a + 1)
                            if n == 3:
                                pool.wait_ge(S["kps"], a + 1)
                            if n == 4:
                                pool.wait_ge(S["vps"], 2 * a + 2)
                            for k in range(KD):
                                pool.wait_ge(S["tm"], 10 * a + 2 * n + k + 1)
                                pool.tensor_tensor(xi[n % 2][:, k, :], tm[:, k, :], yT[:, k, 1:C + 1],
                                                   ALU.add).then_inc(S["xi"], 1)

                        def bonus():
                            pool.wait_ge(S["rT"], a + 1)
                            pool.wait_ge(S["kT"], a + 1)
                            after(pool, S["cp"], a)
                            pool.tensor_tensor(rk[:, :], rT[pa][:, :], kT[pa][:, :], ALU.mult).then_inc(S["rk"], 1)

                        def read(v):
                            pool.wait_ge(S["S"], 16 * it + v + 1)
                            after(pool, S["o"], 16 * it + v - 3)
                            pool.tensor_tensor(Pr[v % 4][:, :], St[:, v, 0:C], rT[par][:, :], ALU.mult).then_inc(S["P"], 1)

                        def gated():
                            pool.wait_ge(S["gn"], c + 1)
                            pool.wait_ge(S["sg"], c + 1)
                            after(pool, S["gv"], c + 1)
                            pool.tensor_tensor(o2[:, :, :], o[:, :, :], sg[pa][:, :, :], ALU.mult).then_inc(S["z"], 1)

                        if has_a:
                            x_sum()
                        for v in range(16):
                            if has_a and 7 <= v <= 10:
                                mixed(v - 7)
                            if has_a and v == 10:
                                bonus()
                            if has_a and v == 12:
                                mixed(4)
                            if has_b:
                                read(v)
                            if has_c and v == 8:
                                gated()
                    iterations(pool, body)

                @block.vector
                def _(dve):
                    dve.wait_ge(S["w"], 16 * 17)
                    dve.wait_ge(S["cst"], 8)
                    LINKS = 12
                    ch = Chain(dve, S["dve"])
                    o_h = o[:, :, :].rearrange("p i (h v) -> p (i h) v", v=DV)
                    o2_h = o2[:, :, :].rearrange("p i (h v) -> p (i h) v", v=DV)

                    def stats(src, st, mv, done):
                        for i in range(TC):
                            last = dve.bn_stats(st[:, i, :], src[:, i, :])
                        ch.link(last)
                        dve.memset(pad[:, 0:1], 0.0)
                        for i in range(TC):
                            last = dve.bn_aggr(mv[:, i, :], st[:, i, :])
                        last.then_inc(done, 1)

                    def scales(sd, mv, rs, nb, done):
                        ch.link(dve.reciprocal(rs[:, :], sd[:, :]))
                        dve.scalar_tensor_tensor(nb[:, :], mv[:, :, 0], -1.0, rs[:, :], ALU.mult,
                                                 ALU.mult).then_inc(done, 1)

                    def body(it, par, has_a, has_b, has_c):
                        a, c = it + 1, it - 1
                        pa = 1 - par

                        def shift():
                            dve.wait_ge(S["yT"], a + 1)
                            ch.link(dve.tensor_tensor(dl[:, :, :], yT[:, :, 0:C], yT[:, :, 1:C + 1], ALU.subtract))
                            for k in range(KD):
                                last = dve.scalar_tensor_tensor(xx[:, k, :], dl[:, k, :], mu[:, k:k + 1],
                                                                yT[:, k, 1:C + 1], ALU.mult, ALU.add)
                            last.then_inc(S["xx"], 1)

                        def mix(n):
                            for k in range(KD):
                                dve.wait_ge(S["mus"], 10 * a + 2 * n + k + 1)
                                after(dve, S["xi"], 10 * a + 2 * n + k - 1)
                                dve.scalar_tensor_tensor(tm[:, k, :], psM[k][:, :], xb[:, k, order[n]:order[n] + 1],
                                                         dl[:, k, :], ALU.add, ALU.mult).then_inc(S["tm"], 1)

                        def carry(lo):
                            after(dve, S["P"], 16 * it)
                            ch.link(dve.tensor_copy(St[:, lo:lo + 8, 0:1], St[:, lo:lo + 8, C:C + 1]))

                        def recur(v):
                            dve.wait_ge(S["spread"], 16 * it + v + 1)
                            dve.tensor_tensor(kv[v % 2][:, :], psV[v % 2][:, :], kT[par][:, :],
                                              ALU.mult).then_inc(S["kv"], 1)
                            dve.wait_ge(S["kv"], 16 * it + v + 1)
                            dve.tensor_tensor_scan(St[:, v, 1:C + 1], dec[par][:, :], kv[v % 2][:, :], St[:, v, 0:1],
                                                   ALU.mult, ALU.add).then_inc(S["S"], 1)

                        def collect():
                            dve.wait_ge(S["o"], 16 * (c + 1))
                            after(dve, S["z"], c)
                            dve.tensor_tensor(o[:, :, :], psO[:, :, :], bo[pa][:, :, :], ALU.add).then_inc(S["oadd"], 1)
                            dve.wait_ge(S["oadd"], c + 1)
                            ch.link(dve.tensor_reduce(gs[:, :], o_h, AX, ALU.add))
                            ch.link(dve.tensor_scalar(gs[:, :], gs[:, :], 1.0 / DV, None, ALU.mult))

                        def centre():
                            dve.tensor_tensor(o_h, o_h, bcast(gs[:, :], 2, DV), ALU.subtract).then_inc(S["oc"], 1)

                        def variance():
                            dve.wait_ge(S["sq"], c + 1)
                            dve.tensor_reduce(gv[:, :], o2_h, AX, ALU.add).then_inc(S["gv"], 1)

                        def normalise():
                            dve.wait_ge(S["gsd"], c + 1)
                            ch.link(dve.reciprocal(gs[:, :], gv[:, :]))
                            ch.link(dve.tensor_tensor(o_h, o_h, bcast(gs[:, :], 2, DV), ALU.mult))

                        def affine():
                            ch.link(dve.tensor_tensor(o[:, :, :], o[:, :, :], bcast(gnw[:, :], 1, TC), ALU.mult))
                            dve.tensor_tensor(o[:, :, :], o[:, :, :], bcast(gnb[:, :], 1, TC), ALU.add).then_inc(S["gn"], 1)

                        for v in range(16):
                            if has_b and v in (0, 8):
                                carry(v)
                            if has_c and v == 2:
                                collect()
                            if has_c and v == 3:
                                centre()
                            if has_c and v == 5:
                                variance()
                            if has_c and v == 6:
                                normalise()
                            if has_c and v == 7:
                                affine()
                            if has_b:
                                recur(v)
                            if has_a and v == 1:
                                dve.wait_ge(S["xsum"], a + 1)
                                stats(x1, st, mv, S["st"])
                            if has_a and v == 2:
                                dve.wait_ge(S["sd"], a + 1)
                                scales(sd, mv, rs, nb, S["rs"])
                            if has_a and v == 4:
                                shift()
                            if has_a and 6 <= v <= 10:
                                mix(v - 6)
                            if has_a and v == 10:
                                dve.wait_ge(S["cp"], a + 1)
                                dve.tensor_copy(cs[:, :], psX[:, 0, 0:TC * H]).then_inc(S["cs"], 1)
                            if has_c and v == 11:
                                dve.wait_ge(S["wo"], c + 1)
                                dve.wait_ge(S["l_x1"], 16 * (c + 1))
                                dve.tensor_tensor(xr[:, :, :], psX_tok, xr[:, :, :], ALU.add).then_inc(S["x2"], 1)
                                dve.wait_ge(S["x2"], c + 1)
                                stats(xr, st2, mv2, S["st2"])
                            if has_a and v == 12:
                                dve.wait_ge(S["vps"], 2 * a + 2)
                                dve.wait_ge(S["cs"], a + 1)
                                dve.tensor_tensor(bo[pa][:, :, :].rearrange("p i (h v) -> p (i h) v", v=DV),
                                                  psX_tok.rearrange("p i (h v) -> p (i h) v", v=DV),
                                                  bcast(cs[:, :], 2, DV), ALU.mult).then_inc(S["bo"], 1)
                            if has_c and v == 12:
                                dve.wait_ge(S["sd2"], c + 1)
                                scales(sd2, mv2, rs2, nb2, S["rs2"])
                            if has_c and v == 15:
                                dve.wait_ge(S["lg"], c + 1)
                                dve.tensor_copy(logits[:, chunk(c), :], psX[:, 0, 0:TC * 16].rearrange(
                                    "p (i e) -> p i e", e=16)[:, :, 0:E]).then_inc(S["lgs"], 1)
                    iterations(dve, body, ch, 2 * LINKS)

                @block.scalar
                def _(act):
                    with nc.allow_non_contiguous_dma(reason="the last columns of each row"):
                        act.dma_start(rows_dram.rearrange("(n p) d -> p n d", p=P)[:, :, IDX:ROW],
                                      bcast(fill[:, IDX:ROW], 1, NB)).then_inc(s_fill, 16)
                    act.wait_ge(S["cst"], 8)
                    act.wait_ge(S["w"], 16 * 17)

                    def norm(dst, src, nb, rs):
                        for i in range(TC):
                            last = act.activation(dst[:, i, :], src[:, i, :], ACT.Identity, bias=nb[:, i:i + 1],
                                                  scale=rs[:, i:i + 1])
                        return last

                    def body(it, par, has_a, has_b, has_c):
                        a, c = it + 1, it - 1
                        pa = 1 - par
                        if has_a:
                            act.wait_ge(S["st"], a + 1)
                            act.activation(sd[:, :], mv[:, :, 1], ACT.Sqrt, bias=eps[:, 0:1]).then_inc(S["sd"], 1)
                            after(act, S["xi"], 10 * a)
                            act.activation(yT[:, :, 0:1], yT[:, :, C:C + 1], ACT.Copy).then_inc(S["yc"], 1)
                            act.wait_ge(S["rs"], a + 1)
                            after(act, S["tr"], a)
                            norm(y, x1, nb, rs).then_inc(S["y"], 1)
                            act.wait_ge(S["tr"], a + 1)
                            act.wait_ge(S["yc"], a + 1)
                            act.activation(yT[:, :, 1:C + 1], psX[:, :, :], ACT.Copy).then_inc(S["yT"], 1)
                        if has_c:
                            act.wait_ge(S["oc"], c + 1)
                            after(act, S["ztr"], c)
                            act.activation(o2[:, :, :], o[:, :, :], ACT.Square).then_inc(S["sq"], 1)
                            act.wait_ge(S["gv"], c + 1)
                            act.activation(gv[:, :], gv[:, :], ACT.Sqrt, bias=eps[:, 0:1],
                                           scale=1.0 / DV).then_inc(S["gsd"], 1)
                        if has_a:
                            act.wait_ge(S["low"], a + 1)
                            act.activation(lowT[:, :], psX[:, 0, :], ACT.Tanh)
                            act.activation(lowTl[:, :], psX[0:LR, 1, :], ACT.Tanh).then_inc(S["lowT"], 1)
                            act.wait_ge(S["rps"], a + 1)
                            after(act, S["P"], 16 * (a - 1))
                            act.activation(rT[pa][:, :], psX[:, 0, :], ACT.Copy).then_inc(S["rT"], 1)
                            act.wait_ge(S["kps"], a + 1)
                            after(act, S["kv"], 16 * (a - 1))
                            act.activation(kT[pa][:, :], psX[:, 1, :], ACT.Copy).then_inc(S["kT"], 1)
                        if has_c:
                            act.wait_ge(S["ztr"], c + 1)
                            after(act, S["o_xnT"], 16 * c)
                            act.activation(zT[:, :, :], psX[:, :, :], ACT.Copy).then_inc(S["zT"], 1)
                        if has_a:
                            act.wait_ge(S["vps"], 2 * a + 1)
                            after(act, S["spread"], 16 * (a - 1))
                            act.activation(vT[pa][:, :, :], psX[:, :, :], ACT.Copy).then_inc(S["vT"], 1)
                        if has_c:
                            act.wait_ge(S["st2"], c + 1)
                            act.activation(sd2[:, :], mv2[:, :, 1], ACT.Sqrt, bias=eps[:, 0:1]).then_inc(S["sd2"], 1)
                            act.wait_ge(S["rs2"], c + 1)
                            after(act, S["ntr"], c)
                            after(act, S["o_xn"], 16 * c)
                            norm(n2, xr, nb2, rs2).then_inc(S["n2"], 1)
                        if has_a:
                            act.wait_ge(S["w1p"], a + 1)
                            act.activation(w1T[:, :], psX[0:GL, 0, :], ACT.Tanh).then_inc(S["w1T"], 1)
                            act.wait_ge(S["w2p"], a + 1)
                            act.activation(ew[:, :], psX[:, 1, :], ACT.Exp, bias=bw2[:, 0:1]).then_inc(S["ew"], 1)
                            act.wait_ge(S["ew"], a + 1)
                            after(act, S["S"], 16 * (a - 1))
                            act.activation(dec[pa][:, :], ew[:, :], ACT.Exp, scale=-1.0).then_inc(S["dec"], 1)
                        if has_c:
                            act.wait_ge(S["ntr"], c + 1)
                            act.activation(zT[:, :, :], psX[:, :, :], ACT.Copy).then_inc(S["nT"], 1)
                        if has_a:
                            act.wait_ge(S["gps"], a + 1)
                            after(act, S["z"], a - 1)
                            act.activation(sg[pa][:, :, :], psX_tok, ACT.Silu).then_inc(S["sg"], 1)
                    iterations(act, body)

                @block.tensor
                def _(pe):
                    pe.wait_ge(S["cst"], 8)
                    pe.wait_ge(S["w"], 16 * 17)

                    def turn(src, done):
                        for k in range(KD):
                            for i in range(TC):
                                last = pe.transpose(psX[:, k, i * P:(i + 1) * P], src[:, i, k * P:(k + 1) * P],
                                                    ident[:, :])
                        last.then_inc(done, 1)

                    def project(dst, w, src):
                        for k in range(KD):
                            last = pe.matmul(dst, w(k), src(k), start=k == 0, stop=k == KD - 1)
                        return last

                    def by_token(w, src, done):
                        for i in range(TC):
                            last = project(psX_tok[:, i, :], lambda k: src[:, k, i * P:(i + 1) * P], lambda k: w[:, k, :])
                        last.then_inc(done, 1)

                    def body(it, par, has_a, has_b, has_c):
                        a, c = it + 1, it - 1
                        pa = 1 - par
                        x_r = x_v = x_g = xi[0]
                        x_k = x_w = xi[1]

                        def mus(n):
                            i = order[n]
                            for k in range(KD):
                                after(pe, S["tm"], 10 * a + 2 * n + k - 1)
                                if i < 4:
                                    ins = pe.matmul(psM[k][:, :], wx2[i * LR:(i + 1) * LR, k * P:(k + 1) * P],
                                                    lowT[i * LR:(i + 1) * LR, :], start=True, stop=True)
                                else:
                                    ins = pe.matmul(psM[k][:, :], wx2l[:, k * P:(k + 1) * P], lowTl[:, :],
                                                    start=True, stop=True)
                                ins.then_inc(S["mus"], 1)

                        def spread(v):
                            if v == 0:
                                pe.wait_ge(S["vT"], it + 1)
                                pe.wait_ge(S["dec"], it + 1)
                            after(pe, S["kv"], 16 * it + v - 1)
                            pe.matmul(psV[v % 2][:, :], sel[:, v % 8, :, :].rearrange("p h k -> p (h k)"),
                                      vT[par][:, v // 8, :], start=True, stop=True).then_inc(S["spread"], 1)

                        def head_sums(t, v):
                            pe.wait_ge(S["P"], 16 * t + v + 1)
                            if v == 0:
                                after(pe, S["oadd"], t)
                            for i in range(TC):
                                last = pe.matmul(psO[:, i, v:D:DV], Pr[v % 4][:, i * P:(i + 1) * P],
                                                 headsum[:, :], start=True, stop=True)
                            last.then_inc(S["o"], 1)

                        if has_b:
                            spread(0)
                        for v in range(16):
                            if has_a and v == 3:
                                pe.wait_ge(S["y"], a + 1)
                                after(pe, S["sg"], a)
                                after(pe, S["lgs"], it - 1)
                                turn(y, S["tr"])
                            if has_a and v == 5:
                                pe.wait_ge(S["xx"], a + 1)
                                pe.wait_ge(S["yT"], a + 1)
                                project(psX[:, 0, :], lambda k: wx1[:, k, 0:P], lambda k: xx[:, k, :])
                                project(psX[0:LR, 1, :], lambda k: wx1[:, k, P:P + LR],
                                        lambda k: xx[:, k, :]).then_inc(S["low"], 1)
                            if has_a and v == 6:
                                pe.wait_ge(S["lowT"], a + 1)
                            if has_a and 6 <= v <= 10:
                                mus(v - 6)
                            if has_a and v == 8:
                                pe.wait_ge(S["xi"], 10 * a + 2)
                                project(psX[:, 0, :], lambda k: wr[:, k, :], lambda k: x_r[:, k, :]).then_inc(S["rps"], 1)
                            if has_a and v == 9:
                                pe.wait_ge(S["xi"], 10 * a + 4)
                                project(psX[:, 1, :], lambda k: wk[:, k, :], lambda k: x_k[:, k, :]).then_inc(S["kps"], 1)
                            if has_a and v == 11:
                                pe.wait_ge(S["rk"], a + 1)
                                pe.wait_ge(S["rT"], a + 1)
                                if has_c:
                                    pe.wait_ge(S["zT"], c + 1)
                                for i in range(TC):
                                    last = pe.matmul(psX[:, 0, i * H:(i + 1) * H], rk[:, i * P:(i + 1) * P], uhead[:, :],
                                                     start=True, stop=True)
                                last.then_inc(S["cp"], 1)
                            if has_a and v == 12:
                                pe.wait_ge(S["vT"], a + 1)
                                if has_c:
                                    pe.wait_ge(S["x2"], c + 1)
                                by_token(wv, x_v, S["vps"])
                            if has_a and v == 13:
                                pe.wait_ge(S["xi"], 10 * a + 8)
                                pe.wait_ge(S["bo"], a + 1)
                                project(psX[0:GL, 0, :], lambda k: ww1[:, k, :],
                                        lambda k: x_w[:, k, :]).then_inc(S["w1p"], 1)
                            if has_b and v < 15:
                                spread(v + 1)
                            if v >= 2 and has_b:
                                head_sums(it, v - 2)
                            if v < 2 and has_c:
                                head_sums(it - 1, 14 + v)
                            if has_c and v == 9:
                                pe.wait_ge(S["z"], c + 1)
                                if has_a:
                                    pe.wait_ge(S["rT"], a + 1)
                                    pe.wait_ge(S["kT"], a + 1)
                                else:
                                    pe.wait_ge(S["lgs"], c)
                                turn(o2, S["ztr"])
                            if has_a and v == 11:
                                pe.wait_ge(S["cs"], a + 1)
                                pe.wait_ge(S["kT"], a + 1)
                                pe.wait_ge(S["xi"], 10 * a + 6)
                                for half in range(KD):
                                    last = project(psX[:, half, :], lambda k: wvT[:, k, half * P:(half + 1) * P],
                                                   lambda k: x_v[:, k, :])
                                last.then_inc(S["vps"], 1)
                            if has_c and v == 11:
                                pe.wait_ge(S["zT"], c + 1)
                                if has_a:
                                    pe.wait_ge(S["vT"], a + 1)
                                by_token(wo, zT, S["wo"])
                            if has_a and v == 13:
                                pe.wait_ge(S["w1T"], a + 1)
                                pe.matmul(psX[:, 1, :], ww2[:, :], w1T[:, :], start=True, stop=True).then_inc(S["w2p"], 1)
                            if has_c and v == 14:
                                pe.wait_ge(S["n2"], c + 1)
                                if has_a:
                                    pe.wait_ge(S["ew"], a + 1)
                                else:
                                    pe.wait_ge(S["x2"], c + 1)
                                turn(n2, S["ntr"])
                            if has_a and v == 15:
                                pe.wait_ge(S["xi"], 10 * a + 10)
                                pe.wait_ge(S["ew"], a + 1)
                                if has_c:
                                    pe.wait_ge(S["nT"], c + 1)
                                by_token(wg, x_g, S["gps"])
                            if has_c and v == 15:
                                pe.wait_ge(S["nT"], c + 1)
                                if has_a:
                                    pe.wait_ge(S["sg"], a + 1)
                                for i in range(TC):
                                    last = project(psX[:, 0, i * 16:i * 16 + E], lambda k: zT[:, k, i * P:(i + 1) * P],
                                                   lambda k: gate[:, k, :])
                                last.then_inc(S["lg"], 1)
                    iterations(pe, body)

        def phase_out():
            s_in = [sem(f"f_in{p}") for p in range(2)]
            s_out = [sem(f"f_out{p}") for p in range(2)]
            s_sum = sem("f_sum")
            with ExitStack() as sc:
                parts = [[sb(f"f_part{p}{q}", [P, TC, D], scope=sc) for q in range(2)] for p in range(2)]
                sum_v = [q.rearrange("(i p) d -> p i d", p=P) for q in sums_dram]
                out_v = out.rearrange("a (i p) d -> p (a i) d", p=P)
                block = sc.enter_context(nc.Block())

                @block.sync
                def _(sp):
                    def turn(h, p):
                        c = 2 * h + p
                        after(sp, s_out[p], 16 * h)
                        for q in range(2):
                            sp.dma_start(parts[p][q][:, :, :], sum_v[q][:, bass.ds(c * TC, TC), :]).then_inc(s_in[p], 16)
                    for p in range(2):
                        turn(0, p)
                    with sp.Fori(1, NC // 2) as h:
                        for p in range(2):
                            turn(h, p)

                @block.scalar
                def _(act):
                    with act.Fori(0, NC // 2) as h:
                        for p in range(2):
                            c = 2 * h + p
                            act.wait_ge(s_sum, c + 1)
                            act.dma_start(out_v[:, bass.ds(c * TC, TC), :], parts[p][0][:, :, :]).then_inc(s_out[p], 16)
                    for p in range(2):
                        act.wait_ge(s_out[p], 8 * NC)

                @block.vector
                def _(dve):
                    with dve.Fori(0, NC // 2) as h:
                        for p in range(2):
                            dve.wait_ge(s_in[p], 32 * h + 32)
                            dve.tensor_tensor(parts[p][0][:, :, :], parts[p][0][:, :, :], parts[p][1][:, :, :],
                                              ALU.add).then_inc(s_sum, 1)

        phase_norm()
        end_phase()
        phase_experts("m1", x.rearrange("a t d -> (a t) d"))
        end_phase()
        phase_attention()
        end_phase()
        phase_experts("m2", x2_dram)
        end_phase()
        phase_out()


def kernel(**inputs):
    import numpy as _np
    import concourse.bacc as _bacc
    from concourse import mybir as _mybir
    from concourse.bass_utils import run_bass_kernel_spmd as _run

    a = {k.replace("L0_attn_", "").replace("L0_ffn_", "f_"): _np.asarray(v) for k, v in inputs.items()}
    w_v = a["W_v"]
    lay = {
        "x": a["x"], "mu_x": a["mu_x"], "W_x1": a["W_x1"],
        "W_x2": a["W_x2"].transpose(1, 2, 0).reshape(5 * LR, D),
        "x_biasT": a["x_bias"].T, "W_r": a["W_r"], "W_w1": a["W_w1"], "W_w2": a["W_w2"], "b_w2": a["b_w2"],
        "W_k": a["W_k"], "W_v": w_v,
        "W_v_vh": w_v.reshape(D, H, DV).transpose(0, 2, 1).reshape(D, D),
        "W_g": a["W_g"], "u": a["u"], "gn_w": a["gn_w"], "gn_b": a["gn_b"], "W_o": a["W_o"],
        "gate_wT": a["f_gate_w"].T, "fc1_wT": a["f_fc1_w"].transpose(0, 2, 1), "fc1_b": a["f_fc1_b"],
        "geglu_mult": a["f_geglu_mult"], "fc2_wT": a["f_fc2_w"].transpose(0, 2, 1), "fc2_b": a["f_fc2_b"],
        "s_fc1_wT": a["f_s_fc1_w"].T, "s_fc1_b": a["f_s_fc1_b"], "s_geglu_mult": a["f_s_geglu_mult"],
        "s_fc2_wT": a["f_s_fc2_w"].T, "s_fc2_b": a["f_s_fc2_b"],
    }
    nc = _bacc.Bacc("TRN2", target_bir_lowering=False, num_devices=1)
    arrays, args = {}, []
    for name, v in lay.items():
        v = _np.ascontiguousarray(v)
        arrays[f"in_{name}"] = v
        args.append(nc.dram_tensor(f"in_{name}", v.shape, _mybir.dt.from_np(v.dtype), kind="ExternalInput").ap())
    res = nc.dram_tensor("out_x", (1, T, D), _mybir.dt.float32, kind="ExternalOutput").ap()
    macaron_kernel(nc, *args, res)
    r = _run(nc, [arrays], core_ids=[0])
    return r.results[0]["out_x"]
```

```python
import concourse.bass as bass
from concourse import mybir
from contextlib import ExitStack, contextmanager

FP32 = mybir.dt.float32
BF16 = mybir.dt.bfloat16
FP32R = mybir.dt.float32r
I32 = mybir.dt.int32
U32 = mybir.dt.uint32
ALU = mybir.AluOpType
ACT = mybir.ActivationFunctionType
AX = mybir.AxisListType.X

P = 128
T = 4096
D = 256
KD = D // P
E = 15
TOPK = 3
F = 256
KF = F // P
FS = 512
KFS = FS // P
H = 16
DK = 8
DV = 16
LR = 32
GL = 64
EPS = 1e-5
NT = T // P
C = 512
NC = T // C
TC = C // P
NB = T * TOPK // P + E
NB += -NB % 4
NQ = NB // 4
W1 = KD * 2 * F + 2 * KF
NBIAS = E * D + D
B2, BS2 = 0, E * D
MIX_R, MIX_W, MIX_K, MIX_V, MIX_G = range(5)


class Chain:

    def __init__(self, eng, sem):
        self.eng, self.sem, self.base, self.n = eng, sem, 0, 0

    def link(self, ins):
        self.n += 1
        ins.then_inc(self.sem, 1)
        self.eng.wait_ge(self.sem, self.base + self.n)

    @contextmanager
    def turns(self, i, count, per_turn):
        before = self.base + self.n
        self.base, self.n = before + i * per_turn, 0
        yield
        assert self.n == per_turn, (self.n, per_turn)
        self.base, self.n = before + count * per_turn, 0


def after(eng, sem, value):
    if not isinstance(value, int) or value > 0:
        eng.wait_ge(sem, value)


def bcast(ap, axis, n):
    ap = ap.unsqueeze(axis)
    shape = list(ap.shape)
    shape[axis] = n
    return ap.to_broadcast(shape)


def macaron_kernel(nc, x, mu_x, W_x1, W_x2, x_biasT, W_r, W_w1, W_w2, b_w2, W_k, W_v, W_g, u, gn_w, gn_b,
                   W_o, gate_wT, fc1_wT, fc1_bT, geglu_multT, fc2_wT, fc2_b, s_fc1_wT, s_fc1_bT, s_geglu_multT,
                   s_fc2_wT, s_fc2_b, out):
    ctx = ExitStack()
    in_use = []
    with ctx:
        def dram(name, shape, dt):
            return nc.dram_tensor(name, shape, dt, kind="Internal").ap()

        def sb(name, shape, dt=FP32, scope=ctx):
            return scope.enter_context(nc.sbuf_tensor(name, shape, dt))

        def ps(name, shape, dt=FP32, scope=ctx):
            return scope.enter_context(nc.psum_tensor(name, shape, dt))

        def sem(name):
            in_use.append(nc.alloc_semaphore(name=name))
            return in_use[-1]

        def end_phase():
            nc.clear_and_free_semaphores(in_use)
            nc.all_engine_barrier()
            in_use.clear()

        xn_dram = dram("xn_scratch", (T + P, D), FP32)
        xnT_dram = dram("xnT_scratch", (D, T), FP32)
        x1_dram = dram("x1_scratch", (T, D), FP32)
        x2_dram = dram("x2_scratch", (T, D), FP32)
        bias_dram = dram("bias_scratch", (3, NBIAS), BF16)
        rows_dram = dram("rows_scratch", (NB * P, 2), FP32)
        rows_v = rows_dram.rearrange("(p b) d -> p b d", b=NB)
        sums_dram = [dram(f"sum{q}_scratch", (T + P, D), FP32) for q in range(2)]

        ident = sb("ident", [P, P])
        eps = sb("eps", [P, 1])
        pad = sb("pad", [P, 2])
        ones3 = sb("ones3", [P, P], BF16)
        tri = sb("tri", [P, P], BF16)
        ones = sb("ones", [P, P], BF16)
        gate = sb("gate", [P, KD, P])
        logits = sb("logits", [P, NT, E])
        bias = sb("bias", [P, NBIAS], BF16)
        zero = sb("zero", [P, D])
        fill = sb("fill", [P, NB, 2])
        s_fill = nc.alloc_semaphore(name="fill")
        turn_experts = sb("turn_experts", [1, NQ], I32)

        def phase_norm():
            s_ident, s_cst, s_zero, s_gate, s_braw, s_bpart, s_bout, s_bin, s_dummy = (
                sem(f"a_{n}") for n in ("ident", "cst", "zero", "gate", "braw", "bpart", "bout", "bin", "dummy"))
            s_xin = [sem(f"a_xin{p}") for p in range(2)]
            s_xnout = [sem(f"a_xnout{p}") for p in range(2)]
            s_xTout = [sem(f"a_xTout{p}") for p in range(2)]
            s_stats, s_std, s_norm, s_tr, s_xT, s_lg, s_lgsb = (
                sem(f"a_{n}") for n in ("stats", "std", "norm", "tr", "xT", "lg", "lgsb"))
            s_dve = sem("a_dve")
            with ExitStack() as sc:
                braw = sb("a_braw", [P, NBIAS // P], scope=sc)
                bpart = sb("a_bpart", [P, 3, NBIAS // P], BF16, scope=sc)
                xin = sb("a_x", [P, NT, D], scope=sc)
                xn = [sb(f"a_xn{p}", [P, TC, D], scope=sc) for p in range(2)]
                xT = [sb(f"a_xT{p}", [P, KD, C], scope=sc) for p in range(2)]
                st = [sb(f"a_st{p}", [P, TC, 6], scope=sc) for p in range(2)]
                mv = [sb(f"a_mv{p}", [P, TC, 2], scope=sc) for p in range(2)]
                sd = [sb(f"a_sd{p}", [P, TC], scope=sc) for p in range(2)]
                rs = [sb(f"a_rs{p}", [P, TC], scope=sc) for p in range(2)]
                psT = [ps(f"a_psT{p}", [P, KD, C], scope=sc) for p in range(2)]
                psL = [ps(f"a_psL{p}", [P, TC, P], scope=sc) for p in range(2)]
                x_v = x.rearrange("a (i p) d -> p (a i) d", p=P)
                xn_v = xn_dram.rearrange("(i p) d -> p i d", p=P)
                xnT_v = xnT_dram.rearrange("(k p) t -> p k t", p=P)
                flat = [(fc2_b.rearrange("e d -> (e d)"), B2, BS2), (s_fc2_b, BS2, NBIAS)]
                block = sc.enter_context(nc.Block())

                def turns(eng, turn, last=None):
                    turn(0, 0, 0, None)
                    turn(0, 1, 1, (0, 0))
                    with eng.Fori(1, NC // 2) as h:
                        turn(h, 0, 2 * h, (h - 1, 1))
                        turn(h, 1, 2 * h + 1, (h, 0))
                    if last:
                        last(NC // 2 - 1, 1)

                @block.sync
                def _(sp):
                    def load(c, p):
                        sp.dma_start(xin[:, bass.ds(c * TC, TC), :], x_v[:, bass.ds(c * TC, TC), :]).then_inc(s_xin[p], 16)

                    def store(c, p):
                        sp.wait_ge(s_norm, c + 1)
                        sp.dma_start(xn_v[:, bass.ds(c * TC, TC), :], xn[p][:, :, :]).then_inc(s_xnout[p], 16)
                    load(0, 0)
                    load(1, 1)
                    sp.wait_ge(s_gate, 1)
                    sp.dma_start(gate[:, :, 0:E], gate_wT.rearrange("(k p) e -> p k e", p=P)).then_inc(s_gate, 16)
                    for src, lo, hi in flat:
                        sp.dma_start(braw[:, lo // P:hi // P], src.rearrange("(p n) -> p n", p=P)).then_inc(s_braw, 16)
                    with sp.Fori(0, NC // 2 - 1) as h:
                        for p in range(2):
                            sp.wait_ge(s_xin[p], 16 * h + 16)
                            load(2 * h + p + 2, p)
                            store(2 * h + p, p)
                    sp.wait_ge(s_bpart, 3)
                    for n in range(3):
                        for src, lo, hi in flat:
                            sp.dma_start(bias_dram[n, lo:hi].rearrange("(p n) -> p n", p=P),
                                         bpart[:, n, lo // P:hi // P]).then_inc(s_bout, 16)
                    for p in range(2):
                        store(NC - 2 + p, p)
                    sp.wait_ge(s_bout, 6 * 16)
                    sp.wait_ge(s_zero, 3)
                    for n, r in enumerate((0, 32, 64)):
                        sp.dma_start(bias[r:r + 1, :], bias_dram[n:n + 1, :]).then_inc(s_bin, 16)
                    sp.wait_ge(s_bin, 3 * 16)
                    for p in range(2):
                        sp.wait_ge(s_xnout[p], 16 * (NC // 2))

                @block.gpsimd
                def _(pool):
                    pool.memset(ident[:, :], 0.0).then_inc(s_ident, 1)
                    pool.memset(eps[:, :], EPS).then_inc(s_cst, 1)
                    pool.wait_ge(s_ident, 1)
                    pool.affine_select(out=ident[:, :], in_=ident[:, :], compare_op=ALU.not_equal, fill=1.0,
                                       base=0, pattern=[[-1, P]], channel_multiplier=1).then_inc(s_ident, 1)
                    pool.memset(gate[:, :, :], 0.0).then_inc(s_gate, 1)
                    pool.memset(zero[:, :], 0.0).then_inc(s_zero, 1)
                    pool.memset(fill[:, :, :], 0.0).then_inc(s_zero, 1)
                    pool.wait_ge(s_zero, 2)
                    pool.iota(fill[:, :, 0], pattern=[[0, NB]], base=T, channel_multiplier=1,
                              allow_small_or_imprecise_dtypes=True).then_inc(s_cst, 1)
                    pool.memset(bias[:, :].bitcast(U32), 0).then_inc(s_zero, 1)
                    pool.memset(ones[:, :], 1.0).then_inc(s_cst, 1)
                    pool.memset(ones3[:, :], 0.0).then_inc(s_cst, 1)
                    pool.wait_ge(s_cst, 4)
                    pool.affine_select(out=tri[:, :], in_=ones[:, :], compare_op=ALU.is_gt, fill=0.0,
                                       base=0, pattern=[[1, P]], channel_multiplier=-1).then_inc(s_cst, 1)
                    for n, r in enumerate((0, 32, 64)):
                        pool.wait_ge(s_cst, 5 + n)
                        pool.memset(ones3[r:r + 1, :], 1.0).then_inc(s_cst, 1)

                @block.vector
                def _(dve):
                    ch = Chain(dve, s_dve)

                    def take(h, p):
                        c = 2 * h + p
                        dve.wait_ge(s_lg, c + 1)
                        dve.tensor_copy(logits[:, bass.ds(c * TC, TC), :], psL[p][:, :, 0:E]).then_inc(s_lgsb, 1)

                    def turn(h, p, c, prev):
                        dve.wait_ge(s_xin[p], 16 * h + 16)
                        for j in range(TC):
                            last = dve.bn_stats(st[p][:, j, :], xin[:, bass.ds(c * TC + j, 1), :])
                        ch.link(last)
                        dve.memset(pad[:, 0:1], 0.0)
                        for j in range(TC):
                            last = dve.bn_aggr(mv[p][:, j, :], st[p][:, j, :])
                        last.then_inc(s_stats, 1)
                        dve.wait_ge(s_std, c + 1)
                        ch.link(dve.reciprocal(rs[p][:, :], sd[p][:, :]))
                        after(dve, s_xnout[p], 16 * h)
                        after(dve, s_tr, c - 1)
                        for j in range(TC):
                            last = dve.tensor_scalar(xn[p][:, j, :], xin[:, bass.ds(c * TC + j, 1), :], mv[p][:, j, 0:1],
                                                     rs[p][:, j:j + 1], ALU.subtract, ALU.mult)
                        last.then_inc(s_norm, 1)
                        if prev:
                            take(*prev)
                    turn(0, 0, 0, None)
                    dve.wait_ge(s_braw, 2 * 16)
                    for n in range(3):
                        if n:
                            ch.link(dve.tensor_tensor(braw[:, :], braw[:, :], bpart[:, n - 1, :], ALU.subtract))
                        dve.tensor_copy(bpart[:, n, :], braw[:, :]).then_inc(s_bpart, 1)
                        dve.wait_ge(s_bpart, n + 1)
                    turn(0, 1, 1, (0, 0))
                    with dve.Fori(1, NC // 2) as h, ch.turns(h - 1, NC // 2 - 1, 2 * 2):
                        turn(h, 0, 2 * h, (h - 1, 1))
                        turn(h, 1, 2 * h + 1, (h, 0))
                    take(NC // 2 - 1, 1)

                @block.scalar
                def _(act):
                    def take(h, p):
                        c = 2 * h + p
                        act.wait_ge(s_tr, c + 1)
                        after(act, s_xTout[p], 16 * h)
                        after(act, s_lg, c - 1)
                        act.activation(xT[p][:, :, :], psT[p][:, :, :], ACT.Copy).then_inc(s_xT, 1)
                        act.wait_ge(s_xT, c + 1)
                        act.dma_start(xnT_v[:, :, bass.ds(c * C, C)], xT[p][:, :, :]).then_inc(s_xTout[p], 16)

                    def turn(h, p, c, prev):
                        if prev:
                            take(*prev)
                        act.wait_ge(s_stats, c + 1)
                        act.activation(sd[p][:, :], mv[p][:, :, 1], ACT.Sqrt, bias=eps[:, 0:1]).then_inc(s_std, 1)
                    act.wait_ge(s_cst, 2)
                    turns(act, turn, take)
                    act.dma_start(rows_v, fill[:, :, :]).then_inc(s_fill, 16)
                    for dst in (xn_dram, *sums_dram):
                        act.dma_start(dst[T:T + P, :], zero[:, :]).then_inc(s_dummy, 16)
                    for p in range(2):
                        act.wait_ge(s_xTout[p], 16 * (NC // 2))
                    act.wait_ge(s_dummy, 16 * 3)

                @block.tensor
                def _(pe):
                    pe.wait_ge(s_ident, 2)
                    pe.wait_ge(s_gate, 17)

                    def take(h, p):
                        c = 2 * h + p
                        pe.wait_ge(s_xT, c + 1)
                        after(pe, s_lgsb, c - 1)
                        for j in range(TC):
                            for k in range(KD):
                                last = pe.matmul(psL[p][:, j, :], xT[p][:, k, j * P:(j + 1) * P],
                                                 gate[:, k, :], start=k == 0, stop=k == KD - 1)
                        last.then_inc(s_lg, 1)

                    def turn(h, p, c, prev):
                        if prev:
                            take(*prev)
                        pe.wait_ge(s_norm, c + 1)
                        after(pe, s_xT, c - 1)
                        for k in range(KD):
                            for j in range(TC):
                                last = pe.transpose(psT[p][:, k, j * P:(j + 1) * P],
                                                    xn[p][:, j, k * P:(k + 1) * P], ident[:, :])
                        last.then_inc(s_tr, 1)
                    turns(pe, turn, take)

        def phase_experts(tag, x_src):
            with ExitStack() as we:
                w1 = sb(f"{tag}_w1", [P, E * W1], scope=we)
                w2 = sb(f"{tag}_w2", [P, E * KF * D], scope=we)
                route(tag, x_src, w1, w2)
                experts(tag, w1, w2)

        def route(tag, x_src, w1, w2):
            def s(n):
                return sem(f"{tag}r_{n}")
            s_w, s_gm, s_ws, s_ws2, s_iota, s_idx, s_fold, s_wfold = (
                s(n) for n in ("w", "gm", "ws", "ws2", "iota", "idx", "fold", "wfold"))
            s_xT = [s(f"xT{p}") for p in range(2)]
            s_xr = [s(f"xr{p}") for p in range(2)]
            s_out = [s(f"out{p}") for p in range(2)]
            s_dve, s_hot, s_rank, s_exp, s_soft, s_pos, s_scat = (
                s(n) for n in ("dve", "hot", "rank", "exp", "soft", "pos", "scat"))
            s_h, s_ge, s_a, s_y, s_acc, s_zeroed, s_whi, s_wlo, s_xhi, s_xlo, s_ahi, s_alo = (
                s(n) for n in ("h", "ge", "a", "y", "acc", "zeroed", "whi", "wlo", "xhi", "xlo", "ahi", "alo"))
            s_w1, s_routed = (s(n) for n in ("w1", "routed"))
            with ExitStack() as sc:
                def small(n, shape, dt=FP32):
                    return sb(f"{tag}_{n}", shape, dt, scope=sc)
                ws1 = w2[:, 0:KD * 2 * FS].rearrange("p (k f) -> p k f", k=KD)
                ws2 = w2[:, KD * 2 * FS:KD * 2 * FS + KFS * D].rearrange("p (k d) -> p k d", k=KFS)

                def table(at, *shape):
                    n = 1
                    for size in shape:
                        n *= size
                    names = "abc"[:len(shape)]
                    return w1[:, at:at + n].rearrange(f"p ({' '.join(names)}) -> p {' '.join(names)}",
                                                      **dict(zip(names, shape)))
                tmp = table(0, NT, E)
                tot, inc, keep = (table(n * NT * E, E, NT) for n in (1, 2, 3))
                hot = table(4 * NT * E, TOPK, NT, E)
                past = table((4 + TOPK) * NT * E, NB, E)[0:1]
                ws1s = small("ws1s", [P, 2, KD, 2 * FS], FP32R)
                ws2s = small("ws2s", [P, 2, KFS, D], FP32R)
                xTs = [small(f"xTs{p}", [P, 2, KD, C], FP32R) for p in range(2)]
                aTs = [small(f"aTs{p}", [P, 2, KFS, C], FP32R) for p in range(2)]
                gms = small("gms", [P, KFS])
                gm = small("gm", [P, E * KF])
                bs1 = small("bs1", [P, 2 * KFS])
                rows = small("rows", [P, TOPK, NT, 2])
                xT = [small(f"xT{p}", [P, KD, C]) for p in range(2)]
                xr = [small(f"xr{p}", [P, TC, D]) for p in range(2)]
                ge = small("ge", [P, 2, C])
                aT = [small(f"aT{q}", [P, C]) for q in range(2)]
                ph = [ps(f"{tag}_ph{q}", [P, 2, C], scope=sc) for q in range(2)]
                py = ps(f"{tag}_py", [P, TC, D], scope=sc)
                prank = ps(f"{tag}_prank", [P, NT * E], scope=sc)
                ptot = ps(f"{tag}_ptot", [P, NT * E], scope=sc)
                top = small("top", [P, NT, 8])
                topi = small("topi", [P, NT, 8], U32)
                chosen = small("chosen", [P, TOPK, NT])
                iota_e = small("iota_e", [P, E])
                iota_b = small("iota_b", [1, NB])
                many = small("many", [P, NT, E], BF16)
                nblk = small("nblk", [P, E])
                nblk_i = small("nblk_i", [P, E], I32)
                endb = small("endb", [P, E])
                off = small("off", [P, E])
                one_e = small("one_e", [P, E])
                block_expert = small("block_expert", [1, NB + 2])
                packed = small("packed", [1, NQ])
                soft = small("soft", [P, NT])
                etop = small("etop", [P, TOPK, NT])
                tables = [table((4 + TOPK) * NT * E + NB * E + n * TOPK * NT, TOPK, NT) for n in range(4)]
                posf = tables[0]
                posi, spot, blk = (t.bitcast(I32) for t in tables[1:])
                pos = small("pos", [P, TOPK, NT], I32)

                x_v = x_src.rearrange("(i p) d -> p i d", p=P)
                xnT_v = xnT_dram.rearrange("(k p) t -> p k t", p=P)
                sum_v, zero_v = (q.rearrange("(i p) d -> p i d", p=P) for q in sums_dram)
                w2_e = w2[:, :].rearrange("p (e k d) -> p e k d", e=E, k=KF)
                w1_e = w1[:, :].rearrange("p (e c) -> p e c", e=E)
                block = sc.enter_context(nc.Block())

                @block.sync
                def _(sp):
                    def load(h, p):
                        c = 2 * h + p
                        after(sp, s_xlo, c - 1)
                        sp.dma_start(xT[p][:, :, :], xnT_v[:, :, bass.ds(c * C, C)]).then_inc(s_xT[p], 16)
                        after(sp, s_out[p], 16 * h)
                        sp.dma_start(xr[p][:, :, :], x_v[:, bass.ds(c * TC, TC), :]).then_inc(s_xr[p], 16)
                    sp.dma_start(ws1[:, :, :], s_fc1_wT.rearrange("(k p) f -> p k f", p=P)).then_inc(s_ws, 16)
                    sp.dma_start(bs1[:, :], s_fc1_bT[:, :]).then_inc(s_ws, 16)
                    load(0, 0)
                    sp.dma_start(ws2[:, :, :], s_fc2_wT.rearrange("(k p) d -> p k d", p=P)).then_inc(s_ws2, 16)
                    load(0, 1)
                    sp.dma_start(gms[:, :], s_geglu_multT[:, :]).then_inc(s_ws2, 16)
                    sp.dma_start(gm[:, :], geglu_multT[:, :]).then_inc(s_gm, 16)
                    sp.wait_ge(s_wlo, 1)
                    sp.wait_ge(s_fold, 2)
                    for e in range(E):
                        sp.dma_start(w2_e[:, e], fc2_wT[e].rearrange("(k p) d -> p k d", p=P)).then_inc(s_w, 16)
                    with sp.Fori(1, NC // 2) as h:
                        for p in range(2):
                            load(h, p)
                    sp.wait_ge(s_w1, 16 * E + 16)

                @block.gpsimd
                def _(pool):
                    pool.iota(iota_e[:, :], pattern=[[1, E]], base=0, channel_multiplier=0,
                              allow_small_or_imprecise_dtypes=True).then_inc(s_iota, 1)
                    pool.iota(iota_b[:, :], pattern=[[1, NB]], base=0, channel_multiplier=0,
                              allow_small_or_imprecise_dtypes=True).then_inc(s_iota, 1)
                    pool.iota(rows[:, :, :, 0], pattern=[[0, TOPK], [P, NT]], base=0, channel_multiplier=1,
                              allow_small_or_imprecise_dtypes=True).then_inc(s_idx, 1)
                    pool.wait_ge(s_idx, 1)
                    pool.wait_ge(s_fill, 16 if tag == "m1" else 32)
                    pool.wait_ge(s_pos, 2)
                    for i in range(NT):
                        for j in range(TOPK):
                            pool.indirect_dma_start(
                                out=rows_dram[:, :], out_offset=bass.IndirectOffsetOnAxis(ap=pos[:, j, i:i + 1], axis=0),
                                in_=rows[:, j, i, :], in_offset=None).then_inc(s_scat, 16)
                    pool.wait_ge(s_scat, 16 * NT * TOPK)

                @block.vector
                def _(dve):
                    ch = Chain(dve, s_dve)

                    def find():
                        for i in range(NT):
                            last = dve.max(top[:, i, :], logits[:, i, :])
                        ch.link(last)
                        for i in range(NT):
                            last = dve.max_index(topi[:, i, :], top[:, i, :], logits[:, i, :])
                        ch.link(last)
                        ch.link(dve.tensor_copy(chosen[:, :, :].rearrange("p j i -> p i j"), topi[:, :, 0:TOPK]))

                    def mark():
                        dve.wait_ge(s_iota, 2)
                        for j in range(TOPK):
                            last = dve.tensor_tensor(hot[:, j, :, :], bcast(iota_e[:, :], 1, NT),
                                                     bcast(chosen[:, j, :], 2, E), ALU.is_equal)
                        ch.link(last)
                        ch.link(dve.tensor_tensor(tmp[:, :, :], hot[:, 0, :, :], hot[:, 1, :, :], ALU.add))
                        dve.tensor_tensor(many[:, :, :], tmp[:, :, :], hot[:, 2, :, :], ALU.add).then_inc(s_hot, 1)

                    def fold():
                        dve.wait_ge(s_ws2, 32)
                        for k in range(KFS):
                            last = dve.tensor_scalar(ws2[:, k, :], ws2[:, k, :], gms[:, k:k + 1], None, ALU.mult)
                        ch.link(last)
                        dve.tensor_copy(ws2s[:, 0, :, :], ws2[:, :, :]).then_inc(s_fold, 1)
                        dve.wait_ge(s_fold, 1)
                        dve.tensor_tensor(ws2s[:, 1, :, :], ws2[:, :, :], ws2s[:, 0, :, :].bitcast(FP32),
                                          ALU.subtract).then_inc(s_fold, 1)

                    def soften():
                        ch.link(dve.memset(keep[:, :, :], 1.0))
                        ch.link(dve.memset(keep[:, :, 0:1], 0.0))
                        ch.link(dve.memset(one_e[:, :], 1.0))
                        dve.tensor_tensor(etop[:, :, :], top[:, :, 0:TOPK].rearrange("p i j -> p j i"),
                                          bcast(top[:, :, 0], 1, TOPK), ALU.subtract)
                        dve.wait_ge(s_hot, 1)
                        dve.tensor_tensor(tmp[:, :, :], logits[:, :, :], bcast(top[:, :, 0], 2, E),
                                          ALU.subtract).then_inc(s_soft, 1)

                    def count():
                        dve.wait_ge(s_rank, 1)
                        ch.link(dve.tensor_copy(tot[:, :, :], ptot[:, :].rearrange("p (i e) -> p e i", e=E)))
                        ch.link(dve.tensor_tensor_scan(inc[:, :, :].rearrange("p e i -> p (e i)"),
                                                       keep[:, :, :].rearrange("p e i -> p (e i)"),
                                                       tot[:, :, :].rearrange("p e i -> p (e i)"), 0.0, ALU.mult,
                                                       ALU.add))
                        ch.link(dve.tensor_scalar(nblk_i[:, :], inc[:, :, NT - 1], float(P - 1), None, ALU.add))
                        ch.link(dve.tensor_scalar(nblk_i[:, :], nblk_i[:, :], 7, None, ALU.arith_shift_right))
                        ch.link(dve.tensor_copy(nblk[:, :], nblk_i[:, :]))
                        ch.link(dve.tensor_tensor_scan(endb[:, :], one_e[:, :], nblk[:, :], 0.0, ALU.mult, ALU.add))
                        ch.link(dve.tensor_tensor(off[:, :], endb[:, :], nblk[:, :], ALU.subtract))
                        ch.link(dve.tensor_scalar(off[:, :], off[:, :], float(P), None, ALU.mult))
                        ch.link(dve.tensor_tensor(inc[:, :, :], inc[:, :, :], tot[:, :, :], ALU.subtract))
                        ch.link(dve.tensor_tensor(inc[:, :, :], inc[:, :, :], bcast(off[:, :], 2, NT), ALU.add))
                        ch.link(dve.tensor_tensor(tot[:, :, :], prank[:, :].rearrange("p (i e) -> p e i", e=E),
                                                  inc[:, :, :], ALU.add))

                    def place():
                        for j in range(TOPK):
                            ch.link(dve.tensor_tensor(inc[:, :, :], hot[:, j, :, :].rearrange("p i e -> p e i"),
                                                      tot[:, :, :], ALU.mult))
                            ch.link(dve.tensor_reduce(posf[:, j, :], inc[:, :, :].rearrange("p e i -> p i e"), AX, ALU.add))
                        ch.link(dve.tensor_copy(posi[:, :, :], posf[:, :, :]))
                        dve.tensor_scalar(spot[:, :, :], posi[:, :, :], P - 1, None, ALU.bitwise_and)
                        ch.link(dve.tensor_scalar(blk[:, :, :], posi[:, :, :], 7, None, ALU.arith_shift_right))
                        dve.scalar_tensor_tensor(pos[:, :, :], spot[:, :, :], float(NB), blk[:, :, :], ALU.mult,
                                                 ALU.add).then_inc(s_pos, 1)

                    def shares():
                        dve.wait_ge(s_exp, 2)
                        ch.link(dve.tensor_reduce(soft[:, :], tmp[:, :, :], AX, ALU.add))
                        ch.link(dve.reciprocal(soft[:, :], soft[:, :]))
                        ch.link(dve.tensor_tensor(etop[:, :, :], etop[:, :, :], bcast(soft[:, :], 1, TOPK), ALU.mult))
                        ch.link(dve.tensor_reduce(soft[:, :], etop[:, :, :].rearrange("p j i -> p i j"), AX, ALU.add))
                        ch.link(dve.tensor_scalar(soft[:, :], soft[:, :], 1e-20, None, ALU.add))
                        ch.link(dve.reciprocal(soft[:, :], soft[:, :]))
                        ch.link(dve.tensor_scalar(soft[:, :], soft[:, :], 0.5, None, ALU.mult))
                        dve.wait_ge(s_idx, 1)
                        dve.tensor_tensor(rows[:, :, :, 1], etop[:, :, :], bcast(soft[:, :], 1, TOPK),
                                          ALU.mult).then_inc(s_pos, 1)

                    def blocks():
                        ch.link(dve.tensor_tensor(past[:, :, :], bcast(iota_b[:, :], 2, E),
                                                  bcast(endb[0:1, :], 1, NB), ALU.is_ge))
                        ch.link(dve.memset(block_expert[:, :], 0.0))
                        ch.link(dve.tensor_reduce(block_expert[:, 1:1 + NB], past[:, :, :], AX, ALU.add))
                        ch.link(dve.tensor_scalar(block_expert[:, :], block_expert[:, :], float(E - 1), None, ALU.min))
                        ch.link(dve.memset(packed[:, :], 0.0))
                        for q in range(6):
                            ch.link(dve.scalar_tensor_tensor(packed[:, :], block_expert[:, q:q + NB - 3:4],
                                                             float(16 ** q), packed[:, :], ALU.mult, ALU.add))
                        dve.tensor_copy(turn_experts[:, :], packed[:, :]).then_inc(s_routed, 1)
                        dve.wait_ge(s_routed, 1)

                    def residual(h, p):
                        dve.wait_ge(s_y, 2 * h + p + 1)
                        dve.wait_ge(s_xr[p], 16 * h + 16)
                        dve.scalar_tensor_tensor(xr[p][:, :, :], py[:, :, :], 0.5, xr[p][:, :, :],
                                                 ALU.mult, ALU.add).then_inc(s_acc, 1)

                    def x_low(h, p):
                        c = 2 * h + p
                        dve.wait_ge(s_xT[p], 16 * h + 16)
                        dve.wait_ge(s_xhi, c + 1)
                        dve.tensor_tensor(xTs[p][:, 1, :, :], xT[p][:, :, :], xTs[p][:, 0, :, :].bitcast(FP32),
                                          ALU.subtract).then_inc(s_xlo, 1)

                    def a_low(h, p, f):
                        dve.wait_ge(s_ahi, (2 * h + p) * KFS + f + 1)
                        dve.tensor_tensor(aTs[p][:, 1, f, :], aT[f % 2][:, :], aTs[p][:, 0, f, :].bitcast(FP32),
                                          ALU.subtract).then_inc(s_alo, 1)

                    def turn(h, p, between=(), last=False):
                        c = 2 * h + p
                        after(dve, s_y, c - 1)
                        for f in range(KFS):
                            dve.wait_ge(s_ge, c * KFS + f + 1)
                            after(dve, s_alo, c * KFS + f - 1)
                            dve.scalar_tensor_tensor(
                                aT[f % 2][:, :], ph[f % 2][:, 0, :], bs1[:, f:f + 1], ge[:, f % 2, :],
                                ALU.add, ALU.mult).then_inc(s_a, 1)
                            if f:
                                a_low(h, p, f - 1)
                            elif p or not isinstance(h, int) or h:
                                a_low(h if p else h - 1, 1 - p, KFS - 1)
                            if f < len(between):
                                between[f]()
                            if f == 1 and not last:
                                x_low(h + p, 1 - p)
                            if f == 2 and (p or not isinstance(h, int) or h):
                                residual(h if p else h - 1, 1 - p)
                    dve.wait_ge(s_ws, 32)
                    dve.wait_ge(s_whi, 1)
                    dve.tensor_tensor(ws1s[:, 1, :, :], ws1[:, :, :], ws1s[:, 0, :, :].bitcast(FP32),
                                      ALU.subtract).then_inc(s_wlo, 1)
                    x_low(0, 0)
                    find()
                    turn(0, 0, (mark, fold, soften, count))
                    turn(0, 1, (place, shares, blocks))
                    with dve.Fori(1, NC // 2 - 1) as h:
                        for p in range(2):
                            turn(h, p)
                    for p in range(2):
                        turn(NC // 2 - 1, p, last=p == 1)
                    a_low(NC // 2 - 1, 1, KFS - 1)
                    dve.wait_ge(s_gm, 16)
                    dve.wait_ge(s_w, 16 * E)
                    for n in range(E * KF // 2, E * KF):
                        last = dve.tensor_scalar(w2[:, n * D:(n + 1) * D], w2[:, n * D:(n + 1) * D], gm[:, n:n + 1],
                                                 None, ALU.mult)
                    last.then_inc(s_wfold, 1)
                    residual(NC // 2 - 1, 1)

                @block.scalar
                def _(act):
                    act.wait_ge(s_ws, 32)
                    act.activation(ws1s[:, 0, :, :], ws1[:, :, :], ACT.Copy).then_inc(s_whi, 1)

                    def store(h, p):
                        c = 2 * h + p
                        act.wait_ge(s_acc, c + 1)
                        act.dma_start(sum_v[:, bass.ds(c * TC, TC), :], xr[p][:, :, :]).then_inc(s_out[p], 16)
                        act.dma_start(zero_v[:, bass.ds(c * TC, TC), :], bcast(zero[:, :], 1, TC)).then_inc(s_zeroed, 16)

                    PER = -(-E // (NC - 3))

                    def load_w1(c):
                        for n in range(PER):
                            e = PER * (c - 2) + n
                            if not isinstance(e, int) or e < E:
                                act.dma_start(w1[:, bass.ds(e * W1, KD * 2 * F)].rearrange("p (k f) -> p k f", k=KD),
                                              fc1_wT[bass.ds(e, 1)].rearrange("e (k p) f -> p (e k) f", p=P)
                                              ).then_inc(s_w1, 16)

                    def x_high(h, p):
                        c = 2 * h + p
                        act.wait_ge(s_xT[p], 16 * h + 16)
                        after(act, s_h, (c - 1) * KFS)
                        act.activation(xTs[p][:, 0, :, :], xT[p][:, :, :], ACT.Copy).then_inc(s_xhi, 1)

                    def a_high(h, p, f):
                        c = 2 * h + p
                        if f == 0:
                            after(act, s_y, c - 1)
                        act.wait_ge(s_a, c * KFS + f + 1)
                        act.activation(aTs[p][:, 0, f, :], aT[f % 2][:, :], ACT.Copy).then_inc(s_ahi, 1)

                    def turn(h, p, last=False):
                        c = 2 * h + p
                        for f in range(KFS):
                            act.wait_ge(s_h, c * KFS + f + 1)
                            after(act, s_a, c * KFS + f - 1)
                            act.activation(ge[:, f % 2, :], ph[f % 2][:, 1, :], ACT.Gelu,
                                           bias=bs1[:, KFS + f:KFS + f + 1]).then_inc(s_ge, 1)
                            if f:
                                a_high(h, p, f - 1)
                            elif p or not isinstance(h, int) or h:
                                a_high(h if p else h - 1, 1 - p, KFS - 1)
                            if f == 1 and not last:
                                x_high(h + p, 1 - p)
                        if not isinstance(h, int) or h and not last:
                            load_w1(c)
                        if p:
                            store(h, 0)
                        elif not isinstance(h, int) or h:
                            store(h - 1, 1)
                    x_high(0, 0)
                    turn(0, 0)
                    act.wait_ge(s_soft, 1)
                    act.activation(tmp[:, :, :], tmp[:, :, :], ACT.Exp).then_inc(s_exp, 1)
                    act.activation(etop[:, :, :], etop[:, :, :], ACT.Exp).then_inc(s_exp, 1)
                    turn(0, 1)
                    act.wait_ge(s_routed, 1)
                    act.dma_start(w1_e[:, :, KD * 2 * F:W1], fc1_bT[:, :, :]).then_inc(s_w1, 16)
                    with act.Fori(1, NC // 2 - 1) as h:
                        for p in range(2):
                            turn(h, p)
                    for p in range(2):
                        turn(NC // 2 - 1, p, last=p == 1)
                    a_high(NC // 2 - 1, 1, KFS - 1)
                    act.wait_ge(s_gm, 16)
                    act.wait_ge(s_w, 16 * E)
                    for n in range(E * KF // 2):
                        last = act.activation(w2[:, n * D:(n + 1) * D], w2[:, n * D:(n + 1) * D], ACT.Copy,
                                              scale=gm[:, n:n + 1])
                    last.then_inc(s_wfold, 1)
                    store(NC // 2 - 1, 1)
                    for p in range(2):
                        act.wait_ge(s_out[p], 8 * NC)
                    act.wait_ge(s_zeroed, 16 * NC)

                @block.tensor
                def _(pe):
                    def ranks():
                        pe.wait_ge(s_hot, 1)
                        pe.matmul(prank[:, :], tri[:, :], many[:, :, :].rearrange("p i e -> p (i e)"), start=True,
                                  stop=True)
                        pe.matmul(ptot[:, :], ones[:, :], many[:, :, :].rearrange("p i e -> p (i e)"), start=True,
                                  stop=True).then_inc(s_rank, 1)

                    def products(dst, left, right, steps, start=True):
                        terms = [(i, j, n) for n in range(steps) for i, j in ((0, 0), (0, 1), (1, 0))]
                        for t, (i, j, n) in enumerate(terms):
                            last = pe.matmul(dst, left(i, n), right(j, n), start=start and t == 0,
                                             stop=t == len(terms) - 1)
                        return last

                    def fc1(c, p, f):
                        after(pe, s_a, c * KFS + f - 1)
                        for side in range(2):
                            lo = side * FS + f * P
                            last = products(ph[f % 2][:, side, :], lambda i, k: ws1s[:, i, k, lo:lo + P],
                                            lambda j, k: xTs[p][:, j, k, :], KD)
                        last.then_inc(s_h, 1)

                    def fc2(c, p):
                        pe.wait_ge(s_alo, (c + 1) * KFS)
                        after(pe, s_acc, c)
                        for t in range(TC):
                            pe.matmul(py[:, t, :], ones3[:, :], bias[:, BS2:NBIAS], start=True, stop=False)
                            last = products(py[:, t, :], lambda i, f: aTs[p][:, i, f, t * P:(t + 1) * P],
                                            lambda j, f: ws2s[:, j, f, :], KFS, start=False)
                        last.then_inc(s_y, 1)

                    def turn(h, p):
                        c = 2 * h + p
                        pe.wait_ge(s_xlo, c + 1)
                        for f in range(KFS):
                            fc1(c, p, f)
                            if f == 1 and (p or not isinstance(h, int) or h):
                                fc2(c - 1, 1 - p)
                            if f == 2 and isinstance(h, int) and not p:
                                ranks()
                    pe.wait_ge(s_wlo, 1)
                    turn(0, 0)
                    pe.wait_ge(s_fold, 2)
                    turn(0, 1)
                    with pe.Fori(1, NC // 2) as h:
                        for p in range(2):
                            turn(h, p)
                    fc2(NC - 1, 1)

        def experts(tag, w1, w2):
            def s(n):
                return sem(f"{tag}e_{n}")
            s_in = [s(f"in{q}") for q in range(4)]
            s_add = [s(f"add{q}") for q in range(2)]
            s_rows, s_dve, s_gidx, s_tr, s_xT, s_w1, s_h, s_ge, s_a, s_y, s_ysb, s_meta, s_pad = (
                s(n) for n in ("rows", "dve", "gidx", "tr", "xT", "w1", "h", "ge", "a", "y", "ysb", "meta", "pad"))
            with ExitStack() as sc:
                rows = sb(f"{tag}_erows", [P, NB, 2], scope=sc)
                idx = sb(f"{tag}_eidx", [P, NB], I32, scope=sc)
                gidx = [sb(f"{tag}_egidx{q}", [P, 1], I32, scope=sc) for q in range(4)]
                sidx = [sb(f"{tag}_esidx{q}", [P, 1], I32, scope=sc) for q in range(4)]
                share = [sb(f"{tag}_eshare{q}", [P, 1], scope=sc) for q in range(4)]
                xn = [sb(f"{tag}_exn{q}", [P, D], scope=sc) for q in range(4)]
                y = [sb(f"{tag}_ey{q}", [P, D], scope=sc) for q in range(4)]
                xT = [sb(f"{tag}_exT{p}", [P, KD, P], scope=sc) for p in range(2)]
                w1s = [sb(f"{tag}_ew1s{q}", [P, W1], scope=sc) for q in range(4)]
                ge = [sb(f"{tag}_ege{p}", [P, KF, P], scope=sc) for p in range(2)]
                aT = [sb(f"{tag}_eaT{p}", [P, KF, P], scope=sc) for p in range(2)]
                apad = sb(f"{tag}_eapad", [P, 2], scope=sc)
                vpad = sb(f"{tag}_evpad", [P, 8], scope=sc)
                pT = [ps(f"{tag}_epT{p}", [P, KD, P], scope=sc) for p in range(2)]
                ph = [ps(f"{tag}_eph{p}", [P, 2 * KF, P], scope=sc) for p in range(2)]
                py = [ps(f"{tag}_epy{p}", [P, D], scope=sc) for p in range(2)]
                b1 = KD * 2 * F
                block = sc.enter_context(nc.Block())

                def experts_of(eng, h, qs):
                    word = eng.value_load(turn_experts[0:1, bass.ds(h, 1)], min_val=0, max_val=16 ** 6 - 1)
                    return {q: eng.snap((word >> (4 * (q + 1))) & 15).with_bounds(min_val=0, max_val=E - 1)
                            for q in qs}

                def at(h, q, ahead):
                    return h + (q + ahead) // 4, (q + ahead) % 4

                def turns(eng, turn):
                    turn(0, True, False)
                    with eng.Fori(1, NQ - 1) as h:
                        turn(h, False, False)
                    turn(NQ - 1, False, True)

                @block.sync
                def _(sp):
                    sp.dma_start(rows[:, :, :], rows_v).then_inc(s_rows, 16)

                @block.gpsimd
                def _(pool):
                    def padding(n):
                        after(pool, s_pad, n)
                        pool.tensor_tensor(pad[:, 1:2], eps[:, :], eps[:, :], ALU.add).then_inc(s_pad, 1)

                    def gather(h, q):
                        b = 4 * h + q
                        pool.wait_ge(s_gidx, b + 1)
                        after(pool, s_tr, b - 3)

                    def fetch(h, q):
                        pool.indirect_dma_start(
                            out=xn[q][:, :], out_offset=None, in_=xn_dram[:, :],
                            in_offset=bass.IndirectOffsetOnAxis(ap=gidx[q][:, 0:1], axis=0)).then_inc(s_in[q], 16)

                    def add(h, q):
                        b = 4 * h + q
                        pool.wait_ge(s_ysb, b + 1)
                        after(pool, s_add[q % 2], 16 * (2 * h + q // 2))

                    def scatter(h, q):
                        pool.indirect_dma_start(
                            out=sums_dram[q % 2][:, :], out_offset=bass.IndirectOffsetOnAxis(ap=sidx[q][:, 0:1], axis=0),
                            in_=y[q][:, :], in_offset=None, compute_op=ALU.add).then_inc(s_add[q % 2], 16)

                    def turn(h, first, last):
                        for q in range(4):
                            b = 4 * h + q
                            if not last or q < 1:
                                gather(*at(h, q, 3))
                                padding(8 * h + 2 * q - 1)
                                fetch(*at(h, q, 3))
                            if not first or q >= 1:
                                add(*at(h, q, -1))
                                padding(8 * h + (q if last else 2 * q))
                                scatter(*at(h, q, -1))
                    for q in range(3):
                        gather(0, q)
                        fetch(0, q)
                    turns(pool, turn)
                    add(NQ - 1, 3)
                    scatter(NQ - 1, 3)
                    for p in range(2):
                        pool.wait_ge(s_add[p], 16 * (NB // 2))

                @block.scalar
                def _(act):
                    def copy_w(h, q, e):
                        b = 4 * h + q
                        after(act, s_a, b - 3)
                        act.activation(apad[:, q % 2:q % 2 + 1], eps[:, :], ACT.Copy)
                        act.activation(w1s[q][:, :], w1[:, bass.ds(e * W1, W1)], ACT.Copy).then_inc(s_w1, 1)

                    def copy_x(h, q):
                        b = 4 * h + q
                        act.wait_ge(s_tr, b + 1)
                        act.activation(xT[q % 2][:, :, :], pT[q % 2][:, :, :], ACT.Copy).then_inc(s_xT, 1)

                    def gelu(h, q):
                        b = 4 * h + q
                        act.wait_ge(s_h, b + 1)
                        for f in range(KF):
                            last = act.activation(ge[q % 2][:, f, :], ph[q % 2][:, KF + f, :], ACT.Gelu,
                                                  bias=w1s[q][:, b1 + KF + f:b1 + KF + f + 1])
                        last.then_inc(s_ge, 1)

                    def turn(h, first, last):
                        es = experts_of(act, h, range(0 if first else 1, 4 if last else 5))
                        if first:
                            copy_w(0, 0, es[0])
                            copy_x(0, 0)
                        for q in range(4):
                            if not last or q < 3:
                                copy_w(*at(h, q, 1), es[q + 1])
                                copy_x(*at(h, q, 1))
                            gelu(h, q)
                    turns(act, turn)

                @block.vector
                def _(dve):
                    ch = Chain(dve, s_dve)
                    dve.wait_ge(s_rows, 16)
                    ch.link(dve.tensor_copy(idx[:, :], rows[:, :, 0]))

                    def stage(h, q):
                        b = 4 * h + q
                        after(dve, s_in[q], 16 * h)
                        dve.memset(vpad[:, q:q + 1], 0.0)
                        dve.tensor_copy(gidx[q][:, :], idx[:, bass.ds(b, 1)]).then_inc(s_gidx, 1)

                    def meta(h, q):
                        b = 4 * h + q
                        after(dve, s_add[q % 2], 16 * (2 * h + q // 2 - 1))
                        dve.memset(vpad[:, 4 + q:5 + q], 0.0)
                        dve.tensor_copy(sidx[q][:, :], idx[:, bass.ds(b, 1)])
                        dve.tensor_copy(share[q][:, :], rows[:, bass.ds(b, 1), 1]).then_inc(s_meta, 1)

                    def product(h, q):
                        b = 4 * h + q
                        dve.wait_ge(s_ge, b + 1)
                        after(dve, s_y, b - 1)
                        for f in range(KF):
                            last = dve.scalar_tensor_tensor(aT[q % 2][:, f, :], ph[q % 2][:, f, :],
                                                            w1s[q][:, b1 + f:b1 + f + 1], ge[q % 2][:, f, :],
                                                            ALU.add, ALU.mult)
                        last.then_inc(s_a, 1)

                    def scale(h, q):
                        b = 4 * h + q
                        dve.wait_ge(s_y, b + 1)
                        dve.wait_ge(s_meta, b + 1)
                        dve.tensor_scalar(y[q][:, :], py[q % 2][:, :], share[q][:, 0:1], None,
                                          ALU.mult).then_inc(s_ysb, 1)

                    def turn(h, first, last):
                        for q in range(4):
                            if not last or q < 1:
                                stage(*at(h, q, 3))
                            meta(h, q)
                            product(h, q)
                            if not first or q >= 1:
                                scale(*at(h, q, -1))
                    for q in range(3):
                        stage(0, q)
                    turns(dve, turn)
                    scale(NQ - 1, 3)

                @block.tensor
                def _(pe):
                    def turn_x(h, q):
                        b = 4 * h + q
                        pe.wait_ge(s_in[q], 16 * h + 16)
                        after(pe, s_xT, b - 1)
                        for k in range(KD):
                            last = pe.transpose(pT[q % 2][:, k, :], xn[q][:, k * P:(k + 1) * P], ident[:, :])
                        last.then_inc(s_tr, 1)

                    def fc1(h, q):
                        b = 4 * h + q
                        pe.wait_ge(s_w1, b + 1)
                        pe.wait_ge(s_xT, b + 1)
                        after(pe, s_a, b - 1)
                        for f in (2, 3, 0, 1):
                            for k in range(KD):
                                last = pe.matmul(ph[q % 2][:, f, :],
                                                 w1s[q][:, k * 2 * F + f * P:k * 2 * F + (f + 1) * P],
                                                 xT[q % 2][:, k, :], start=k == 0, stop=k == KD - 1)
                        last.then_inc(s_h, 1)

                    def fc2(h, q, e):
                        b = 4 * h + q
                        pe.wait_ge(s_a, b + 1)
                        after(pe, s_ysb, b - 1)
                        pe.matmul(py[q % 2][:, :], ones3[:, :], bias[:, bass.ds(e * D + B2, D)], start=True, stop=False)
                        for k in range(KF):
                            last = pe.matmul(py[q % 2][:, :], aT[q % 2][:, k, :],
                                             w2[:, bass.ds(e * (KF * D) + k * D, D)],
                                             start=False, stop=k == KF - 1)
                        last.then_inc(s_y, 1)

                    def turn(h, first, last):
                        es = experts_of(pe, h, range(0 if first else -1, 4 if last else 3))
                        for q in range(4):
                            if not last or q < 3:
                                turn_x(*at(h, q, 1))
                            fc1(h, q)
                            if not first or q >= 1:
                                fc2(*at(h, q, -1), es[q - 1])
                        if last:
                            fc2(h, 3, es[3])
                    turn_x(0, 0)
                    turns(pe, turn)

        def phase_attention():
            names = ("w", "cst", "xsum", "st", "sd", "rs", "y", "tr", "yc", "yT", "xx", "low", "lowT", "mus", "tm", "xi",
                     "rps", "kps", "vps", "w1p", "w2p", "gps", "rT", "kT", "rk", "cp", "cs", "v", "rep", "bo", "w1T", "ew",
                     "dec", "sg", "spread", "kv", "S", "P", "o", "oadd", "oc", "sq", "gv", "gsd", "gn", "z", "ztr",
                     "zT", "wo", "x2", "st2", "sd2", "rs2", "n2", "ntr", "nT", "lg", "lgs", "dve",
                     "l_sum", "o_x1", "l_x1", "o_x2", "o_xn", "o_xnT")
            S = {n: sem(f"t_{n}") for n in names}
            with ExitStack() as sc:
                def t(n, shape, dt=FP32):
                    return sb(f"t_{n}", shape, dt, scope=sc)
                wx1 = t("wx1", [P, KD, 5 * LR])
                wx2 = t("wx2", [P, D])
                wx2l = t("wx2l", [LR, D])
                xb = t("xb", [P, KD, 5])
                mu = t("mu", [P, KD])
                wr, wk = t("wr", [P, KD, P]), t("wk", [P, KD, P])
                ww1 = t("ww1", [P, KD, GL])
                ww2 = t("ww2", [GL, P])
                bw2 = t("bw2", [P, 1])
                wv, wg, wo = (t(n, [P, KD, D]) for n in ("wv", "wg", "wo"))
                gnw, gnb = t("gnw", [P, D]), t("gnb", [P, D])
                uk = t("uk", [P, 1])
                HS = P - H
                headsum = t("headsum", [P, HS + P])
                uhead = t("uhead", [P, P])
                parts = [t(f"part{q}", [P, TC, D]) for q in range(2)]
                x1 = t("x1", [P, TC, D])
                st = t("st", [P, TC, 6])
                mv = t("mv", [P, TC, 2])
                sd = t("sd", [P, TC])
                rs = t("rs", [P, TC])
                nb = t("nb", [P, TC])
                y = t("y", [P, TC, D])
                yT = t("yT", [P, KD, C + 1])
                dl = t("dl", [P, KD, C])
                xx = t("xx", [P, KD, C])
                lowT = t("lowT", [P, C])
                lowTl = t("lowTl", [LR, C])
                tm = t("tm", [P, 2, C])
                xi = [t(f"xi{q}", [P, KD, C]) for q in range(2)]
                ew = t("ew", [P, C])
                w1T = t("w1T", [GL, C])
                rk = t("rk", [P, C])
                cs = t("cs", [P, TC * H])
                rT = [t(f"rT{q}", [P, C]) for q in range(2)]
                kT = [t(f"kT{q}", [P, C]) for q in range(2)]
                dec = [t(f"dec{q}", [P, C]) for q in range(2)]
                vs = [t(f"v{q}", [P, TC, D]) for q in range(2)]
                bo = [t(f"bo{q}", [P, TC, D]) for q in range(2)]
                sg = [t(f"sg{q}", [P, TC, D]) for q in range(2)]
                rep = [t(f"rep{q}", [P, TC, P]) for q in range(4)]
                kv = [t(f"kv{q}", [P, C]) for q in range(2)]
                St = t("S", [P, DV, C + 1])
                Pr = [t(f"P{q}", [P, C]) for q in range(4)]
                o = t("o", [P, TC, D])
                o2 = t("o2", [P, TC, D])
                gs = t("gs", [P, TC * H])
                gv = t("gv", [P, TC * H])
                zT = t("zT", [P, KD, C])
                xr = t("xr", [P, TC, D])
                st2 = t("st2", [P, TC, 6])
                mv2 = t("mv2", [P, TC, 2])
                sd2 = t("sd2", [P, TC])
                rs2 = t("rs2", [P, TC])
                nb2 = t("nb2", [P, TC])
                n2 = t("n2", [P, TC, D])
                psX = ps("t_psX", [P, KD, C], scope=sc)
                psX_tok = psX[:, :, :].rearrange("p a (b d) -> p (a b) d", d=D)
                psX_narrow = psX[:, 0, :].rearrange("p (i e) -> p i e", e=P)
                psO = ps("t_psO", [P, TC, D], scope=sc)
                psM = [ps(f"t_psM{q}", [P, C], scope=sc) for q in range(2)]
                psV = [ps(f"t_psV{q}", [P, C], scope=sc) for q in range(2)]

                def tok(ap):
                    return ap.rearrange("(i p) d -> p i d", p=P)
                sum_v = [tok(q) for q in sums_dram]
                x1_v, x2_v, xn_v = tok(x1_dram), tok(x2_dram), tok(xn_dram)
                xnT_v = xnT_dram.rearrange("(k p) t -> p k t", p=P)
                order = (MIX_R, MIX_K, MIX_V, MIX_W, MIX_G)
                block = sc.enter_context(nc.Block())

                def chunk(c):
                    return bass.ds(c * TC, TC)

                def iterations(eng, body, ch=None, per_turn=0):
                    for it in (-1, 0, 1):
                        body(it, it % 2, True, True, it >= 0, it >= 1)
                    with eng.Fori(1, NC // 2 - 1) as h, ExitStack() as counted:
                        if ch:
                            counted.enter_context(ch.turns(h - 1, NC // 2 - 2, per_turn))
                        for q in range(2):
                            body(2 * h + q, q, True, True, True, True)
                    for it in (NC - 2, NC - 1, NC):
                        body(it, it % 2, False, it < NC - 1, it < NC, True)

                @block.sync
                def _(sp):
                    def load(n):
                        for q in range(2):
                            sp.dma_start(parts[q][:, :, :], sum_v[q][:, chunk(n), :]).then_inc(S["l_sum"], 16)

                    def store(n):
                        sp.wait_ge(S["xsum"], n + 1)
                        sp.dma_start(x1_v[:, chunk(n), :], x1[:, :, :]).then_inc(S["o_x1"], 16)

                    with nc.allow_non_contiguous_dma(reason="small per-channel vectors"):
                        loads = (
                            (wx1[:, :, :], W_x1.rearrange("(k p) r -> p k r", p=P)),
                            (wx2[:, :], W_x2[0:P, :]), (wx2l[:, :], W_x2[P:P + LR, :]),
                            (xb[:, :, :], x_biasT.rearrange("(k p) i -> p k i", p=P)),
                            (mu[:, :], mu_x.rearrange("(k p) -> p k", p=P)),
                            (wr[:, :, :], W_r.rearrange("(k p) m -> p k m", p=P)),
                            (wk[:, :, :], W_k.rearrange("(k p) m -> p k m", p=P)),
                            (ww1[:, :, :], W_w1.rearrange("(k p) m -> p k m", p=P)),
                            (ww2[:, :], W_w2[:, :]), (bw2[:, :], b_w2.unsqueeze(1)),
                            (wv[:, :, :], W_v.rearrange("(k p) m -> p k m", p=P)),
                            (wg[:, :, :], W_g.rearrange("(k p) m -> p k m", p=P)),
                            (wo[:, :, :], W_o.rearrange("(k p) m -> p k m", p=P)),
                            (gnw[:, :], bcast(gn_w, 0, P)), (gnb[:, :], bcast(gn_b, 0, P)),
                            (uk[:, :], u.rearrange("h k -> (h k)").unsqueeze(1)))
                        for n, (dst, src) in enumerate(loads):
                            if n == 0:
                                load(0)
                            sp.dma_start(dst, src).then_inc(S["w"], 16)
                        assert len(loads) == 16
                    store(0)

                    def body(it, par, has_l, has_a, has_b, has_c):
                        if has_l:
                            sp.wait_ge(S["xsum"], it + 2)
                            load(it + 2)
                        if has_c:
                            c = it - 1
                            after(sp, S["o_x2"], 16 * c)
                            after(sp, S["n2"], c)
                            sp.dma_start(xr[:, :, :], x1_v[:, chunk(c), :]).then_inc(S["l_x1"], 16)
                        if has_l:
                            store(it + 2)
                        if has_c:
                            sp.wait_ge(S["x2"], c + 1)
                            sp.dma_start(x2_v[:, chunk(c), :], xr[:, :, :]).then_inc(S["o_x2"], 16)
                            sp.wait_ge(S["n2"], c + 1)
                            sp.dma_start(xn_v[:, chunk(c), :], n2[:, :, :]).then_inc(S["o_xn"], 16)
                            sp.wait_ge(S["nT"], c + 1)
                            sp.dma_start(xnT_v[:, :, bass.ds(c * C, C)], zT[:, :, :]).then_inc(S["o_xnT"], 16)
                    iterations(sp, body)
                    sp.wait_ge(S["o_x1"], 16 * NC)
                    for n in ("o_x2", "o_xn", "o_xnT"):
                        sp.wait_ge(S[n], 16 * NC)

                @block.gpsimd
                def _(pool):
                    def x_sum(n):
                        pool.wait_ge(S["l_sum"], 32 * (n + 1))
                        after(pool, S["y"], n)
                        after(pool, S["o_x1"], 16 * n)
                        pool.tensor_tensor(x1[:, :, :], parts[0][:, :, :], parts[1][:, :, :],
                                           ALU.add).then_inc(S["xsum"], 1)

                    pool.memset(headsum[:, :], 0.0).then_inc(S["cst"], 1)
                    pool.wait_ge(S["cst"], 1)
                    pool.memset(headsum[:, HS:P], 1.0).then_inc(S["cst"], 1)
                    pool.memset(St[:, :, C:C + 1], 0.0).then_inc(S["cst"], 1)
                    pool.memset(yT[:, :, C:C + 1], 0.0).then_inc(S["cst"], 1)
                    pool.wait_ge(S["cst"], 4)
                    pool.affine_select(out=headsum[:, HS:P], in_=headsum[:, HS:P], compare_op=ALU.is_ge, fill=0.0,
                                       base=0, pattern=[[-DK, H]], channel_multiplier=1).then_inc(S["cst"], 1)
                    pool.wait_ge(S["cst"], 5)
                    pool.affine_select(out=headsum[:, HS:P], in_=headsum[:, HS:P], compare_op=ALU.is_ge, fill=0.0,
                                       base=DK - 1, pattern=[[DK, H]], channel_multiplier=-1).then_inc(S["cst"], 1)
                    pool.wait_ge(S["cst"], 6)
                    x_sum(0)
                    pool.wait_ge(S["w"], 16 * 16)
                    pool.tensor_scalar(uhead[:, :], headsum[:, HS:HS + P], uk[:, 0:1], None, ALU.mult).then_inc(S["cst"], 1)

                    def body(it, par, has_l, has_a, has_b, has_c):
                        a, c = it + 1, it - 1
                        pa = 1 - par

                        def mixed(n):
                            if n < 2:
                                after(pool, S["gps"], a)
                            else:
                                pool.wait_ge(S[{2: "rps", 3: "kps", 4: "vps"}[n]], a + 1)
                            for k in range(KD):
                                pool.wait_ge(S["tm"], 10 * a + 2 * n + k + 1)
                                pool.tensor_tensor(xi[n % 2][:, k, :], tm[:, k, :], yT[:, k, 1:C + 1],
                                                   ALU.add).then_inc(S["xi"], 1)

                        def bonus():
                            pool.wait_ge(S["rT"], a + 1)
                            pool.wait_ge(S["kT"], a + 1)
                            after(pool, S["cp"], a)
                            pool.tensor_tensor(rk[:, :], rT[pa][:, :], kT[pa][:, :], ALU.mult).then_inc(S["rk"], 1)

                        def weigh():
                            pool.wait_ge(S["v"], a + 1)
                            pool.wait_ge(S["cs"], a + 1)
                            after(pool, S["oadd"], a - 1)
                            pool.tensor_tensor(bo[pa][:, :, :].rearrange("p i (h v) -> p (i h) v", v=DV),
                                               vs[pa][:, :, :].rearrange("p i (h v) -> p (i h) v", v=DV),
                                               bcast(cs[:, :], 2, DV), ALU.mult).then_inc(S["bo"], 1)

                        def read(v):
                            pool.wait_ge(S["S"], 16 * it + v + 1)
                            after(pool, S["o"], 16 * it + v - 3)
                            pool.tensor_tensor(Pr[v % 4][:, :], St[:, v, 0:C], rT[par][:, :], ALU.mult).then_inc(S["P"], 1)

                        def gated():
                            pool.wait_ge(S["gn"], c + 1)
                            pool.wait_ge(S["sg"], c + 1)
                            after(pool, S["gv"], c + 1)
                            pool.tensor_tensor(o2[:, :, :], o[:, :, :], sg[pa][:, :, :], ALU.mult).then_inc(S["z"], 1)

                        for v in range(16):
                            if has_a and 4 <= v <= 8:
                                mixed(v - 4)
                            if has_a and v == 8:
                                bonus()
                            if has_l and v == 6:
                                x_sum(it + 2)
                            if has_b:
                                read(v)
                            if has_c and v == 8:
                                gated()
                            if has_a and v == 11:
                                weigh()
                    iterations(pool, body)

                @block.vector
                def _(dve):
                    LINKS = 12
                    ch = Chain(dve, S["dve"])
                    o_h = o[:, :, :].rearrange("p i (h v) -> p (i h) v", v=DV)
                    o2_h = o2[:, :, :].rearrange("p i (h v) -> p (i h) v", v=DV)

                    def stats(src, st, mv, done):
                        for i in range(TC):
                            last = dve.bn_stats(st[:, i, :], src[:, i, :])
                        ch.link(last)
                        dve.memset(pad[:, 0:1], 0.0)
                        for i in range(TC):
                            last = dve.bn_aggr(mv[:, i, :], st[:, i, :])
                        last.then_inc(done, 1)

                    def scales(sd, mv, rs, nb, done):
                        ch.link(dve.reciprocal(rs[:, :], sd[:, :]))
                        dve.scalar_tensor_tensor(nb[:, :], mv[:, :, 0], -1.0, rs[:, :], ALU.mult,
                                                 ALU.mult).then_inc(done, 1)

                    def moments(n):
                        dve.wait_ge(S["xsum"], n + 1)
                        stats(x1, st, mv, S["st"])

                    def scale(n):
                        dve.wait_ge(S["sd"], n + 1)
                        scales(sd, mv, rs, nb, S["rs"])

                    def body(it, par, has_l, has_a, has_b, has_c):
                        a, c = it + 1, it - 1
                        pa = 1 - par

                        def shift():
                            dve.wait_ge(S["yT"], a + 1)
                            ch.link(dve.tensor_tensor(dl[:, :, :], yT[:, :, 0:C], yT[:, :, 1:C + 1], ALU.subtract))
                            for k in range(KD):
                                last = dve.scalar_tensor_tensor(xx[:, k, :], dl[:, k, :], mu[:, k:k + 1],
                                                                yT[:, k, 1:C + 1], ALU.mult, ALU.add)
                            last.then_inc(S["xx"], 1)

                        def mix(n):
                            for k in range(KD):
                                dve.wait_ge(S["mus"], 10 * a + 2 * n + k + 1)
                                after(dve, S["xi"], 10 * a + 2 * n + k - 1)
                                dve.scalar_tensor_tensor(tm[:, k, :], psM[k][:, :], xb[:, k, order[n]:order[n] + 1],
                                                         dl[:, k, :], ALU.add, ALU.mult).then_inc(S["tm"], 1)

                        def carry(lo):
                            after(dve, S["P"], 16 * it)
                            ch.link(dve.tensor_copy(St[:, lo:lo + 8, 0:1], St[:, lo:lo + 8, C:C + 1]))

                        def recur(v):
                            dve.wait_ge(S["spread"], 16 * it + v + 1)
                            dve.tensor_tensor(kv[v % 2][:, :], psV[v % 2][:, :], kT[par][:, :],
                                              ALU.mult).then_inc(S["kv"], 1)
                            dve.wait_ge(S["kv"], 16 * it + v + 1)
                            dve.tensor_tensor_scan(St[:, v, 1:C + 1], dec[par][:, :], kv[v % 2][:, :], St[:, v, 0:1],
                                                   ALU.mult, ALU.add).then_inc(S["S"], 1)

                        def collect():
                            dve.wait_ge(S["o"], 16 * (c + 1))
                            after(dve, S["z"], c)
                            dve.tensor_tensor(*(q[:, :, :].rearrange(f"p i ({w}) -> p i h v", h=H)
                                                for q, w in ((o, "h v"), (psO, "v h"), (bo[pa], "h v"))), ALU.add).then_inc(S["oadd"], 1)
                            dve.wait_ge(S["oadd"], c + 1)
                            ch.link(dve.tensor_reduce(gs[:, :], o_h, AX, ALU.add))
                            ch.link(dve.tensor_scalar(gs[:, :], gs[:, :], 1.0 / DV, None, ALU.mult))

                        def centre():
                            dve.tensor_tensor(o_h, o_h, bcast(gs[:, :], 2, DV), ALU.subtract).then_inc(S["oc"], 1)

                        def variance():
                            dve.wait_ge(S["sq"], c + 1)
                            dve.tensor_reduce(gv[:, :], o2_h, AX, ALU.add).then_inc(S["gv"], 1)

                        def normalise():
                            dve.wait_ge(S["gsd"], c + 1)
                            ch.link(dve.reciprocal(gs[:, :], gv[:, :]))
                            ch.link(dve.tensor_tensor(o_h, o_h, bcast(gs[:, :], 2, DV), ALU.mult))

                        def affine():
                            ch.link(dve.tensor_tensor(o[:, :, :], o[:, :, :], bcast(gnw[:, :], 1, TC), ALU.mult))
                            dve.tensor_tensor(o[:, :, :], o[:, :, :], bcast(gnb[:, :], 1, TC), ALU.add).then_inc(S["gn"], 1)

                        for v in range(16):
                            if has_b and v in (0, 8):
                                carry(v)
                            if has_c and v == 2:
                                collect()
                            if has_c and v == 3:
                                centre()
                            if has_c and v == 5:
                                variance()
                            if has_c and v == 7:
                                normalise()
                            if has_c and v == 8:
                                affine()
                            if has_b:
                                recur(v)
                            if has_a and v == 1:
                                shift()
                            if has_a and 3 <= v <= 7:
                                mix(v - 3)
                            if has_a and v == 9:
                                dve.wait_ge(S["cp"], a + 1)
                                after(dve, S["bo"], a)
                                dve.tensor_copy(cs[:, :].rearrange("p (i h) -> p i h", h=H), psX_narrow[:, :, 0:H]).then_inc(S["cs"], 1)
                            if has_l and v == 9:
                                moments(it + 2)
                            if has_l and v == 10:
                                scale(it + 2)
                            if has_c and v == 12:
                                dve.wait_ge(S["wo"], c + 1)
                                dve.wait_ge(S["l_x1"], 16 * (c + 1))
                                dve.tensor_tensor(xr[:, :, :], psX_tok, xr[:, :, :], ALU.add).then_inc(S["x2"], 1)
                                dve.wait_ge(S["x2"], c + 1)
                                stats(xr, st2, mv2, S["st2"])
                            if has_c and v == 13:
                                dve.wait_ge(S["sd2"], c + 1)
                                scales(sd2, mv2, rs2, nb2, S["rs2"])
                            if has_c and v == 15:
                                dve.wait_ge(S["lg"], c + 1)
                                dve.tensor_copy(logits[:, chunk(c), :], psX_narrow[:, :, 0:E]).then_inc(S["lgs"], 1)
                    moments(0)
                    scale(0)
                    dve.wait_ge(S["w"], 16 * 16)
                    dve.wait_ge(S["cst"], 7)
                    iterations(dve, body, ch, 2 * LINKS)

                @block.scalar
                def _(act):
                    act.dma_start(rows_v, fill[:, :, :]).then_inc(s_fill, 16)

                    def norm(dst, src, nb, rs):
                        for i in range(TC):
                            last = act.activation(dst[:, i, :], src[:, i, :], ACT.Identity, bias=nb[:, i:i + 1],
                                                  scale=rs[:, i:i + 1])
                        return last

                    def norm_1(n):
                        act.wait_ge(S["st"], n + 1)
                        act.activation(sd[:, :], mv[:, :, 1], ACT.Sqrt, bias=eps[:, 0:1]).then_inc(S["sd"], 1)
                        act.wait_ge(S["rs"], n + 1)
                        after(act, S["tr"], n)
                        norm(y, x1, nb, rs).then_inc(S["y"], 1)

                    def body(it, par, has_l, has_a, has_b, has_c):
                        a, c = it + 1, it - 1
                        pa = 1 - par
                        def repeat(t, v, src):
                            after(act, S["spread"], 16 * t + v - 3)
                            act.activation(rep[v % 4][:, :, :].rearrange("p i (h k) -> p i h k", k=DK),
                                           bcast(src[:, :, v:D:DV], 3, DK), ACT.Copy).then_inc(S["rep"], 1)

                        for v in range(16):
                            if has_b and v < 13:
                                repeat(it, v + 3, vs[par])
                            if has_a and v >= 13:
                                repeat(a, v - 13, vs[pa])
                            if has_a and v == 0:
                                after(act, S["xi"], 10 * a)
                                act.activation(yT[:, :, 0:1], yT[:, :, C:C + 1], ACT.Copy).then_inc(S["yc"], 1)
                                act.wait_ge(S["tr"], a + 1)
                                act.wait_ge(S["yc"], a + 1)
                                act.activation(yT[:, :, 1:C + 1], psX[:, :, :], ACT.Copy).then_inc(S["yT"], 1)
                            if has_a and v == 2:
                                act.preload_act_table(ACT.Tanh)
                                act.wait_ge(S["low"], a + 1)
                                act.activation(lowT[:, :], psX[:, 0, :], ACT.Tanh)
                                act.activation(lowTl[:, :], psX[0:LR, 1, :], ACT.Tanh).then_inc(S["lowT"], 1)
                            if has_c and v == 3:
                                act.wait_ge(S["oc"], c + 1)
                                after(act, S["ztr"], c)
                                act.activation(o2[:, :, :], o[:, :, :], ACT.Square).then_inc(S["sq"], 1)
                            if has_a and v == 5:
                                act.wait_ge(S["rps"], a + 1)
                                after(act, S["P"], 16 * (a - 1))
                                act.activation(rT[pa][:, :], psX[:, 0, :], ACT.Copy).then_inc(S["rT"], 1)
                            if has_c and v == 5:
                                act.preload_act_table(ACT.Sqrt)
                                act.wait_ge(S["gv"], c + 1)
                                act.activation(gv[:, :], gv[:, :], ACT.Sqrt, bias=eps[:, 0:1],
                                               scale=1.0 / DV).then_inc(S["gsd"], 1)
                            if has_a and v == 6:
                                act.wait_ge(S["kps"], a + 1)
                                after(act, S["kv"], 16 * (a - 1))
                                act.activation(kT[pa][:, :], psX[:, 1, :], ACT.Copy).then_inc(S["kT"], 1)
                            if has_a and v == 7:
                                act.wait_ge(S["vps"], a + 1)
                                after(act, S["bo"], a - 1)
                                act.activation(vs[pa][:, :, :], psX_tok, ACT.Copy).then_inc(S["v"], 1)
                                act.wait_ge(S["v"], a + 1)
                            if has_a and v == 8:
                                act.preload_act_table(ACT.Tanh)
                                act.wait_ge(S["w1p"], a + 1)
                                act.activation(w1T[:, :], psX[0:GL, 0, :], ACT.Tanh).then_inc(S["w1T"], 1)
                            if has_a and v == 9:
                                act.wait_ge(S["w2p"], a + 1)
                                act.activation(ew[:, :], psX[:, 1, :], ACT.Exp, bias=bw2[:, 0:1]).then_inc(S["ew"], 1)
                                act.wait_ge(S["ew"], a + 1)
                                after(act, S["S"], 16 * (a - 1))
                                act.activation(dec[pa][:, :], ew[:, :], ACT.Exp, scale=-1.0).then_inc(S["dec"], 1)
                            if has_c and v == 10:
                                act.wait_ge(S["ztr"], c + 1)
                                after(act, S["o_xnT"], 16 * c)
                                act.activation(zT[:, :, :], psX[:, :, :], ACT.Copy).then_inc(S["zT"], 1)
                            if has_l and v == 10:
                                act.preload_act_table(ACT.Sqrt)
                                norm_1(it + 2)
                            if has_c and v == 12:
                                act.wait_ge(S["st2"], c + 1)
                                act.activation(sd2[:, :], mv2[:, :, 1], ACT.Sqrt, bias=eps[:, 0:1]).then_inc(S["sd2"], 1)
                            if has_a and v == 13:
                                act.preload_act_table(ACT.Silu)
                            if has_c and v == 13:
                                act.wait_ge(S["rs2"], c + 1)
                                after(act, S["ntr"], c)
                                after(act, S["o_xn"], 16 * c)
                                norm(n2, xr, nb2, rs2).then_inc(S["n2"], 1)
                            if has_a and v == 13:
                                act.wait_ge(S["gps"], a + 1)
                                after(act, S["z"], a - 1)
                                act.activation(sg[pa][:, :, :], psX_tok, ACT.Silu).then_inc(S["sg"], 1)
                            if has_c and v == 14:
                                act.wait_ge(S["ntr"], c + 1)
                                act.activation(zT[:, :, :], psX[:, :, :], ACT.Copy).then_inc(S["nT"], 1)
                    norm_1(0)
                    act.wait_ge(S["cst"], 7)
                    act.wait_ge(S["w"], 16 * 16)
                    iterations(act, body)

                @block.tensor
                def _(pe):
                    pe.wait_ge(S["cst"], 7)
                    pe.wait_ge(S["w"], 16 * 16)

                    def turn(src, done):
                        for k in range(KD):
                            for i in range(TC):
                                last = pe.transpose(psX[:, k, i * P:(i + 1) * P], src[:, i, k * P:(k + 1) * P],
                                                    ident[:, :])
                        last.then_inc(done, 1)

                    def project(dst, w, src):
                        for k in range(KD):
                            last = pe.matmul(dst, w(k), src(k), start=k == 0, stop=k == KD - 1)
                        return last

                    def by_token(w, src, done):
                        for i in range(TC):
                            last = project(psX_tok[:, i, :], lambda k: src[:, k, i * P:(i + 1) * P], lambda k: w[:, k, :])
                        last.then_inc(done, 1)

                    def body(it, par, has_l, has_a, has_b, has_c):
                        a, c = it + 1, it - 1
                        pa = 1 - par
                        x_r = x_v = x_g = xi[0]
                        x_k = x_w = xi[1]

                        def mus(n):
                            i = order[n]
                            for k in range(KD):
                                after(pe, S["tm"], 10 * a + 2 * n + k - 1)
                                if i < 4:
                                    ins = pe.matmul(psM[k][:, :], wx2[i * LR:(i + 1) * LR, k * P:(k + 1) * P],
                                                    lowT[i * LR:(i + 1) * LR, :], start=True, stop=True)
                                else:
                                    ins = pe.matmul(psM[k][:, :], wx2l[:, k * P:(k + 1) * P], lowTl[:, :],
                                                    start=True, stop=True)
                                ins.then_inc(S["mus"], 1)

                        def spread(v):
                            if v == 0:
                                pe.wait_ge(S["dec"], it + 1)
                            pe.wait_ge(S["rep"], 16 * it + v + 1)
                            after(pe, S["kv"], 16 * it + v - 1)
                            for i in range(TC):
                                last = pe.transpose(psV[v % 2][:, i * P:(i + 1) * P], rep[v % 4][:, i, :], ident[:, :])
                            last.then_inc(S["spread"], 1)

                        def head_sums(t, v):
                            pe.wait_ge(S["P"], 16 * t + v + 1)
                            if v == 0:
                                after(pe, S["oadd"], t)
                            for i in range(TC):
                                half = v // 8
                                last = pe.matmul(psO[:, i, half * P:(half + 1) * P], Pr[v % 4][:, i * P:(i + 1) * P],
                                                 headsum[:, HS - H * (v % 8):HS - H * (v % 8) + P],
                                                 start=v == 0 and i % 2 == 0, stop=v == 15, skip_group_check=True)
                            last.then_inc(S["o"], 1)

                        if has_b:
                            spread(0)
                        for v in range(16):
                            if has_a and v == 0:
                                pe.wait_ge(S["y"], a + 1)
                                after(pe, S["sg"], a)
                                after(pe, S["lgs"], it - 1)
                                turn(y, S["tr"])
                            if has_a and v == 2:
                                pe.wait_ge(S["xx"], a + 1)
                                pe.wait_ge(S["yT"], a + 1)
                                project(psX[:, 0, :], lambda k: wx1[:, k, 0:P], lambda k: xx[:, k, :])
                                project(psX[0:LR, 1, :], lambda k: wx1[:, k, P:P + LR],
                                        lambda k: xx[:, k, :]).then_inc(S["low"], 1)
                            if has_a and v == 3:
                                pe.wait_ge(S["lowT"], a + 1)
                            if has_a and 3 <= v <= 7:
                                mus(v - 3)
                            if has_a and v == 5:
                                pe.wait_ge(S["xi"], 10 * a + 2)
                                project(psX[:, 0, :], lambda k: wr[:, k, :], lambda k: x_r[:, k, :]).then_inc(S["rps"], 1)
                            if has_a and v == 6:
                                pe.wait_ge(S["xi"], 10 * a + 4)
                                project(psX[:, 1, :], lambda k: wk[:, k, :], lambda k: x_k[:, k, :]).then_inc(S["kps"], 1)
                            if has_a and v == 7:
                                pe.wait_ge(S["xi"], 10 * a + 6)
                                pe.wait_ge(S["rT"], a + 1)
                                pe.wait_ge(S["kT"], a + 1)
                                by_token(wv, x_v, S["vps"])
                            if has_a and v == 8:
                                pe.wait_ge(S["xi"], 10 * a + 8)
                                pe.wait_ge(S["v"], a + 1)
                                project(psX[0:GL, 0, :], lambda k: ww1[:, k, :],
                                        lambda k: x_w[:, k, :]).then_inc(S["w1p"], 1)
                            if has_a and v == 9:
                                pe.wait_ge(S["w1T"], a + 1)
                                pe.matmul(psX[:, 1, :], ww2[:, :], w1T[:, :], start=True, stop=True).then_inc(S["w2p"], 1)
                                pe.wait_ge(S["rk"], a + 1)
                                for i in range(TC):
                                    last = pe.matmul(psX[:, 0, i * P:(i + 1) * P], rk[:, i * P:(i + 1) * P], uhead[:, :],
                                                     start=True, stop=True)
                                last.then_inc(S["cp"], 1)
                            if has_c and v == 10:
                                pe.wait_ge(S["z"], c + 1)
                                if has_a:
                                    pe.wait_ge(S["ew"], a + 1)
                                    pe.wait_ge(S["cs"], a + 1)
                                else:
                                    pe.wait_ge(S["lgs"], c)
                                turn(o2, S["ztr"])
                            if has_c and v == 12:
                                pe.wait_ge(S["zT"], c + 1)
                                by_token(wo, zT, S["wo"])
                            if has_a and v == 13:
                                pe.wait_ge(S["xi"], 10 * a + 10)
                                if has_c:
                                    pe.wait_ge(S["x2"], c + 1)
                                else:
                                    pe.wait_ge(S["ew"], a + 1)
                                    pe.wait_ge(S["cs"], a + 1)
                                by_token(wg, x_g, S["gps"])
                            if has_c and v == 14:
                                pe.wait_ge(S["n2"], c + 1)
                                pe.wait_ge(S["x2"], c + 1)
                                if has_a:
                                    pe.wait_ge(S["sg"], a + 1)
                                turn(n2, S["ntr"])
                            if has_c and v == 15:
                                pe.wait_ge(S["nT"], c + 1)
                                for i in range(TC):
                                    last = project(psX_narrow[:, i, :], lambda k: zT[:, k, i * P:(i + 1) * P],
                                                   lambda k: gate[:, k, :])
                                last.then_inc(S["lg"], 1)
                            if has_b and v < 15:
                                spread(v + 1)
                            if v >= 2 and has_b:
                                head_sums(it, v - 2)
                            if v < 2 and has_c:
                                head_sums(it - 1, 14 + v)
                    iterations(pe, body)

        def phase_out():
            s_in = [sem(f"f_in{p}") for p in range(2)]
            s_out = [sem(f"f_out{p}") for p in range(2)]
            s_sum = sem("f_sum")
            with ExitStack() as sc:
                parts = [[sb(f"f_part{p}{q}", [P, TC, D], scope=sc) for q in range(2)] for p in range(2)]
                sum_v = [q.rearrange("(i p) d -> p i d", p=P) for q in sums_dram]
                out_v = out.rearrange("a (i p) d -> p (a i) d", p=P)
                block = sc.enter_context(nc.Block())

                @block.sync
                def _(sp):
                    def turn(h, p):
                        c = 2 * h + p
                        after(sp, s_out[p], 16 * h)
                        for q in range(2):
                            sp.dma_start(parts[p][q][:, :, :], sum_v[q][:, bass.ds(c * TC, TC), :]).then_inc(s_in[p], 16)
                    for p in range(2):
                        turn(0, p)
                    with sp.Fori(1, NC // 2) as h:
                        for p in range(2):
                            turn(h, p)

                @block.scalar
                def _(act):
                    with act.Fori(0, NC // 2) as h:
                        for p in range(2):
                            c = 2 * h + p
                            act.wait_ge(s_sum, c + 1)
                            act.dma_start(out_v[:, bass.ds(c * TC, TC), :], parts[p][0][:, :, :]).then_inc(s_out[p], 16)
                    for p in range(2):
                        act.wait_ge(s_out[p], 8 * NC)

                @block.vector
                def _(dve):
                    with dve.Fori(0, NC // 2) as h:
                        for p in range(2):
                            dve.wait_ge(s_in[p], 32 * h + 32)
                            dve.tensor_tensor(parts[p][0][:, :, :], parts[p][0][:, :, :], parts[p][1][:, :, :],
                                              ALU.add).then_inc(s_sum, 1)

        phase_norm()
        end_phase()
        phase_experts("m1", x.rearrange("a t d -> (a t) d"))
        end_phase()
        phase_attention()
        end_phase()
        phase_experts("m2", x2_dram)
        end_phase()
        phase_out()


def kernel(**inputs):
    import numpy as _np
    import concourse.bacc as _bacc
    from concourse import mybir as _mybir
    from concourse.bass_utils import run_bass_kernel_spmd as _run

    a = {k.replace("L0_attn_", "").replace("L0_ffn_", "f_"): _np.asarray(v) for k, v in inputs.items()}
    lay = {
        "x": a["x"], "mu_x": a["mu_x"], "W_x1": a["W_x1"],
        "W_x2": a["W_x2"].transpose(1, 2, 0).reshape(5 * LR, D),
        "x_biasT": a["x_bias"].T, "W_r": a["W_r"], "W_w1": a["W_w1"], "W_w2": a["W_w2"], "b_w2": a["b_w2"],
        "W_k": a["W_k"], "W_v": a["W_v"],
        "W_g": a["W_g"], "u": a["u"], "gn_w": a["gn_w"], "gn_b": a["gn_b"], "W_o": a["W_o"],
        "gate_wT": a["f_gate_w"].T, "fc1_wT": a["f_fc1_w"].transpose(0, 2, 1),
        "fc1_bT": a["f_fc1_b"].reshape(E, 2 * KF, P).transpose(2, 0, 1),
        "geglu_multT": a["f_geglu_mult"].reshape(E * KF, P).T, "fc2_wT": a["f_fc2_w"].transpose(0, 2, 1), "fc2_b": a["f_fc2_b"],
        "s_fc1_wT": a["f_s_fc1_w"].T, "s_fc1_bT": a["f_s_fc1_b"].reshape(2 * KFS, P).T,
        "s_geglu_multT": a["f_s_geglu_mult"].reshape(KFS, P).T,
        "s_fc2_wT": a["f_s_fc2_w"].T, "s_fc2_b": a["f_s_fc2_b"],
    }
    nc = _bacc.Bacc("TRN2", target_bir_lowering=False, num_devices=1)
    arrays, args = {}, []
    for name, v in lay.items():
        v = _np.ascontiguousarray(v)
        arrays[f"in_{name}"] = v
        args.append(nc.dram_tensor(f"in_{name}", v.shape, _mybir.dt.from_np(v.dtype), kind="ExternalInput").ap())
    res = nc.dram_tensor("out_x", (1, T, D), _mybir.dt.float32, kind="ExternalOutput").ap()
    macaron_kernel(nc, *args, res)
    r = _run(nc, [arrays], core_ids=[0])
    return r.results[0]["out_x"]
```
